# Optimizing a Trainium2 kernel written in Bass

```python
import numpy as np
import jax
import jax.numpy as jnp

def _softmax(x, axis=-1):
    return jax.nn.softmax(x, axis=axis)

def _gelu(x):
    return jax.nn.gelu(x, approximate=True)

def _silu(x):
    return jax.nn.silu(x)

def _sigmoid(x):
    return jax.nn.sigmoid(x)

def _layernorm(x, axis=-1, eps=1e-05):
    m = jnp.mean(x, axis=axis, keepdims=True)
    v = jnp.var(x, axis=axis, keepdims=True)
    return (x - m) / jnp.sqrt(v + eps)

def _scatter_add(tgt, idx, src, axis=0):
    return tgt.at[idx].add(src)

def _segment_sum(src, seg, n):
    return jax.ops.segment_sum(src, seg, n)
kernel_name = 'mk_lm_tower_d2_tok_ids512_r4_ae2697'

def setup_inputs(seed: int=0):
    np.random.seed(seed)
    _w = jnp.asarray

    def _rec_inputs():
        import jax
        import jax.numpy as jnp
        _rk = jax.random.key(seed)
        x = jax.random.randint(jax.random.fold_in(_rk, 1), (1, 2048), 0, 12564, jnp.int32)
        return x
    x = _rec_inputs()

    def _L0_tok_setup():
        import jax, jax.numpy as jnp
        import numpy as np
        VOCAB = 50257
        D_MODEL = 128
        B, S = (4, 1024)
        key = jax.random.key(seed)
        k_ids, k_w = jax.random.split(key)
        token_ids = jax.random.randint(k_ids, (B, S), 0, VOCAB, dtype=jnp.int64 if jax.config.jax_enable_x64 else jnp.int32)
        w = jax.random.truncated_normal(k_w, -3.0, 3.0, (VOCAB, D_MODEL), dtype=jnp.float32)
        return {'token_ids': token_ids, 'w': w}
    _L0_tok_all = _L0_tok_setup()
    _L0_tok_in = {k: v for k, v in _L0_tok_all.items() if k in ('w',)}
    del _L0_tok_all

    def _L0_attn_setup():
        import jax, jax.numpy as jnp
        import numpy as np
        NUM_HEADS = 8
        ATTENTION_SPAN = 128
        LOOKAHEAD = True
        NEG_INF = -1000000000.0

        def _band_mask(S: int) -> jnp.ndarray:
            idx = jnp.arange(S)
            m = jnp.abs(idx[None, :] - idx[:, None]) <= ATTENTION_SPAN
            if not LOOKAHEAD:
                m = m & (idx[None, :] <= idx[:, None])
            return m
        key = jax.random.key(seed)
        k1, k2, k3 = jax.random.split(key, 3)
        B, S, D = (4, 512, 128)
        x = jax.random.normal(k1, (B, S, D), dtype=jnp.float32)
        w_qkv = jax.random.normal(k2, (D, 3 * D), dtype=jnp.float32) * D ** (-0.5)
        w_proj = jax.random.normal(k3, (D, D), dtype=jnp.float32) * D ** (-0.5)
        return {'x': x, 'w_qkv': w_qkv, 'w_proj': w_proj}
    _L0_attn_all = _L0_attn_setup()
    _L0_attn_in = {k: v for k, v in _L0_attn_all.items() if k in ('w_qkv', 'w_proj')}
    del _L0_attn_all

    def _L0_ffn_setup():
        import jax, jax.numpy as jnp
        import numpy as np
        B, S, H = (4, 1024, 128)
        E, K = (64, 8)
        IE, IS = (128, 352)
        key = jax.random.key(seed)
        ks = jax.random.split(key, 8)
        scale = 0.02
        return {'x': jax.random.normal(ks[0], (B, S, H), jnp.float32), 'gate_w': jax.random.normal(ks[1], (E, H), jnp.float32) * scale, 'w1': jax.random.normal(ks[2], (E, H, IE), jnp.float32) * scale, 'w3': jax.random.normal(ks[3], (E, H, IE), jnp.float32) * scale, 'w2': jax.random.normal(ks[4], (E, IE, H), jnp.float32) * scale, 'sw1': jax.random.normal(ks[5], (H, IS), jnp.float32) * scale, 'sw3': jax.random.normal(ks[6], (H, IS), jnp.float32) * scale, 'sw2': jax.random.normal(ks[7], (IS, H), jnp.float32) * scale}
    _L0_ffn_all = _L0_ffn_setup()
    _L0_ffn_in = {k: v for k, v in _L0_ffn_all.items() if k in ('gate_w', 'w1', 'w3', 'w2', 'sw1', 'sw3', 'sw2')}
    del _L0_ffn_all

    def _L1_attn_setup():
        import jax, jax.numpy as jnp
        import numpy as np
        from jax import lax
        B, T, D, H = (2, 512, 128, 8)
        HD = D // H
        EPS = 1e-05

        def _layernorm(x, g, b):
            m = jnp.mean(x, axis=-1, keepdims=True)
            v = jnp.var(x, axis=-1, keepdims=True)
            return (x - m) / jnp.sqrt(v + EPS) * g + b
        key = jax.random.key(seed)
        ks = jax.random.split(key, 16)
        s = 0.02
        return {'x': jax.random.normal(ks[0], (B, T, D), jnp.float32), 'pe': jax.random.normal(ks[1], (B, T, D), jnp.float32), 'conv_w': jax.random.normal(ks[2], (D, D, 3), jnp.float32) * s, 'conv_b': jnp.zeros((D,), jnp.float32), 'in_proj_w': jax.random.normal(ks[3], (3 * D, D), jnp.float32) * s, 'in_proj_b': jnp.zeros((3 * D,), jnp.float32), 'out_proj_w': jax.random.normal(ks[4], (D, D), jnp.float32) * s, 'out_proj_b': jnp.zeros((D,), jnp.float32), 'ln1_g': jnp.ones((D,), jnp.float32), 'ln1_b': jnp.zeros((D,), jnp.float32), 'w1': jax.random.normal(ks[5], (2 * D, D), jnp.float32) * s, 'b1': jnp.zeros((2 * D,), jnp.float32), 'w2': jax.random.normal(ks[6], (D, 2 * D), jnp.float32) * s, 'b2': jnp.zeros((D,), jnp.float32), 'ln2_g': jnp.ones((D,), jnp.float32), 'ln2_b': jnp.zeros((D,), jnp.float32)}
    _L1_attn_all = _L1_attn_setup()
    _L1_attn_in = {k: v for k, v in _L1_attn_all.items() if k in ('pe', 'conv_w', 'conv_b', 'in_proj_w', 'in_proj_b', 'out_proj_w', 'out_proj_b', 'ln1_g', 'ln1_b', 'w1', 'b1', 'w2', 'b2', 'ln2_g', 'ln2_b')}
    del _L1_attn_all

    def _L1_ffn_setup():
        import jax, jax.numpy as jnp
        import numpy as np
        from jax import lax
        B, S, IN, D, E, NH = (8, 128, 128, 256, 4, 16)
        DH = D // NH
        EPS = 1e-05
        SCALE = np.float32(1.0 / np.sqrt(DH))

        def _ln(x, g, b):
            m = x.mean(-1, keepdims=True)
            v = ((x - m) ** 2).mean(-1, keepdims=True)
            return (x - m) * lax.rsqrt(v + EPS) * g + b

        def _lstm_dir(x, Wi, Wh, b):
            bsz = x.shape[0]
            h0 = jnp.zeros((bsz, Wh.shape[0]), x.dtype)

            def step(carry, xt):
                h, c = carry
                zg = xt @ Wi + h @ Wh + b
                i, f, g, o = jnp.split(zg, 4, axis=-1)
                c = jax.nn.sigmoid(f) * c + jax.nn.sigmoid(i) * jnp.tanh(g)
                h = jax.nn.sigmoid(o) * jnp.tanh(c)
                return ((h, c), h)
            _, hs = lax.scan(step, (h0, h0), jnp.swapaxes(x, 0, 1))
            return jnp.swapaxes(hs, 0, 1)

        def _expert(x, p):
            ew1, eb1, ew2, eb2, eg, ebeta, aiw, aib, aow, aob, wif, whf, bf, wibk, whbk, bbk, sw1, sb1, sw2, sb2, tw1, tb1, tw2, tb2, dw1, db1, dw2, db2, dg, dbeta = p
            h = _ln(jax.nn.relu(x @ ew1 + eb1) @ ew2 + eb2, eg, ebeta)
            qkv = h @ aiw + aib
            q, k, v = jnp.split(qkv, 3, axis=-1)

            def heads(t):
                return t.reshape(t.shape[0], t.shape[1], NH, DH).transpose(0, 2, 1, 3)
            q, k, v = (heads(q), heads(k), heads(v))
            attn = jax.nn.softmax(jnp.einsum('bhqd,bhkd->bhqk', q, k) * SCALE, axis=-1)
            o = jnp.einsum('bhqk,bhkd->bhqd', attn, v).transpose(0, 2, 1, 3).reshape(h.shape)
            h = o @ aow + aob
            hf = _lstm_dir(h, wif, whf, bf)
            hb = _lstm_dir(h[:, ::-1], wibk, whbk, bbk)[:, ::-1]
            mem = jnp.concatenate([hf, hb], axis=-1)
            gate_s = jax.nn.sigmoid(jax.nn.relu(mem @ sw1 + sb1) @ sw2 + sb2)
            gate_t = jnp.tanh(jax.nn.relu(mem @ tw1 + tb1) @ tw2 + tb2)
            g = gate_s * gate_t
            return _ln(jax.nn.relu(g @ dw1 + db1) @ dw2 + db2, dg, dbeta)

        def _forward(x, router_w, router_b, *p):
            outs = jax.vmap(lambda pe: _expert(x, pe))(tuple(p))
            w = jax.nn.softmax(x @ router_w + router_b, axis=-1)
            return jnp.einsum('ebsd,bse->bsd', outs, w)
        key = jax.random.key(seed)
        ks = iter(jax.random.split(key, 64))

        def rn(shape, scale=0.02):
            return jax.random.normal(next(ks), shape, dtype=jnp.float32) * scale
        z = lambda shape: jnp.zeros(shape, dtype=jnp.float32)
        return {'x': jax.random.normal(next(ks), (B, S, IN), dtype=jnp.float32), 'router_w': rn((IN, E)), 'router_b': z((E,)), 'enc_w1': rn((E, IN, D)), 'enc_b1': z((E, D)), 'enc_w2': rn((E, D, D)), 'enc_b2': z((E, D)), 'enc_g': jnp.ones((E, D), jnp.float32), 'enc_beta': z((E, D)), 'attn_in_w': rn((E, D, 3 * D)), 'attn_in_b': z((E, 3 * D)), 'attn_out_w': rn((E, D, D)), 'attn_out_b': z((E, D)), 'lstm_wi_f': rn((E, D, 4 * D)), 'lstm_wh_f': rn((E, D, 4 * D)), 'lstm_b_f': z((E, 4 * D)), 'lstm_wi_b': rn((E, D, 4 * D)), 'lstm_wh_b': rn((E, D, 4 * D)), 'lstm_b_b': z((E, 4 * D)), 'sig_w1': rn((E, 2 * D, D)), 'sig_b1': z((E, D)), 'sig_w2': rn((E, D, D)), 'sig_b2': z((E, D)), 'tan_w1': rn((E, 2 * D, D)), 'tan_b1': z((E, D)), 'tan_w2': rn((E, D, D)), 'tan_b2': z((E, D)), 'dec_w1': rn((E, D, D)), 'dec_b1': z((E, D)), 'dec_w2': rn((E, D, IN)), 'dec_b2': z((E, IN)), 'dec_g': jnp.ones((E, IN), jnp.float32), 'dec_beta': z((E, IN))}
    _L1_ffn_all = _L1_ffn_setup()
    _L1_ffn_in = {k: v for k, v in _L1_ffn_all.items() if k in ('router_w', 'router_b', 'enc_w1', 'enc_b1', 'enc_w2', 'enc_b2', 'enc_g', 'enc_beta', 'attn_in_w', 'attn_in_b', 'attn_out_w', 'attn_out_b', 'lstm_wi_f', 'lstm_wh_f', 'lstm_b_f', 'lstm_wi_b', 'lstm_wh_b', 'lstm_b_b', 'sig_w1', 'sig_b1', 'sig_w2', 'sig_b2', 'tan_w1', 'tan_b1', 'tan_w2', 'tan_b2', 'dec_w1', 'dec_b1', 'dec_w2', 'dec_b2', 'dec_g', 'dec_beta')}
    del _L1_ffn_all
    return {'x': x, 'L0_tok_w': _L0_tok_in['w'], 'L0_attn_w_qkv': _L0_attn_in['w_qkv'], 'L0_attn_w_proj': _L0_attn_in['w_proj'], 'L0_ffn_gate_w': _L0_ffn_in['gate_w'], 'L0_ffn_w1': _L0_ffn_in['w1'], 'L0_ffn_w3': _L0_ffn_in['w3'], 'L0_ffn_w2': _L0_ffn_in['w2'], 'L0_ffn_sw1': _L0_ffn_in['sw1'], 'L0_ffn_sw3': _L0_ffn_in['sw3'], 'L0_ffn_sw2': _L0_ffn_in['sw2'], 'L1_attn_pe': _L1_attn_in['pe'], 'L1_attn_conv_w': _L1_attn_in['conv_w'], 'L1_attn_conv_b': _L1_attn_in['conv_b'], 'L1_attn_in_proj_w': _L1_attn_in['in_proj_w'], 'L1_attn_in_proj_b': _L1_attn_in['in_proj_b'], 'L1_attn_out_proj_w': _L1_attn_in['out_proj_w'], 'L1_attn_out_proj_b': _L1_attn_in['out_proj_b'], 'L1_attn_ln1_g': _L1_attn_in['ln1_g'], 'L1_attn_ln1_b': _L1_attn_in['ln1_b'], 'L1_attn_w1': _L1_attn_in['w1'], 'L1_attn_b1': _L1_attn_in['b1'], 'L1_attn_w2': _L1_attn_in['w2'], 'L1_attn_b2': _L1_attn_in['b2'], 'L1_attn_ln2_g': _L1_attn_in['ln2_g'], 'L1_attn_ln2_b': _L1_attn_in['ln2_b'], 'L1_ffn_router_w': _L1_ffn_in['router_w'], 'L1_ffn_router_b': _L1_ffn_in['router_b'], 'L1_ffn_enc_w1': _L1_ffn_in['enc_w1'], 'L1_ffn_enc_b1': _L1_ffn_in['enc_b1'], 'L1_ffn_enc_w2': _L1_ffn_in['enc_w2'], 'L1_ffn_enc_b2': _L1_ffn_in['enc_b2'], 'L1_ffn_enc_g': _L1_ffn_in['enc_g'], 'L1_ffn_enc_beta': _L1_ffn_in['enc_beta'], 'L1_ffn_attn_in_w': _L1_ffn_in['attn_in_w'], 'L1_ffn_attn_in_b': _L1_ffn_in['attn_in_b'], 'L1_ffn_attn_out_w': _L1_ffn_in['attn_out_w'], 'L1_ffn_attn_out_b': _L1_ffn_in['attn_out_b'], 'L1_ffn_lstm_wi_f': _L1_ffn_in['lstm_wi_f'], 'L1_ffn_lstm_wh_f': _L1_ffn_in['lstm_wh_f'], 'L1_ffn_lstm_b_f': _L1_ffn_in['lstm_b_f'], 'L1_ffn_lstm_wi_b': _L1_ffn_in['lstm_wi_b'], 'L1_ffn_lstm_wh_b': _L1_ffn_in['lstm_wh_b'], 'L1_ffn_lstm_b_b': _L1_ffn_in['lstm_b_b'], 'L1_ffn_sig_w1': _L1_ffn_in['sig_w1'], 'L1_ffn_sig_b1': _L1_ffn_in['sig_b1'], 'L1_ffn_sig_w2': _L1_ffn_in['sig_w2'], 'L1_ffn_sig_b2': _L1_ffn_in['sig_b2'], 'L1_ffn_tan_w1': _L1_ffn_in['tan_w1'], 'L1_ffn_tan_b1': _L1_ffn_in['tan_b1'], 'L1_ffn_tan_w2': _L1_ffn_in['tan_w2'], 'L1_ffn_tan_b2': _L1_ffn_in['tan_b2'], 'L1_ffn_dec_w1': _L1_ffn_in['dec_w1'], 'L1_ffn_dec_b1': _L1_ffn_in['dec_b1'], 'L1_ffn_dec_w2': _L1_ffn_in['dec_w2'], 'L1_ffn_dec_b2': _L1_ffn_in['dec_b2'], 'L1_ffn_dec_g': _L1_ffn_in['dec_g'], 'L1_ffn_dec_beta': _L1_ffn_in['dec_beta']}

def reference(x, L0_tok_w, L0_attn_w_qkv, L0_attn_w_proj, L0_ffn_gate_w, L0_ffn_w1, L0_ffn_w3, L0_ffn_w2, L0_ffn_sw1, L0_ffn_sw3, L0_ffn_sw2, L1_attn_pe, L1_attn_conv_w, L1_attn_conv_b, L1_attn_in_proj_w, L1_attn_in_proj_b, L1_attn_out_proj_w, L1_attn_out_proj_b, L1_attn_ln1_g, L1_attn_ln1_b, L1_attn_w1, L1_attn_b1, L1_attn_w2, L1_attn_b2, L1_attn_ln2_g, L1_attn_ln2_b, L1_ffn_router_w, L1_ffn_router_b, L1_ffn_enc_w1, L1_ffn_enc_b1, L1_ffn_enc_w2, L1_ffn_enc_b2, L1_ffn_enc_g, L1_ffn_enc_beta, L1_ffn_attn_in_w, L1_ffn_attn_in_b, L1_ffn_attn_out_w, L1_ffn_attn_out_b, L1_ffn_lstm_wi_f, L1_ffn_lstm_wh_f, L1_ffn_lstm_b_f, L1_ffn_lstm_wi_b, L1_ffn_lstm_wh_b, L1_ffn_lstm_b_b, L1_ffn_sig_w1, L1_ffn_sig_b1, L1_ffn_sig_w2, L1_ffn_sig_b2, L1_ffn_tan_w1, L1_ffn_tan_b1, L1_ffn_tan_w2, L1_ffn_tan_b2, L1_ffn_dec_w1, L1_ffn_dec_b1, L1_ffn_dec_w2, L1_ffn_dec_b2, L1_ffn_dec_g, L1_ffn_dec_beta):
    import jax
    import jax.numpy as jnp

    def _L0_tok_ref(token_ids, w):
        import jax, jax.numpy as jnp
        import numpy as np
        VOCAB = 50257
        D_MODEL = 128
        B, S = (4, 1024)
        return jnp.take(w, token_ids, axis=0)

    def _L0_attn_ref(x, w_qkv, w_proj):
        import jax, jax.numpy as jnp
        import numpy as np
        NUM_HEADS = 8
        ATTENTION_SPAN = 128
        LOOKAHEAD = True
        NEG_INF = -1000000000.0

        def _band_mask(S: int) -> jnp.ndarray:
            idx = jnp.arange(S)
            m = jnp.abs(idx[None, :] - idx[:, None]) <= ATTENTION_SPAN
            if not LOOKAHEAD:
                m = m & (idx[None, :] <= idx[:, None])
            return m
        B, S, D = x.shape
        H = NUM_HEADS
        hd = D // H
        scale = D ** (-0.5)
        qkv = x @ w_qkv
        qkv = qkv.reshape(B, S, H, 3 * hd).transpose(0, 2, 1, 3)
        q, k, v = jnp.split(qkv, 3, axis=-1)
        scores = jnp.einsum('bhqd,bhkd->bhqk', q, k) * scale
        mask = _band_mask(S)[None, None, :, :]
        scores = scores + (1.0 - mask.astype(scores.dtype)) * NEG_INF
        attn = jax.nn.softmax(scores, axis=-1)
        out = jnp.einsum('bhqk,bhkd->bhqd', attn, v)
        out = out.transpose(0, 2, 1, 3).reshape(B, S, D)
        return out @ w_proj

    def _L0_ffn_ref(x, gate_w, w1, w3, w2, sw1, sw3, sw2):
        import jax, jax.numpy as jnp
        import numpy as np
        B, S, H = (4, 1024, 128)
        E, K = (64, 8)
        IE, IS = (128, 352)
        b, s, h = x.shape
        xf = x.reshape(-1, h)
        T = xf.shape[0]
        logits = xf @ gate_w.T
        topk_w, topk_idx = jax.lax.top_k(logits, K)
        topk_w = jax.nn.softmax(topk_w, axis=-1)
        expert_flat = topk_idx.reshape(-1)
        order = jnp.argsort(expert_flat)
        group_sizes = jnp.bincount(expert_flat, length=E).astype(jnp.int32)
        tok_ids = (jnp.arange(T * K) // K)[order]
        xg = xf[tok_ids]
        hid = jax.nn.silu(jax.lax.ragged_dot(xg, w1, group_sizes)) * jax.lax.ragged_dot(xg, w3, group_sizes)
        y = jax.lax.ragged_dot(hid, w2, group_sizes)
        y = y * topk_w.reshape(-1)[order][:, None]
        routed = jnp.zeros_like(xf).at[tok_ids].add(y)
        shared = jax.nn.silu(xf @ sw1) * (xf @ sw3) @ sw2
        return (routed + shared).reshape(b, s, h)

    def _L1_attn_ref(x, pe, conv_w, conv_b, in_proj_w, in_proj_b, out_proj_w, out_proj_b, ln1_g, ln1_b, w1, b1, w2, b2, ln2_g, ln2_b):
        import jax, jax.numpy as jnp
        import numpy as np
        from jax import lax
        B, T, D, H = (2, 512, 128, 8)
        HD = D // H
        EPS = 1e-05

        def _layernorm(x, g, b):
            m = jnp.mean(x, axis=-1, keepdims=True)
            v = jnp.var(x, axis=-1, keepdims=True)
            return (x - m) / jnp.sqrt(v + EPS) * g + b
        Bv, Tv, Dv = x.shape
        window = max(Tv // 4, 1)
        half = window // 2
        idx = jnp.arange(Tv)
        blocked = jnp.abs(idx[:, None] - idx[None, :]) > half
        mask = jnp.where(blocked, -jnp.inf, 0.0).astype(x.dtype)
        xT = jnp.transpose(x, (0, 2, 1))
        v_in = lax.conv_general_dilated(xT, conv_w, window_strides=(1,), padding=((1, 1),), dimension_numbers=('NCH', 'OIH', 'NCH'))
        v_in = jnp.transpose(v_in + conv_b[None, :, None], (0, 2, 1))
        Wq, Wk, Wv = jnp.split(in_proj_w, 3, axis=0)
        bq, bk, bv = jnp.split(in_proj_b, 3, axis=0)
        q = (x @ Wq.T + bq).reshape(Bv, Tv, H, HD).transpose(0, 2, 1, 3)
        k = (x @ Wk.T + bk).reshape(Bv, Tv, H, HD).transpose(0, 2, 1, 3)
        v = (v_in @ Wv.T + bv).reshape(Bv, Tv, H, HD).transpose(0, 2, 1, 3)
        scores = jnp.einsum('bhqd,bhkd->bhqk', q, k) / np.sqrt(HD).astype(x.dtype)
        scores = scores + mask[None, None]
        attn = jax.nn.softmax(scores, axis=-1)
        ctx = jnp.einsum('bhqk,bhkd->bhqd', attn, v)
        ctx = ctx.transpose(0, 2, 1, 3).reshape(Bv, Tv, Dv)
        attn_out = ctx @ out_proj_w.T + out_proj_b
        h = _layernorm(x + attn_out, ln1_g, ln1_b)
        ffn = jax.nn.relu(h @ w1.T + b1) @ w2.T + b2
        return _layernorm(h + ffn, ln2_g, ln2_b)

    def _L1_ffn_ref(x, router_w, router_b, enc_w1, enc_b1, enc_w2, enc_b2, enc_g, enc_beta, attn_in_w, attn_in_b, attn_out_w, attn_out_b, lstm_wi_f, lstm_wh_f, lstm_b_f, lstm_wi_b, lstm_wh_b, lstm_b_b, sig_w1, sig_b1, sig_w2, sig_b2, tan_w1, tan_b1, tan_w2, tan_b2, dec_w1, dec_b1, dec_w2, dec_b2, dec_g, dec_beta):
        import jax, jax.numpy as jnp
        import numpy as np
        from jax import lax
        B, S, IN, D, E, NH = (8, 128, 128, 256, 4, 16)
        DH = D // NH
        EPS = 1e-05
        SCALE = np.float32(1.0 / np.sqrt(DH))

        def _ln(x, g, b):
            m = x.mean(-1, keepdims=True)
            v = ((x - m) ** 2).mean(-1, keepdims=True)
            return (x - m) * lax.rsqrt(v + EPS) * g + b

        def _lstm_dir(x, Wi, Wh, b):
            bsz = x.shape[0]
            h0 = jnp.zeros((bsz, Wh.shape[0]), x.dtype)

            def step(carry, xt):
                h, c = carry
                zg = xt @ Wi + h @ Wh + b
                i, f, g, o = jnp.split(zg, 4, axis=-1)
                c = jax.nn.sigmoid(f) * c + jax.nn.sigmoid(i) * jnp.tanh(g)
                h = jax.nn.sigmoid(o) * jnp.tanh(c)
                return ((h, c), h)
            _, hs = lax.scan(step, (h0, h0), jnp.swapaxes(x, 0, 1))
            return jnp.swapaxes(hs, 0, 1)

        def _expert(x, p):
            ew1, eb1, ew2, eb2, eg, ebeta, aiw, aib, aow, aob, wif, whf, bf, wibk, whbk, bbk, sw1, sb1, sw2, sb2, tw1, tb1, tw2, tb2, dw1, db1, dw2, db2, dg, dbeta = p
            h = _ln(jax.nn.relu(x @ ew1 + eb1) @ ew2 + eb2, eg, ebeta)
            qkv = h @ aiw + aib
            q, k, v = jnp.split(qkv, 3, axis=-1)

            def heads(t):
                return t.reshape(t.shape[0], t.shape[1], NH, DH).transpose(0, 2, 1, 3)
            q, k, v = (heads(q), heads(k), heads(v))
            attn = jax.nn.softmax(jnp.einsum('bhqd,bhkd->bhqk', q, k) * SCALE, axis=-1)
            o = jnp.einsum('bhqk,bhkd->bhqd', attn, v).transpose(0, 2, 1, 3).reshape(h.shape)
            h = o @ aow + aob
            hf = _lstm_dir(h, wif, whf, bf)
            hb = _lstm_dir(h[:, ::-1], wibk, whbk, bbk)[:, ::-1]
            mem = jnp.concatenate([hf, hb], axis=-1)
            gate_s = jax.nn.sigmoid(jax.nn.relu(mem @ sw1 + sb1) @ sw2 + sb2)
            gate_t = jnp.tanh(jax.nn.relu(mem @ tw1 + tb1) @ tw2 + tb2)
            g = gate_s * gate_t
            return _ln(jax.nn.relu(g @ dw1 + db1) @ dw2 + db2, dg, dbeta)

        def _forward(x, router_w, router_b, *p):
            outs = jax.vmap(lambda pe: _expert(x, pe))(tuple(p))
            w = jax.nn.softmax(x @ router_w + router_b, axis=-1)
            return jnp.einsum('ebsd,bse->bsd', outs, w)
        return _forward(x, router_w, router_b, enc_w1, enc_b1, enc_w2, enc_b2, enc_g, enc_beta, attn_in_w, attn_in_b, attn_out_w, attn_out_b, lstm_wi_f, lstm_wh_f, lstm_b_f, lstm_wi_b, lstm_wh_b, lstm_b_b, sig_w1, sig_b1, sig_w2, sig_b2, tan_w1, tan_b1, tan_w2, tan_b2, dec_w1, dec_b1, dec_w2, dec_b2, dec_g, dec_beta)
    h = _L0_tok_ref(x, L0_tok_w)
    h = h + _L0_attn_ref(_layernorm(h, axis=-1), L0_attn_w_qkv, L0_attn_w_proj)
    h = h + _L0_ffn_ref(_layernorm(h, axis=-1), L0_ffn_gate_w, L0_ffn_w1, L0_ffn_w3, L0_ffn_w2, L0_ffn_sw1, L0_ffn_sw3, L0_ffn_sw2)
    h = h + _L1_attn_ref(_layernorm(h, axis=-1), L1_attn_pe, L1_attn_conv_w, L1_attn_conv_b, L1_attn_in_proj_w, L1_attn_in_proj_b, L1_attn_out_proj_w, L1_attn_out_proj_b, L1_attn_ln1_g, L1_attn_ln1_b, L1_attn_w1, L1_attn_b1, L1_attn_w2, L1_attn_b2, L1_attn_ln2_g, L1_attn_ln2_b)
    h = h + _L1_ffn_ref(_layernorm(h, axis=-1), L1_ffn_router_w, L1_ffn_router_b, L1_ffn_enc_w1, L1_ffn_enc_b1, L1_ffn_enc_w2, L1_ffn_enc_b2, L1_ffn_enc_g, L1_ffn_enc_beta, L1_ffn_attn_in_w, L1_ffn_attn_in_b, L1_ffn_attn_out_w, L1_ffn_attn_out_b, L1_ffn_lstm_wi_f, L1_ffn_lstm_wh_f, L1_ffn_lstm_b_f, L1_ffn_lstm_wi_b, L1_ffn_lstm_wh_b, L1_ffn_lstm_b_b, L1_ffn_sig_w1, L1_ffn_sig_b1, L1_ffn_sig_w2, L1_ffn_sig_b2, L1_ffn_tan_w1, L1_ffn_tan_b1, L1_ffn_tan_w2, L1_ffn_tan_b2, L1_ffn_dec_w1, L1_ffn_dec_b1, L1_ffn_dec_w2, L1_ffn_dec_b2, L1_ffn_dec_g, L1_ffn_dec_beta)
    return h

_drawn_inputs = setup_inputs


def setup_inputs(seed=0):
    import zlib

    import numpy as np

    out = dict(_drawn_inputs(seed))
    spreads = {'L1_attn_conv_b': (0.0, 0.8),
     'L1_attn_in_proj_b': (0.0, 0.748),
     'L1_attn_out_proj_b': (0.0, 0.39),
     'L1_attn_ln1_g': (1.0, 0.2),
     'L1_attn_ln1_b': (0.0, 0.1),
     'L1_attn_b1': (0.0, 0.8),
     'L1_attn_b2': (0.0, 0.1),
     'L1_attn_ln2_g': (1.0, 0.2),
     'L1_attn_ln2_b': (0.0, 0.1),
     'L1_ffn_router_b': (0.0, 0.3),
     'L1_ffn_enc_b1': (0.0, 0.8),
     'L1_ffn_enc_b2': (0.0, 0.8),
     'L1_ffn_enc_g': (1.0, 0.6),
     'L1_ffn_enc_beta': (0.0, 0.8),
     'L1_ffn_attn_in_b': (0.0, 0.8),
     'L1_ffn_attn_out_b': (0.0, 0.8),
     'L1_ffn_lstm_b_f': (0.0, 2.0),
     'L1_ffn_lstm_b_b': (0.0, 2.0),
     'L1_ffn_sig_b1': (0.0, 0.8),
     'L1_ffn_sig_b2': (0.0, 2.0),
     'L1_ffn_tan_b1': (0.0, 0.8),
     'L1_ffn_tan_b2': (0.0, 0.8),
     'L1_ffn_dec_b1': (0.0, 0.599),
     'L1_ffn_dec_b2': (0.0, 0.1),
     'L1_ffn_dec_g': (1.0, 0.2),
     'L1_ffn_dec_beta': (0.0, 0.332)}
    factors = {'L0_ffn_gate_w': 8.0,
     'L0_ffn_w1': 8.0,
     'L0_ffn_w3': 8.0,
     'L0_ffn_w2': 8.0,
     'L0_ffn_sw1': 6.036,
     'L0_ffn_sw3': 6.027,
     'L0_ffn_sw2': 6.046,
     'L1_attn_conv_w': 8.0,
     'L1_attn_in_proj_w': 8.0,
     'L1_attn_out_proj_w': 5.148,
     'L1_attn_w1': 2.715,
     'L1_ffn_enc_w1': 8.0,
     'L1_ffn_enc_w2': 8.0,
     'L1_ffn_attn_in_w': 8.0,
     'L1_ffn_attn_out_w': 8.0,
     'L1_ffn_lstm_wi_f': 8.0,
     'L1_ffn_lstm_wh_f': 8.0,
     'L1_ffn_lstm_wi_b': 8.0,
     'L1_ffn_lstm_wh_b': 8.0,
     'L1_ffn_sig_w1': 8.0,
     'L1_ffn_sig_w2': 8.0,
     'L1_ffn_tan_w1': 8.0,
     'L1_ffn_tan_w2': 8.0,
     'L1_ffn_dec_w1': 6.303}
    for name, (base, spread) in spreads.items():
        noise = np.random.default_rng([zlib.crc32(name.encode()), seed]).standard_normal(out[name].shape)
        drawn = base * np.exp(spread * noise) if base else spread * noise
        out[name] = jnp.asarray(drawn.astype(out[name].dtype))
    for name, factor in factors.items():
        out[name] = (out[name] * factor).astype(out[name].dtype)
    return out
```

```python
import numpy as np
from contextlib import ExitStack

import concourse.bass as bass
from concourse import mybir
from concourse.alu_op_type import AluOpType as ALU

F32 = mybir.dt.float32
BF16 = mybir.dt.bfloat16
I32 = mybir.dt.int32
ACT = mybir.ActivationFunctionType
AX = mybir.AxisListType.X

P = 128
T = 2048
D = 128
TILES = T // P
BLK = 512
BLKS = T // BLK
EPS = 1e-5
NEG = -1e30
HEADS = 8
HD = D // HEADS


class Core:

    def __init__(self, nc, ctx):
        self.nc = nc
        self.loaded = nc.alloc_semaphore("loaded")
        self.loaded_odd = nc.alloc_semaphore("loaded_odd")
        self.stored = nc.alloc_semaphore("stored")
        self.multiplied = nc.alloc_semaphore("multiplied")
        self.evacuated = nc.alloc_semaphore("evacuated")
        self.activated = nc.alloc_semaphore("activated")
        self.stepped = nc.alloc_semaphore("stepped")
        self.vectored = nc.alloc_semaphore("vectored")
        self.transposed = nc.alloc_semaphore("transposed")
        self.copied = nc.alloc_semaphore("copied")
        self.scored = nc.alloc_semaphore("scored")
        self.reduced = nc.alloc_semaphore("reduced")
        self.turned = nc.alloc_semaphore("turned")
        self.pooled = nc.alloc_semaphore("pooled")
        self.gathered = nc.alloc_semaphore("gathered")
        self.first, self.last = self.loaded.num, self.pooled.num
        self.count = 0
        self.psum = ctx.enter_context(nc.psum_tensor("banks", [P, 8, BLK], F32))
        self.ident = ctx.enter_context(nc.sbuf_tensor("ident", [P, P], F32))
        self.identb = ctx.enter_context(nc.sbuf_tensor("identb", [P, P], BF16))
        self.headmask = ctx.enter_context(nc.sbuf_tensor("headmask", [P, HEADS], F32))
        self.x = ctx.enter_context(nc.sbuf_tensor("x_resid", [P, TILES, D], F32))

    def sb(self, mem, name, shape, dtype=F32):
        self.count += 1
        return mem.enter_context(self.nc.sbuf_tensor(f"{name}_{self.count}", shape, dtype))

    def clear(self):
        with self.nc.Block() as block:
            @block.vector
            def _(dve):
                dve.sem_clear(range(self.first, self.last + 1))


class Chain:

    def __init__(self, eng, sem):
        self.eng, self.sem, self.n = eng, sem, 0

    def __call__(self, ins):
        self.n += 1
        ins.then_inc(self.sem, 1)
        self.eng.wait_ge(self.sem, self.n)


def constants(c):
    nc = c.nc
    with nc.Block() as block:
        @block.gpsimd
        def _(pool):
            step = Chain(pool, c.pooled)
            step(nc.gpsimd.memset(c.ident[:, :], 0.0))
            step(nc.gpsimd.affine_select(out=c.ident[:, :], in_=c.ident[:, :], compare_op=ALU.not_equal,
                                         fill=1.0, base=0, pattern=[[-1, P]], channel_multiplier=1))
            step(nc.gpsimd.memset(c.identb[:, :], 0.0))
            step(nc.gpsimd.affine_select(out=c.identb[:, :], in_=c.identb[:, :], compare_op=ALU.not_equal,
                                         fill=1.0, base=0, pattern=[[-1, P]], channel_multiplier=1))
            step(nc.gpsimd.memset(c.headmask[:, :], 1.0))
            step(nc.gpsimd.affine_select(out=c.headmask[:, :], in_=c.headmask[:, :], compare_op=ALU.is_ge,
                                         fill=0.0, base=0, pattern=[[-HD, HEADS]], channel_multiplier=1))
            step(nc.gpsimd.affine_select(out=c.headmask[:, :], in_=c.headmask[:, :], compare_op=ALU.is_ge,
                                         fill=0.0, base=HD - 1, pattern=[[HD, HEADS]], channel_multiplier=-1))
    c.clear()


def gather(c, ids, table):
    nc = c.nc
    with nc.sbuf_tensor("token_ids", [P, TILES], I32) as idx, nc.Block() as block:
        @block.gpsimd
        def _(pool):
            nc.gpsimd.dma_start(idx[:, :], ids).then_inc(c.gathered, 16)
            pool.wait_ge(c.gathered, 16)
            for i in range(TILES):
                nc.gpsimd.indirect_dma_start(
                    out=c.x[:, i, :], out_offset=None, in_=table,
                    in_offset=bass.IndirectOffsetOnAxis(ap=idx[:, i:i + 1], axis=0),
                ).then_inc(c.gathered, 16)
            pool.wait_ge(c.gathered, 16 * (TILES + 1))


def normalize(c, src, dst, n, width, gamma=None, beta=None, loads=(), plus=None, residual=None):
    nc = c.nc
    with ExitStack() as mem:
        sq = c.sb(mem, "ln_squares", [P, n, width])
        mean = c.sb(mem, "ln_mean", [P, n])
        var = c.sb(mem, "ln_var", [P, n])
        std = c.sb(mem, "ln_std", [P, n])
        block = mem.enter_context(nc.Block())

        def wide(ap):
            return ap.unsqueeze(2).to_broadcast([P, n, width])

        def row(ap):
            return ap.unsqueeze(1).to_broadcast([P, n, width])

        @block.sync
        def _(sp):
            for to, frm in loads:
                sp.dma_start(to, frm).then_inc(c.loaded, 16)
            if loads:
                sp.wait_ge(c.loaded, 16 * len(loads))

        @block.vector
        def _(dve):
            step = Chain(dve, c.stepped)
            inp = src
            if plus is not None:
                step(nc.vector.tensor_tensor(dst, src, plus, ALU.add))
                inp = dst
            step(nc.vector.tensor_reduce(mean[:, :], inp, AX, ALU.add))
            step(nc.vector.tensor_scalar(mean[:, :], mean[:, :], 1.0 / width, None, ALU.mult))
            step(nc.vector.tensor_tensor(dst, inp, wide(mean[:, :]), ALU.subtract))
            step(nc.vector.tensor_tensor(sq[:, :, :], dst, dst, ALU.mult))
            step(nc.vector.tensor_reduce(var[:, :], sq[:, :, :], AX, ALU.add))
            nc.vector.tensor_scalar(var[:, :], var[:, :], 1.0 / width, EPS, ALU.mult, ALU.add).then_inc(c.vectored, 1)
            dve.wait_ge(c.activated, 1)
            step(nc.vector.reciprocal(std[:, :], std[:, :]))
            step(nc.vector.tensor_tensor(dst, dst, wide(std[:, :]), ALU.mult))
            if gamma is not None:
                step(nc.vector.tensor_tensor(dst, dst, row(gamma), ALU.mult))
                step(nc.vector.tensor_tensor(dst, dst, row(beta), ALU.add))
            if residual is not None:
                step(nc.vector.tensor_tensor(residual, residual, dst, ALU.add))

        @block.scalar
        def _(act):
            act.wait_ge(c.vectored, 1)
            nc.scalar.activation(std[:, :], var[:, :], ACT.Sqrt).then_inc(c.activated, 1)
    c.clear()


def transpose_tiles(c, tiles):
    nc = c.nc
    with nc.Block() as block:
        @block.tensor
        def _(pe):
            for j, (sources, _) in enumerate(tiles):
                if j >= 8:
                    pe.wait_ge(c.evacuated, j - 7)
                for q, source in enumerate(sources):
                    last = nc.tensor.transpose(c.psum[:, j % 8, q * P:(q + 1) * P], source, c.ident[:, :])
                last.then_inc(c.transposed, 1)

        @block.scalar
        def _(act):
            for j, (sources, target) in enumerate(tiles):
                act.wait_ge(c.transposed, j + 1)
                nc.scalar.activation(target, c.psum[:, j % 8, :len(sources) * P], ACT.Copy).then_inc(c.evacuated, 1)
    c.clear()


def dense_features(c, xT, w, kt, mt, out, func, bias=None, loads=(), m_size=P):
    nc = c.nc
    jobs = [(m, b) for m in range(mt) for b in range(BLKS)]
    with nc.Block() as block:
        @block.sync
        def _(sp):
            for to, frm in loads:
                sp.dma_start(to, frm).then_inc(c.loaded, 16)

        @block.tensor
        def _(pe):
            if loads:
                pe.wait_ge(c.loaded, 16 * len(loads))
            for j, (m, b) in enumerate(jobs):
                if j >= 8:
                    pe.wait_ge(c.evacuated, j - 7)
                for k in range(kt):
                    last = nc.tensor.matmul(c.psum[0:m_size, j % 8, :], w(k, m), xT(k, b),
                                            start=(k == 0), stop=(k == kt - 1))
                last.then_inc(c.multiplied, 1)

        @block.scalar
        def _(act):
            if loads:
                act.wait_ge(c.loaded, 16 * len(loads))
            for j, (m, b) in enumerate(jobs):
                act.wait_ge(c.multiplied, j + 1)
                if bias is None:
                    ins = nc.scalar.activation(out(m, b), c.psum[0:m_size, j % 8, :], func)
                else:
                    ins = nc.scalar.activation(out(m, b), c.psum[0:m_size, j % 8, :], func, bias=bias(m))
                ins.then_inc(c.evacuated, 1)
    c.clear()


def dense_tokens(c, xT, w, kt, cols, out, plus=None, loads=(), scale=None):
    nc = c.nc
    jobs = [(i, n) for i in range(TILES) for n in range(len(cols))]
    with nc.Block() as block:
        @block.sync
        def _(sp):
            for to, frm in loads:
                sp.dma_start(to, frm).then_inc(c.loaded, 16)

        @block.tensor
        def _(pe):
            if loads:
                pe.wait_ge(c.loaded, 16 * len(loads))
            for j, (i, n) in enumerate(jobs):
                if j >= 8:
                    pe.wait_ge(c.evacuated, j - 7)
                for k in range(kt):
                    last = nc.tensor.matmul(c.psum[:, j % 8, 0:cols[n]], xT(k, i), w(k, n),
                                            start=(k == 0), stop=(k == kt - 1))
                last.then_inc(c.multiplied, 1)

        @block.vector
        def _(dve):
            if loads:
                dve.wait_ge(c.loaded, 16 * len(loads))
            for j, (i, n) in enumerate(jobs):
                dve.wait_ge(c.multiplied, j + 1)
                ps = c.psum[:, j % 8, 0:cols[n]]
                if plus is None:
                    ins = nc.vector.tensor_copy(out(i, n), ps)
                else:
                    ins = nc.vector.tensor_tensor(out(i, n), ps, plus(i, n), ALU.add)
                ins.then_inc(c.evacuated, 1)
    c.clear()


def windowed_attention(c, qT, kTm, v, oT, w, scale):
    nc = c.nc
    span = 2 * w + 1
    hb = 8 if span * P <= BLK else 4
    per = 8 // hb
    with ExitStack() as mem:
        mask = c.sb(mem, "band_mask", [P, span * P])
        s = c.sb(mem, "scores", [P, hb, span * P])
        pT = c.sb(mem, "probs_T", [P, hb * span, P])
        qt = c.sb(mem, "q_tile", [P, P])
        mx = c.sb(mem, "row_max", [P, HEADS])
        total = c.sb(mem, "row_sum", [P, HEADS])
        o = c.sb(mem, "o_tile", [P, D])

        with nc.Block() as block:
            @block.gpsimd
            def _(pool):
                step = Chain(pool, c.pooled)
                step(nc.gpsimd.memset(mask[:, :], 0.0))
                step(nc.gpsimd.affine_select(out=mask[:, :], in_=mask[:, :], compare_op=ALU.is_ge, fill=NEG,
                                             base=0, pattern=[[1, span * P]], channel_multiplier=-1))
                step(nc.gpsimd.affine_select(out=mask[:, :], in_=mask[:, :], compare_op=ALU.is_ge, fill=NEG,
                                             base=2 * w * P, pattern=[[-1, span * P]], channel_multiplier=1))
        c.clear()

        def tile(i, lo, n, skip):
            cols = n * P
            banks = c.psum[:, :, :].rearrange("p (h two) f -> p h (two f)", two=per)
            flat = c.psum[:, :, :].rearrange("p b f -> p (b f)")
            for h0 in range(0, HEADS, hb):
                heads = range(h0, h0 + hb)
                with nc.Block() as block:
                    @block.tensor
                    def _(pe):
                        pe.wait_ge(c.stepped, 1)
                        for h in heads:
                            for at in range(0, cols, BLK):
                                size = min(BLK, cols - at)
                                last = nc.tensor.matmul(banks[:, h - h0, at:at + size], qt[:, :],
                                                        kTm[:, h, bass.ds(lo * P + at, size)], start=True, stop=True)
                        last.then_inc(c.multiplied, 1)
                        pe.wait_ge(c.activated, hb)
                        for j in range(hb * n):
                            h, kt = divmod(j, n)
                            last = nc.tensor.transpose(flat[:, j * P:(j + 1) * P], s[:, h, kt * P:(kt + 1) * P],
                                                       c.ident[:, :])
                        last.then_inc(c.transposed, 1)
                        pe.wait_ge(c.copied, 1)
                        for h in heads:
                            for kt in range(n):
                                last = nc.tensor.matmul(c.psum[:, 7, h * HD:(h + 1) * HD], pT[:, (h - h0) * n + kt, :],
                                                        v[:, bass.ds(lo + kt, 1), h * HD:(h + 1) * HD],
                                                        start=(kt == 0), stop=(kt == n - 1))
                        last.then_inc(c.multiplied, 1)
                        if h0 + hb == HEADS:
                            pe.wait_ge(c.vectored, 2)
                            nc.tensor.transpose(c.psum[:, 6, 0:P], o[:, :], c.ident[:, :]).then_inc(c.transposed, 1)

                    @block.vector
                    def _(dve):
                        step = Chain(dve, c.stepped)
                        step(nc.vector.tensor_copy(qt[:, :], qT[:, bass.ds(i * P, P)]))
                        dve.wait_ge(c.multiplied, 1)
                        step(nc.vector.tensor_tensor(
                            s[:, :, 0:cols], banks[:, 0:hb, 0:cols],
                            mask[:, skip:skip + cols].unsqueeze(1).to_broadcast([P, hb, cols]), ALU.add))
                        step(nc.vector.tensor_reduce(mx[:, 0:hb], s[:, :, 0:cols], AX, ALU.max))
                        nc.vector.tensor_scalar(mx[:, 0:hb], mx[:, 0:hb], -scale, None, ALU.mult).then_inc(c.vectored, 1)
                        dve.wait_ge(c.activated, hb)
                        step(nc.vector.reciprocal(total[:, 0:hb], total[:, 0:hb]))
                        dve.wait_ge(c.multiplied, 2)
                        nc.vector.tensor_tensor(
                            o[:, h0 * HD:(h0 + hb) * HD].rearrange("p (h d) -> p h d", d=HD),
                            c.psum[:, 7, h0 * HD:(h0 + hb) * HD].rearrange("p (h d) -> p h d", d=HD),
                            total[:, 0:hb].unsqueeze(2).to_broadcast([P, hb, HD]), ALU.mult).then_inc(c.vectored, 1)

                    @block.scalar
                    def _(act):
                        act.wait_ge(c.vectored, 1)
                        for j in range(hb):
                            nc.scalar.activation(s[:, j, 0:cols], s[:, j, 0:cols], ACT.Exp, bias=mx[:, j:j + 1],
                                                 scale=scale, accum_out=total[:, j:j + 1]).then_inc(c.activated, 1)
                        act.wait_ge(c.transposed, 1)
                        nc.scalar.activation(pT[:, 0:hb * n, :].rearrange("p a b -> p (a b)"), flat[:, 0:hb * n * P],
                                             ACT.Copy).then_inc(c.copied, 1)
                        if h0 + hb == HEADS:
                            act.wait_ge(c.transposed, 2)
                            nc.scalar.activation(oT[:, bass.ds(i * P, P)], c.psum[:, 6, 0:P], ACT.Copy).then_inc(c.copied, 1)
                c.clear()

        for i in range(w):
            tile(i, 0, i + w + 1, (w - i) * P)
        with nc.Fori(w, TILES - w) as i:
            tile(i, i - w, span, 0)
        for i in range(TILES - w, TILES):
            tile(i, i - w, TILES - i + w, 0)


def layer0_attention(c, w_qkv, w_proj):
    nc = c.nc
    with ExitStack() as mem:
        def sb(name, shape):
            return c.sb(mem, name, shape)
        xn = sb("a0_xn", [P, TILES, D])
        xT = sb("a0_xT", [P, T])
        wq = sb("a0_wqkv", [P, 3 * D])
        wp = sb("a0_wproj", [P, D])
        qT, kT, kTm = sb("a0_qT", [P, T]), sb("a0_kT", [P, T]), sb("a0_kTm", [P, HEADS, T])
        v = sb("a0_v", [P, TILES, D])
        normalize(c, c.x[:, :, :], xn[:, :, :], TILES, D)
        transpose_tiles(c, [([xn[:, 4 * b + q, :] for q in range(4)], xT[:, b * BLK:(b + 1) * BLK]) for b in range(BLKS)])
        dense_features(c, lambda k, b: xT[:, b * BLK:(b + 1) * BLK], lambda k, m: wq[:, m * D:(m + 1) * D], 1, 2,
                       lambda m, b: (qT, kT)[m][:, b * BLK:(b + 1) * BLK], ACT.Copy,
                       loads=[(wq[:, :], w_qkv), (wp[:, :], w_proj)])
        dense_tokens(c, lambda k, i: xT[:, i * P:(i + 1) * P], lambda k, n: wq[:, 2 * D:3 * D], 1, [D],
                     lambda i, n: v[:, i, :])
        mask_keys(c, kT, kTm)
        oT = kT
        windowed_attention(c, qT, kTm, v, oT, 1, float(D) ** -0.5)
        dense_tokens(c, lambda k, i: oT[:, i * P:(i + 1) * P], lambda k, n: wp[:, :], 1, [D],
                     lambda i, n: c.x[:, i, :], plus=lambda i, n: c.x[:, i, :])


def mask_keys(c, kT, kTm):
    nc = c.nc
    with nc.Block() as block:
        @block.vector
        def _(dve):
            for h in range(HEADS):
                nc.vector.tensor_scalar(kTm[:, h, :], kT[:, :], c.headmask[:, h:h + 1], None, ALU.mult)
    c.clear()


EXPERTS0, TOPK, SHARED = 64, 8, 352
SHARED_PARTS = [(0, 128), (128, 128), (256, 96)]


def moe(c, gate_wT, w1, w3, w2, sw1, sw3, sw2):
    nc = c.nc
    with ExitStack() as mem:
        def sb(name, shape):
            return c.sb(mem, name, shape)
        xn = sb("m_xn", [P, TILES, D])
        xT = sb("m_xT", [P, T])
        gw = sb("m_gate_w", [P, EXPERTS0])
        logits = sb("m_logits", [P, TILES, EXPERTS0])
        rest = sb("m_rest", [P, TILES, EXPERTS0])
        best = sb("m_best", [P, TILES, TOPK])
        gate = sb("m_gate", [P, TILES, EXPERTS0])
        total = sb("m_total", [P, TILES])
        s1, s3 = sb("m_sw1", [P, SHARED]), sb("m_sw3", [P, SHARED])
        s2 = sb("m_sw2", [P, 3, D])
        normalize(c, c.x[:, :, :], xn[:, :, :], TILES, D)
        transpose_tiles(c, [([xn[:, 4 * b + q, :] for q in range(4)], xT[:, b * BLK:(b + 1) * BLK]) for b in range(BLKS)])
        dense_tokens(c, lambda k, i: xT[:, i * P:(i + 1) * P], lambda k, n: gw[:, :], 1, [EXPERTS0],
                     lambda i, n: logits[:, i, :],
                     loads=[(gw[:, :], gate_wT), (s1[:, :], sw1), (s3[:, :], sw3)]
                     + [(s2[0:n, j, :], sw2[a:a + n, :]) for j, (a, n) in enumerate(SHARED_PARTS)])
        with nc.Block() as block:
            @block.vector
            def _(dve):
                step = Chain(dve, c.stepped)
                for i in range(TILES):
                    nc.vector.max(best[:, i, :], logits[:, i, :]).then_inc(c.vectored, 1)
                for i in range(TILES):
                    dve.wait_ge(c.vectored, i + 1)
                    last = nc.vector.match_replace(rest[:, i, :], best[:, i, :], logits[:, i, :], -3e38)
                step(last)
                step(nc.vector.tensor_tensor(gate[:, :, :], logits[:, :, :],
                                             best[:, :, 0:1].to_broadcast([P, TILES, EXPERTS0]), ALU.subtract))
                step(nc.vector.tensor_tensor(rest[:, :, :], rest[:, :, :], logits[:, :, :], ALU.not_equal))
                dve.wait_ge(c.activated, 1)
                step(nc.vector.tensor_tensor(gate[:, :, :], gate[:, :, :], rest[:, :, :], ALU.mult))
                step(nc.vector.tensor_reduce(total[:, :], gate[:, :, :], AX, ALU.add))
                step(nc.vector.reciprocal(total[:, :], total[:, :]))
                step(nc.vector.tensor_tensor(gate[:, :, :], gate[:, :, :],
                                             total[:, :].unsqueeze(2).to_broadcast([P, TILES, EXPERTS0]), ALU.mult))

            @block.scalar
            def _(act):
                act.wait_ge(c.stepped, 2)
                nc.scalar.activation(gate[:, :, :], gate[:, :, :], ACT.Exp).then_inc(c.activated, 1)
        c.clear()
        shared_expert(c, xT, s1, s3, s2)
        routed_experts(c, xT, gate, w1, w3, w2)


def shared_expert(c, xT, s1, s3, s2):
    nc = c.nc
    parts = len(SHARED_PARTS)
    with ExitStack() as mem:
        hid = c.sb(mem, "m_shared_hidden", [P, parts, T])
        sig = c.sb(mem, "m_sig", [P, 2, BLK])
        jobs = [(m, b) for m in range(parts) for b in range(BLKS)]
        with nc.Block() as block:
            @block.tensor
            def _(pe):
                for j, (m, b) in enumerate(jobs):
                    a, n = SHARED_PARTS[m]
                    if j >= 4:
                        pe.wait_ge(c.evacuated, j - 3)
                    nc.tensor.matmul(c.psum[0:n, 2 * (j % 4), :], s1[:, a:a + n], xT[:, b * BLK:(b + 1) * BLK],
                                     start=True, stop=True)
                    nc.tensor.matmul(c.psum[0:n, 2 * (j % 4) + 1, :], s3[:, a:a + n], xT[:, b * BLK:(b + 1) * BLK],
                                     start=True, stop=True).then_inc(c.multiplied, 1)

            @block.scalar
            def _(act):
                for j, (m, b) in enumerate(jobs):
                    n = SHARED_PARTS[m][1]
                    act.wait_ge(c.multiplied, j + 1)
                    if j >= 2:
                        act.wait_ge(c.evacuated, j - 1)
                    nc.scalar.activation(sig[0:n, j % 2, :], c.psum[0:n, 2 * (j % 4), :], ACT.Sigmoid).then_inc(c.activated, 1)

            @block.vector
            def _(dve):
                step = Chain(dve, c.stepped)
                for j, (m, b) in enumerate(jobs):
                    n = SHARED_PARTS[m][1]
                    h = hid[0:n, m, b * BLK:(b + 1) * BLK]
                    dve.wait_ge(c.activated, j + 1)
                    step(nc.vector.tensor_tensor(h, sig[0:n, j % 2, :], c.psum[0:n, 2 * (j % 4), :], ALU.mult))
                    nc.vector.tensor_tensor(h, h, c.psum[0:n, 2 * (j % 4) + 1, :], ALU.mult).then_inc(c.evacuated, 1)
        c.clear()
        dense_tokens(c, lambda k, i: hid[0:SHARED_PARTS[k][1], k, i * P:(i + 1) * P],
                     lambda k, n: s2[0:SHARED_PARTS[k][1], k, :], parts, [D],
                     lambda i, n: c.x[:, i, :], plus=lambda i, n: c.x[:, i, :])


def routed_experts(c, xT, gate, w1, w3, w2):
    nc = c.nc
    PAIRS = EXPERTS0 // 2
    LAST = (PAIRS - 1) * 8
    with ExitStack() as mem:
        wt = c.sb(mem, "m_weights", [P, 2, 3, D])
        sig = c.sb(mem, "m_sigmoid", [P, 2, BLK])
        hid = c.sb(mem, "m_hidden", [P, 2, BLK])
        hidden, output, added = c.vectored, c.transposed, c.evacuated
        weights = (c.loaded, c.loaded_odd)
        with nc.Block() as block:
            @block.vector
            def _(dve):
                dve.sem_inc(hidden, 2)
                dve.sem_inc(output, 6)
                dve.sem_inc(added, 4)

        with nc.Block() as block:
            @block.sync
            def _(sp):
                with sp.Fori(0, PAIRS) as pair:
                    for par in range(2):
                        sp.wait_ge(output, pair * 8 + (4 * par + 2))
                        for j, w in enumerate((w1, w3, w2)):
                            sp.dma_start(wt[:, par, j, :], w[bass.ds(pair * 2 + par, 1), :, :].rearrange("a p n -> p (a n)")
                                         ).then_inc(weights[par], 16)

            @block.tensor
            def _(pe):
                def up(n0, pos):
                    b, par, q = pos % 4, pos // 4 % 2, pos % 2
                    if b == 0:
                        pe.wait_ge(weights[par], (n0 + pos - 4 * par) * 6 + 48)
                    pe.wait_ge(hidden, n0 + pos + 1)
                    nc.tensor.matmul(c.psum[:, 2 * q, :], wt[:, par, 0, :], xT[:, b * BLK:(b + 1) * BLK],
                                     start=True, stop=True)
                    nc.tensor.matmul(c.psum[:, 2 * q + 1, :], wt[:, par, 1, :], xT[:, b * BLK:(b + 1) * BLK],
                                     start=True, stop=True).then_inc(c.multiplied, 1)

                def down(n0, pos):
                    par, q = pos // 4 % 2, pos % 2
                    pe.wait_ge(hidden, n0 + pos + 3)
                    pe.wait_ge(added, n0 + pos + 3)
                    for t in range(4):
                        last = nc.tensor.matmul(c.psum[:, 4 + q, t * D:(t + 1) * D], hid[:, q, t * P:(t + 1) * P],
                                                wt[:, par, 2, :], start=True, stop=True)
                    last.then_inc(output, 1)

                up(0, 0)
                with pe.Fori(0, PAIRS - 1) as pair:
                    for pos in range(8):
                        up(pair * 8, pos + 1)
                        down(pair * 8, pos)
                for pos in range(8):
                    if pos < 7:
                        up(LAST, pos + 1)
                    down(LAST, pos)

            @block.scalar
            def _(act):
                with act.Fori(0, PAIRS) as pair:
                    for pos in range(8):
                        act.wait_ge(c.multiplied, pair * 8 + (pos + 1))
                        act.wait_ge(hidden, pair * 8 + (pos + 1))
                        nc.scalar.activation(sig[:, pos % 2, :], c.psum[:, 2 * (pos % 2), :], ACT.Sigmoid).then_inc(c.activated, 1)

            @block.vector
            def _(dve):
                def make_hidden(n0, pos):
                    q = pos % 2
                    dve.wait_ge(c.activated, n0 + pos + 1)
                    nc.vector.tensor_tensor(sig[:, q, :], sig[:, q, :], c.psum[:, 2 * q, :], ALU.mult).then_inc(c.stepped, 1)
                    dve.wait_ge(c.stepped, n0 + pos + 1)
                    dve.wait_ge(output, n0 + pos + 5)
                    nc.vector.tensor_tensor(hid[:, q, :], sig[:, q, :], c.psum[:, 2 * q + 1, :], ALU.mult).then_inc(hidden, 1)

                def add(n0, pos, e):
                    b, q = pos % 4, pos % 2
                    dve.wait_ge(output, n0 + pos + 7)
                    dve.wait_ge(added, n0 + pos + 1)
                    for t in range(4):
                        i = 4 * b + t
                        last = nc.vector.scalar_tensor_tensor(
                            out=c.x[:, i, :], in0=c.psum[:, 4 + q, t * D:(t + 1) * D], scalar=gate[:, i, bass.ds(e, 1)],
                            in1=c.x[:, i, :], op0=ALU.mult, op1=ALU.add)
                    last.then_inc(added, 1)

                make_hidden(0, 0)
                with dve.Fori(0, PAIRS - 1) as pair:
                    for pos in range(8):
                        make_hidden(pair * 8, pos + 1)
                        add(pair * 8, pos, pair * 2 + pos // 4)
                for pos in range(8):
                    if pos < 7:
                        make_hidden(LAST, pos + 1)
                    add(LAST, pos, EXPERTS0 - 2 + pos // 4)
        c.clear()


def layer1_attention(c, a):
    nc = c.nc
    with ExitStack() as mem:
        def sb(name, shape):
            return c.sb(mem, name, shape)
        xn = sb("a1_xn", [P, TILES, D])
        xT = sb("a1_xT", [P, T + 2])
        conv, conv_b = sb("a1_conv", [P, 3, D]), sb("a1_conv_b", [P, 1])
        win, qk_b = sb("a1_in_proj", [P, 3 * D]), sb("a1_qk_b", [P, 2])
        v_b, out_b, b2 = sb("a1_v_b", [P, D]), sb("a1_out_b", [P, D]), sb("a1_b2", [P, D])
        ln = sb("a1_ln", [P, 4, D])
        wo, w1, b1, w2 = sb("a1_wo", [P, D]), sb("a1_w1", [P, 2 * D]), sb("a1_b1", [P, 2]), sb("a1_w2", [P, 2, D])
        v = sb("a1_v", [P, TILES, D])
        h = sb("a1_h", [P, TILES, D])

        def cols(b, tap=1):
            return xT[:, b * BLK + tap:(b + 1) * BLK + tap]

        def wide(row):
            return row.partition_broadcast(P)

        loads = [(conv[:, :, :], a["L1_attn_conv_w"]), (conv_b[:, :], a["L1_attn_conv_b"]),
                 (win[:, :], a["L1_attn_in_proj_w"]), (qk_b[:, :], a["L1_attn_qk_b"]),
                 (v_b[:, :], wide(a["L1_attn_v_b"])), (out_b[:, :], wide(a["L1_attn_out_proj_b"])),
                 (b2[:, :], wide(a["L1_attn_b2"])), (wo[:, :], a["L1_attn_out_proj_w"]),
                 (w1[:, :], a["L1_attn_w1"]), (b1[:, :], a["L1_attn_b1"]), (w2[:, :, :], a["L1_attn_w2"])]
        loads += [(ln[:, j, :], wide(a["L1_attn_" + n])) for j, n in enumerate(("ln1_g", "ln1_b", "ln2_g", "ln2_b"))]
        normalize(c, c.x[:, :, :], xn[:, :, :], TILES, D, loads=loads)
        with nc.Block() as block:
            @block.vector
            def _(dve):
                nc.vector.memset(xT[:, 0:1], 0.0)
                nc.vector.memset(xT[:, T + 1:T + 2], 0.0)
        transpose_tiles(c, [([xn[:, 4 * b + q, :] for q in range(4)], cols(b)) for b in range(BLKS)])
        with ExitStack() as inner:
            vinT = c.sb(inner, "a1_vinT", [P, T])
            qT = c.sb(inner, "a1_qT", [P, T])
            kT = c.sb(inner, "a1_kT", [P, T])
            kTm = c.sb(inner, "a1_kTm", [P, HEADS, T])
            dense_features(c, lambda k, b: cols(b, k), lambda k, m: conv[:, k, :], 3, 1,
                           lambda m, b: vinT[:, b * BLK:(b + 1) * BLK], ACT.Identity, bias=lambda m: conv_b[:, 0:1])
            dense_features(c, lambda k, b: cols(b), lambda k, m: win[:, m * D:(m + 1) * D], 1, 2,
                           lambda m, b: (qT, kT)[m][:, b * BLK:(b + 1) * BLK], ACT.Identity,
                           bias=lambda m: qk_b[:, m:m + 1])
            dense_tokens(c, lambda k, i: vinT[:, i * P:(i + 1) * P], lambda k, n: win[:, 2 * D:3 * D], 1, [D],
                         lambda i, n: v[:, i, :], plus=lambda i, n: v_b[:, :])
            mask_keys(c, kT, kTm)
            oT = kT
            windowed_attention(c, qT, kTm, v, oT, 2, float(HD) ** -0.5)
            dense_tokens(c, lambda k, i: oT[:, i * P:(i + 1) * P], lambda k, n: wo[:, :], 1, [D],
                         lambda i, n: h[:, i, :], plus=lambda i, n: xn[:, i, :])
        with nc.Block() as block:
            @block.vector
            def _(dve):
                nc.vector.tensor_tensor(h[:, :, :], h[:, :, :], out_b[:, :].unsqueeze(1).to_broadcast([P, TILES, D]), ALU.add)
        normalize(c, h[:, :, :], xn[:, :, :], TILES, D, gamma=ln[:, 0, :], beta=ln[:, 1, :])
        transpose_tiles(c, [([xn[:, 4 * b + q, :] for q in range(4)], cols(b)) for b in range(BLKS)])
        with ExitStack() as inner:
            hid = c.sb(inner, "a1_hidden", [P, 2, T])
            dense_features(c, lambda k, b: cols(b), lambda k, m: w1[:, m * D:(m + 1) * D], 1, 2,
                           lambda m, b: hid[:, m, b * BLK:(b + 1) * BLK], ACT.Relu, bias=lambda m: b1[:, m:m + 1])
            dense_tokens(c, lambda k, i: hid[:, k, i * P:(i + 1) * P], lambda k, n: w2[:, k, :], 2, [D],
                         lambda i, n: h[:, i, :], plus=lambda i, n: b2[:, :])
        normalize(c, h[:, :, :], h[:, :, :], TILES, D, gamma=ln[:, 2, :], beta=ln[:, 3, :], plus=xn[:, :, :],
                  residual=c.x[:, :, :])


EXPERTS = 4
W = 256
KT = W // P
GROUPS = 4
GH = 4
PARTS = 6
STACK = PARTS * HD
GATES = 4 * W
UNITS = W // 4
CH = 8
SUPER = 64


def wide(row):
    return row.partition_broadcast(P)


def expert_front(c, a, e, xT, zx):
    nc = c.nc
    with ExitStack() as mem:
        oT = c.sb(mem, "f_oT", [P, GROUPS, T])
        with ExitStack() as m1:
            qkv = c.sb(m1, "f_qkv", [P, TILES, 3 * W])
            with ExitStack() as m2:
                w1, b1 = c.sb(m2, "f_w1", [P, W]), c.sb(m2, "f_b1", [P, KT])
                w2, rows = c.sb(m2, "f_w2", [P, KT, W]), c.sb(m2, "f_rows", [P, 3, W])
                hid, h = c.sb(m2, "f_hid", [P, KT, T]), c.sb(m2, "f_h", [P, TILES, W])
                loads = [(w1[:, :], a["enc_w1"][e]), (b1[:, :], a["enc_b1"][e]), (w2[:, :, :], a["enc_w2"][e])]
                loads += [(rows[:, j, :], wide(a[n][e])) for j, n in enumerate(("enc_b2", "enc_g", "enc_beta"))]
                dense_features(c, lambda k, b: xT[:, b * BLK:(b + 1) * BLK], lambda k, m: w1[:, m * P:(m + 1) * P], 1, KT,
                               lambda m, b: hid[:, m, b * BLK:(b + 1) * BLK], ACT.Relu, bias=lambda m: b1[:, m:m + 1],
                               loads=loads)
                dense_tokens(c, lambda k, i: hid[:, k, i * P:(i + 1) * P], lambda k, n: w2[:, k, :], KT, [W],
                             lambda i, n: h[:, i, :], plus=lambda i, n: rows[:, 0, :])
                normalize(c, h[:, :, :], h[:, :, :], TILES, W, gamma=rows[:, 1, :], beta=rows[:, 2, :])
                transpose_tiles(c, [([h[:, 4 * b + q, k * P:(k + 1) * P] for q in range(4)], hid[:, k, b * BLK:(b + 1) * BLK])
                                    for k in range(KT) for b in range(BLKS)])
                with ExitStack() as m3:
                    win, bin_ = c.sb(m3, "f_in_w", [P, KT, 3 * W]), c.sb(m3, "f_in_b", [P, 3 * W])
                    at = [(0, BLK), (BLK, 3 * W)]
                    dense_tokens(c, lambda k, i: hid[:, k, i * P:(i + 1) * P], lambda k, n: win[:, k, at[n][0]:at[n][1]],
                                 KT, [y - x for x, y in at], lambda i, n: qkv[:, i, at[n][0]:at[n][1]],
                                 plus=lambda i, n: bin_[:, at[n][0]:at[n][1]],
                                 loads=[(win[:, :, :], a["attn_in_w"][e]), (bin_[:, :], wide(a["attn_in_b"][e]))])
            full_attention(c, qkv, oT)
        hT = c.sb(mem, "f_hT", [P, KT, T])
        wo, bo = c.sb(mem, "f_wo", [P, GROUPS, W]), c.sb(mem, "f_bo", [P, KT])
        with nc.Block() as block:
            @block.vector
            def _(dve):
                nc.vector.memset(wo[:, :, :], 0.0)
        loads = [(wo[32 * h:32 * h + HD, :, :], a["attn_out_w"][e][:, h, :, :].rearrange("g d n -> d g n")) for h in range(GH)]
        dense_features(c, lambda k, b: oT[:, k, b * BLK:(b + 1) * BLK], lambda k, m: wo[:, k, m * P:(m + 1) * P], GROUPS, KT,
                       lambda m, b: hT[:, m, b * BLK:(b + 1) * BLK], ACT.Identity, bias=lambda m: bo[:, m:m + 1],
                       loads=loads + [(bo[:, :], a["attn_out_b"][e])])
        for d, way in enumerate("fb"):
            input_projection(c, hT, a["lstm_wi_" + way][e], a["lstm_b_" + way][e], zx[d], e)


def input_projection(c, hT, wi_dram, b_dram, zx, e):
    nc = c.nc
    with ExitStack() as mem:
        wi, bias = c.sb(mem, "p_wi", [P, KT, GATES]), c.sb(mem, "p_b", [P, GATES])
        stage = c.sb(mem, "p_stage", [P, 4, GATES])
        with nc.Block() as block:
            @block.sync
            def _(sp):
                sp.dma_start(wi[:, :, :], wi_dram).then_inc(c.loaded, 16)
                sp.dma_start(bias[:, :], wide(b_dram)).then_inc(c.loaded, 16)
                for i in range(TILES):
                    sp.wait_ge(c.evacuated, 2 * (i + 1))
                    sp.dma_start(zx[i * P:(i + 1) * P, :, bass.ds(e, 1), :].rearrange("t j c n -> t j (c n)"),
                                 stage[:, i % 4, :].rearrange("p (j n) -> p j n", j=4)).then_inc(c.stored, 16)
                    if i % 4 == 3:
                        sp.wait_ge(c.stored, 16 * (i + 1))
                        sp.sem_inc(c.pooled, 1)

            @block.tensor
            def _(pe):
                pe.wait_ge(c.loaded, 32)
                for j in range(2 * TILES):
                    i, n = divmod(j, 2)
                    if j >= 8:
                        pe.wait_ge(c.evacuated, j - 7)
                    for k in range(KT):
                        last = nc.tensor.matmul(c.psum[:, j % 8, :], hT[:, k, i * P:(i + 1) * P],
                                                wi[:, k, n * BLK:(n + 1) * BLK], start=(k == 0), stop=(k == KT - 1))
                    last.then_inc(c.multiplied, 1)

            @block.vector
            def _(dve):
                dve.wait_ge(c.loaded, 32)
                for j in range(2 * TILES):
                    i, n = divmod(j, 2)
                    dve.wait_ge(c.multiplied, j + 1)
                    if j % 8 == 0 and j:
                        dve.wait_ge(c.pooled, j // 8)
                    nc.vector.tensor_tensor(stage[:, i % 4, n * BLK:(n + 1) * BLK], c.psum[:, j % 8, :],
                                            bias[:, n * BLK:(n + 1) * BLK], ALU.add).then_inc(c.evacuated, 1)
        c.clear()


def full_attention(c, qkv, oT):
    nc = c.nc
    with ExitStack() as mem:
        qs, ks = c.sb(mem, "g_qs", [P, GH, T], BF16), c.sb(mem, "g_ks", [P, GH, T], BF16)
        v4 = c.sb(mem, "g_v4", [P, TILES, GH, 32])
        sel = c.sb(mem, "g_sel", [P, GH, 32])
        with nc.Block() as block:
            @block.gpsimd
            def _(pool):
                step = Chain(pool, c.pooled)
                step(nc.gpsimd.memset(sel[:, :, :], 0.0))
                step(nc.gpsimd.affine_select(out=sel[:, :, :], in_=sel[:, :, :], compare_op=ALU.not_equal, fill=1.0,
                                             base=-HD, pattern=[[-32, GH], [0, 32]], channel_multiplier=1))
                step(nc.gpsimd.memset(v4[:, :, :, HD:32], 0.0))
                step(nc.gpsimd.memset(v4[:, :, :, HD:HD + 1], 1.0))

            @block.vector
            def _(dve):
                nc.vector.memset(ks[STACK:STACK + 3, :, :], 1.0)
        c.clear()
        with nc.Fori(0, GROUPS) as g:
            split_heads(c, qkv, qs, ks, v4, g)
            first_maxima(c, qs, ks)
            with nc.Fori(0, BLKS - 1) as b:
                attend(c, qs, ks, v4, sel, oT, g, b)
            attend(c, qs, ks, v4, sel, oT, g, BLKS - 1, last_block=True)


def banks_bf16(c):
    return c.psum[:, :, :].rearrange("p b f -> p (b f)").bitcast(BF16).rearrange("p (b f) -> p b f", b=8)


def split_heads(c, qkv, qs, ks, v4, g):
    nc = c.nc
    with ExitStack() as mem:
        stacks = [c.sb(mem, "h_q", [P, TILES, GH, STACK], BF16), c.sb(mem, "h_k", [P, TILES, GH, STACK], BF16)]
        rest = [c.sb(mem, "h_qrest", [P, TILES, GH * HD]), c.sb(mem, "h_krest", [P, TILES, GH * HD])]
        places = [((0, 3, 5), (1, 4), (2,)), ((0, 1, 2), (3, 4), (5,))]

        def heads(ap):
            return ap.rearrange("p i (h d) -> p i h d", d=HD)

        def part(s, n):
            return stacks[s][:, :, :, n * HD:(n + 1) * HD]

        bf = banks_bf16(c)
        jobs = [(h, half, s) for h in range(GH) for half in range(2) for s in range(2)]
        with nc.Block() as block:
            @block.gpsimd
            def _(pool):
                for level in range(2):
                    for s in range(2):
                        pool.wait_ge(c.activated, 2 * level + s + 1)
                        for n in places[s][level][1:]:
                            nc.gpsimd.tensor_copy(part(s, n), part(s, places[s][level][0])).then_inc(c.pooled, 1)
                nc.gpsimd.tensor_copy(v4[:, :, :, 0:HD], heads(qkv[:, :, bass.ds(g * (GH * HD) + 2 * W, GH * HD)]))

            @block.scalar
            def _(act):
                for level in range(3):
                    for s in range(2):
                        if level:
                            act.wait_ge(c.vectored, 2 * (level - 1) + s + 1)
                        src = qkv[:, :, bass.ds(g * (GH * HD) + s * W, GH * HD)] if level == 0 else rest[s][:, :, :]
                        nc.scalar.activation(part(s, places[s][level][0]), heads(src), ACT.Copy).then_inc(c.activated, 1)
                for j, (h, half, s) in enumerate(jobs):
                    if s == 0:
                        continue
                    act.wait_ge(c.transposed, j + 1)
                    nc.scalar.activation(ks[0:STACK, h, half * 1024:(half + 1) * 1024], bf[0:STACK, j % 8, :],
                                         ACT.Copy).then_inc(c.copied, 1)

            @block.vector
            def _(dve):
                for level in range(2):
                    for s in range(2):
                        dve.wait_ge(c.activated, 2 * level + s + 1)
                        src = heads(qkv[:, :, bass.ds(g * (GH * HD) + s * W, GH * HD)]) if level == 0 else heads(rest[s][:, :, :])
                        if level:
                            dve.wait_ge(c.vectored, s + 1)
                        nc.vector.tensor_tensor(heads(rest[s][:, :, :]), src, part(s, places[s][level][0]),
                                                ALU.subtract).then_inc(c.vectored, 1)
                for j, (h, half, s) in enumerate(jobs):
                    if s == 1:
                        continue
                    dve.wait_ge(c.transposed, j + 1)
                    nc.vector.tensor_copy(qs[0:STACK, h, half * 1024:(half + 1) * 1024], bf[0:STACK, j % 8, :]).then_inc(c.evacuated, 1)

            @block.tensor
            def _(pe):
                pe.wait_ge(c.activated, 6)
                pe.wait_ge(c.pooled, 6)
                for j, (h, half, s) in enumerate(jobs):
                    if j >= 8:
                        pe.wait_ge(c.copied if s else c.evacuated, (j - 8) // 2 + 1)
                    for q in range(8):
                        last = nc.tensor.transpose(bf[0:STACK, j % 8, q * P:(q + 1) * P], stacks[s][:, half * 8 + q, h, :],
                                                   c.identb[:, :])
                    last.then_inc(c.transposed, 1)
        c.clear()


MAX_JOBS = GH * 4 * BLKS
MAX_BANK = 6


class Maxima:

    def __init__(self, c, mem, qs, ks, b):
        self.c, self.qs, self.ks, self.b = c, qs, ks, b
        self.best = c.sb(mem, "r_best", [P, MAX_JOBS])
        self.neg = c.sb(mem, "r_neg", [P, GH * 4])
        self.parts = c.sb(mem, "r_parts", [P, GH * 4, 4], BF16)

    def multiply(self, pe, m):
        c = self.c
        h, i, kb = m // 16, m // 4 % 4, m % 4
        if m >= 2:
            pe.wait_ge(c.reduced, m - 1)
        c.nc.tensor.matmul(c.psum[:, MAX_BANK + m % 2, :], self.qs[0:STACK, h, bass.ds(self.b * BLK + i * P, P)],
                           self.ks[0:STACK, h, kb * BLK:(kb + 1) * BLK], start=True, stop=True).then_inc(c.scored, 1)

    def reduce(self, dve, m):
        c = self.c
        dve.wait_ge(c.scored, m + 1)
        c.nc.vector.tensor_reduce(self.best[:, m:m + 1], c.psum[:, MAX_BANK + m % 2, :], AX, ALU.max).then_inc(c.reduced, 1)

    def multiply_row(self, pe, r):
        c = self.c
        if r >= 2:
            pe.wait_ge(c.reduced, r - 1)
        for kb in range(BLKS):
            last = c.nc.tensor.matmul(c.psum[:, 4 * (r % 2) + kb, :], self.qs[0:STACK, r // 4, bass.ds(self.b * BLK + r % 4 * P, P)],
                                      self.ks[0:STACK, r // 4, kb * BLK:(kb + 1) * BLK], start=True, stop=True)
        last.then_inc(c.scored, 1)

    def reduce_row(self, dve, r):
        c = self.c
        dve.wait_ge(c.scored, r + 1)
        c.nc.vector.tensor_reduce(self.best[:, r:r + 1], c.psum[:, 4 * (r % 2):4 * (r % 2) + 4, :].rearrange("p b f -> p (b f)"),
                                  AX, ALU.max).then_inc(c.reduced, 1)

    def split(self, dve, jobs=MAX_JOBS):
        c, nc = self.c, self.c.nc
        dve.wait_ge(c.reduced, jobs)
        step = Chain(dve, c.stepped)
        if jobs == MAX_JOBS:
            step(nc.vector.tensor_reduce(self.neg[:, :], self.best[:, :].rearrange("p (m k) -> p m k", k=BLKS), AX, ALU.max,
                                         negate=True))
        else:
            step(nc.vector.tensor_scalar(self.neg[:, :], self.best[:, 0:jobs], -1.0, None, ALU.mult))
        for n in range(3):
            step(nc.vector.tensor_copy(self.parts[:, :, n], self.neg[:, :]))
            if n < 2:
                step(nc.vector.tensor_tensor(self.neg[:, :], self.neg[:, :], self.parts[:, :, n], ALU.subtract))

    SPLIT_STEPS = 6

    def turn(self, pe):
        c = self.c
        bf = banks_bf16(c)
        pe.wait_ge(c.stepped, self.SPLIT_STEPS)
        for m in range(GH * 4):
            last = c.nc.tensor.transpose(bf[STACK:STACK + 3, MAX_BANK + m // 8, m % 8 * P:(m % 8 + 1) * P],
                                         self.parts[:, m, 0:3], c.identb[:, :])
        last.then_inc(c.turned, 1)

    def place(self, act):
        c = self.c
        bf = banks_bf16(c)
        act.wait_ge(c.turned, 1)
        for two in range(2):
            c.nc.scalar.activation(self.qs[STACK:STACK + 3, 2 * two:2 * two + 2, bass.ds(self.b * BLK, BLK)],
                                   bf[STACK:STACK + 3, MAX_BANK + two, :].rearrange("p (h f) -> p h f", f=BLK), ACT.Copy)


def first_maxima(c, qs, ks):
    with ExitStack() as mem:
        maxima = Maxima(c, mem, qs, ks, 0)
        with c.nc.Block() as block:
            @block.tensor
            def _(pe):
                for r in range(GH * 4):
                    maxima.multiply_row(pe, r)
                maxima.turn(pe)

            @block.vector
            def _(dve):
                for r in range(GH * 4):
                    maxima.reduce_row(dve, r)
                maxima.split(dve, GH * 4)

            @block.scalar
            def _(act):
                maxima.place(act)
        c.clear()


def attend(c, qs, ks, v4, sel, oT, g, b, last_block=False):
    nc = c.nc
    jobs, rows = 2 * TILES, STACK + 3
    per = MAX_JOBS // jobs
    with ExitStack() as mem:
        probs = c.sb(mem, "t_probs", [P, 3, 2 * BLK])
        got, inv = c.sb(mem, "t_got", [P, BLK]), c.sb(mem, "t_inv", [P, BLK])
        maxima = None if last_block else Maxima(c, mem, qs, ks, b + 1)
        ring = 3 if last_block else 2
        out, sums = (6, 7) if last_block else (4, 5)
        with nc.Block() as block:
            @block.tensor
            def _(pe):
                def scores(n):
                    for two in range(2):
                        h = 2 * (n % 2) + two
                        last = nc.tensor.matmul(c.psum[:, 2 * (n % ring) + two, :], ks[0:rows, h, n // 2 * P:(n // 2 + 1) * P],
                                                qs[0:rows, h, bass.ds(b * BLK, BLK)], start=True, stop=True)
                    last.then_inc(c.multiplied, 1)

                for n in range(ring):
                    scores(n)
                for n in range(jobs):
                    pe.wait_ge(c.activated, n + 1)
                    if n + ring < jobs:
                        scores(n + ring)
                    for two in range(2):
                        h = 2 * (n % 2) + two
                        last = nc.tensor.matmul(c.psum[32 * h:32 * h + 32, out, :], v4[:, n // 2, h, :],
                                                probs[:, n % 3, two * BLK:(two + 1) * BLK],
                                                start=(n < 2), stop=(n >= jobs - 2))
                    last.then_inc(c.copied, 1)
                    if maxima:
                        for m in range(per * n, per * (n + 1)):
                            maxima.multiply(pe, m)
                if maxima:
                    maxima.turn(pe)
                pe.wait_ge(c.vectored, 1)
                nc.tensor.matmul(c.psum[:, sums, :], sel[:, :, :].rearrange("p h m -> p (h m)"), got[:, :],
                                 start=True, stop=True).then_inc(c.transposed, 1)

            @block.scalar
            def _(act):
                for n in range(jobs):
                    act.wait_ge(c.multiplied, n + 1)
                    if n >= 3:
                        act.wait_ge(c.copied, n - 2)
                    pair = c.psum[:, 2 * (n % ring):2 * (n % ring) + 2, :].rearrange("p a f -> p (a f)")
                    nc.scalar.activation(probs[:, n % 3, :], pair, ACT.Exp, scale=float(HD) ** -0.5).then_inc(c.activated, 1)
                if maxima:
                    maxima.place(act)

            @block.vector
            def _(dve):
                if maxima:
                    for m in range(MAX_JOBS):
                        maxima.reduce(dve, m)
                    maxima.split(dve)
                dve.wait_ge(c.copied, jobs)
                nc.vector.tensor_copy(got[:, :], c.psum[:, out, :]).then_inc(c.vectored, 1)
                dve.wait_ge(c.transposed, 1)
                nc.vector.reciprocal(inv[:, :], c.psum[:, sums, :]).then_inc(c.vectored, 1)
                dve.wait_ge(c.vectored, 2)
                nc.vector.tensor_tensor(oT[:, bass.ds(g, 1), bass.ds(b * BLK, BLK)].rearrange("p a f -> p (a f)"),
                                        got[:, :], inv[:, :], ALU.mult)
        c.clear()


def lstms(c, a, zx, hist):
    nc = c.nc
    steps = T
    with ExitStack() as mem:
        wh = c.sb(mem, "l_wh", [P, 2, EXPERTS, KT, GATES])
        sel = c.sb(mem, "l_sel", [P, 2, KT, EXPERTS, EXPERTS])
        state = c.sb(mem, "l_state", [P, 2, KT, EXPERTS, 32])
        xin = c.sb(mem, "l_xin", [P, 2, 2, CH, W])
        z = c.sb(mem, "l_z", [P, 2, W])
        gates = c.sb(mem, "l_gates", [P, 2, W])
        cell = c.sb(mem, "l_cell", [P, 2, UNITS])
        kept = c.sb(mem, "l_kept", [P, 2, UNITS])
        fresh = c.sb(mem, "l_fresh", [P, 2, UNITS])
        squashed = c.sb(mem, "l_squashed", [P, 2, UNITS])
        h = c.sb(mem, "l_h", [P, 2, UNITS])
        past = c.sb(mem, "l_past", [P, 2, 2, KT, EXPERTS, SUPER])
        sems = {}
        for what in ("summed", "z_made", "gated", "cell_made", "squashed", "h_made", "turned", "state_made", "kept"):
            sems[what] = [nc.alloc_semaphore(f"{what}_{d}") for d in range(2)]
        dve_step = [nc.alloc_semaphore(f"products_{d}") for d in range(2)]
        xin_in = [[nc.alloc_semaphore(f"xin_{d}_{q}") for q in range(2)] for d in range(2)]
        past_out = [nc.alloc_semaphore(f"past_{q}") for q in range(2)]
        wh_in = nc.alloc_semaphore("wh_in")
        ready = nc.alloc_semaphore("constants_made")
        chunks = nc.alloc_semaphore("chunks_begun")

        with nc.Block() as block:
            @block.sync
            def _(sp):
                for d, way in enumerate("fb"):
                    for e in range(EXPERTS):
                        sp.dma_start(wh[:, d, e, :, :], a["lstm_wh_" + way][e]).then_inc(wh_in, 16)
                sp.wait_ge(wh_in, 16 * 2 * EXPERTS)

            @block.vector
            def _(dve):
                nc.vector.memset(state[:, :, :, :, :], 0.0)
                nc.vector.memset(cell[:, :, :], 0.0)
                nc.vector.memset(h[:, :, :], 0.0)
                nc.vector.memset(xin[:, :, :, :, :], 0.0)

            @block.gpsimd
            def _(pool):
                step = Chain(pool, ready)
                step(nc.gpsimd.memset(sel[:, :, :, :, :], 0.0))
                for half in range(2):
                    step(nc.gpsimd.affine_select(
                        out=sel[:, half, :, :, :], in_=sel[:, half, :, :, :], compare_op=ALU.not_equal, fill=1.0,
                        base=-32 * half, pattern=[[-64, KT], [-1, EXPERTS], [0, EXPERTS]], channel_multiplier=1))
                    step(nc.gpsimd.affine_select(
                        out=sel[:, half, :, :, :], in_=sel[:, half, :, :, :], compare_op=ALU.is_equal, fill=0.0,
                        base=0, pattern=[[0, KT], [1, EXPERTS], [-1, EXPERTS]], channel_multiplier=0))

        with nc.Block() as block:
            @block.vector
            def _(dve):
                for d in range(2):
                    dve.sem_inc(sems["summed"][d], 2 * CH)
                    dve.sem_inc(sems["kept"][d], 1)

        with nc.Block() as block:
            @block.sync
            def _(sp):
                with sp.Fori(0, steps // (2 * CH)) as pair:
                    for q in range(2):
                        for d in range(2):
                            at = pair * (2 * CH) + q * CH
                            sp.wait_ge(sems["summed"][d], at + CH)
                            first = at if d == 0 else at * (-1) + (steps - CH)
                            for j in range(4):
                                sp.dma_start(xin[32 * j:32 * j + EXPERTS, d, q, :, :],
                                             zx[d][bass.ds(first, CH), j, :, :].rearrange("t c n -> c t n")
                                             ).then_inc(xin_in[d][q], 16)

            @block.tensor
            def _(pe):
                half_way = 5 * KT * EXPERTS // 8

                def products(d, s, part):
                    if part == 0 and s is not None:
                        pe.wait_ge(sems["state_made"][d], s)
                        pe.wait_ge(sems["summed"][d], s + 2 * CH)
                    for n in range(half_way) if part == 0 else range(half_way, EXPERTS * KT):
                        e, k = divmod(n, KT)
                        for j in range(4):
                            last = nc.tensor.matmul(c.psum[32 * j:32 * j + 32, d, 0:W], state[:, d, k, e, :],
                                                    wh[:, d, e, k, j * W:(j + 1) * W],
                                                    start=(n == 0), stop=(n == EXPERTS * KT - 1))
                    if part == 1:
                        last.then_inc(sems["z_made"][d], 1)

                def turn(d, s):
                    pe.wait_ge(sems["h_made"][d], s + 1)
                    for q in range(4):
                        half, u = divmod(q, 2)
                        last = nc.tensor.matmul(c.psum[32 * q:32 * q + 32, 2 + d, 0:KT * EXPERTS * EXPERTS],
                                                h[:, d, u * 32:(u + 1) * 32],
                                                sel[:, half, :, :, :].rearrange("p k e f -> p (k e f)"), start=True, stop=True)
                    last.then_inc(sems["turned"][d], 1)

                products(0, None, 0)
                products(0, None, 1)
                products(1, None, 0)
                turn(0, 0)
                products(1, None, 1)
                with pe.Fori(1, steps) as s:
                    products(0, s, 0)
                    turn(1, s - 1)
                    products(0, s, 1)
                    products(1, s, 0)
                    turn(0, s)
                    products(1, s, 1)
                turn(1, steps - 1)

            @block.scalar
            def _(act):
                nc.scalar.activation(squashed[:, :, :], h[:, :, :], ACT.Sigmoid)
                with act.Fori(0, steps) as s:
                    for d in range(2):
                        act.wait_ge(sems["summed"][d], s + (2 * CH + 1))
                        nc.scalar.activation(gates[:, d, 0:3 * UNITS], z[:, d, 0:3 * UNITS], ACT.Sigmoid).then_inc(sems["gated"][d], 1)
                        nc.scalar.activation(gates[:, d, 3 * UNITS:W], z[:, d, 3 * UNITS:W], ACT.Tanh).then_inc(sems["gated"][d], 1)
                        act.wait_ge(sems["cell_made"][d], s + 1)
                        nc.scalar.activation(squashed[:, d, :], cell[:, d, :], ACT.Tanh).then_inc(sems["squashed"][d], 1)

            @block.vector
            def _(dve):
                def gate(d, n):
                    return gates[:, d, n * UNITS:(n + 1) * UNITS]

                with dve.Fori(0, steps // (2 * CH)) as pair:
                    for q in range(2):
                        for d in range(2):
                            dve.wait_ge(xin_in[d][q], pair * 64 + 64)
                        dve.sem_inc(chunks, 1)
                        with dve.Fori(0, CH) as r:
                            s = pair * (2 * CH) + (r + q * CH)
                            for d in range(2):
                                at = r if d == 0 else r * (-1) + (CH - 1)
                                dve.wait_ge(sems["z_made"][d], s + 1)
                                nc.vector.tensor_tensor(z[:, d, :], c.psum[:, d, 0:W],
                                                        xin[:, d, q, bass.ds(at, 1), :].rearrange("p a n -> p (a n)"),
                                                        ALU.add).then_inc(sems["summed"][d], 1)
                                dve.wait_ge(sems["gated"][d], s * 2 + 1)
                                nc.vector.tensor_tensor(kept[:, d, :], gate(d, 1), cell[:, d, :], ALU.mult).then_inc(dve_step[d], 1)
                                dve.wait_ge(sems["gated"][d], s * 2 + 2)
                                nc.vector.tensor_tensor(fresh[:, d, :], gate(d, 0), gate(d, 3), ALU.mult).then_inc(dve_step[d], 1)
                                dve.wait_ge(dve_step[d], s * 2 + 2)
                                nc.vector.tensor_tensor(cell[:, d, :], kept[:, d, :], fresh[:, d, :], ALU.add).then_inc(sems["cell_made"][d], 1)
                                dve.wait_ge(sems["squashed"][d], s + 1)
                                nc.vector.tensor_tensor(h[:, d, :], gate(d, 2), squashed[:, d, :], ALU.mult).then_inc(sems["h_made"][d], 1)
                                dve.wait_ge(sems["turned"][d], s + 1)
                                dve.wait_ge(sems["kept"][d], s + 1)
                                nc.vector.tensor_copy(state[:, d, :, :, 0:EXPERTS].rearrange("p k e f -> p (k e) f"),
                                                      c.psum[:, 2 + d, 0:KT * EXPERTS * EXPERTS].rearrange("p (a f) -> p a f", f=EXPERTS)
                                                      ).then_inc(sems["state_made"][d], 1)

            @block.gpsimd
            def _(pool):
                def chunk(big, q, first):
                    if not first:
                        pool.wait_ge(past_out[q], big * 64)
                        pool.sem_inc(chunks, 1)
                    with pool.Fori(0, SUPER) as r:
                        s = big * (2 * SUPER) + (r + q * SUPER)
                        for d in range(2):
                            at = r if d == 0 else r * (-1) + (SUPER - 1)
                            pool.wait_ge(sems["state_made"][d], s + 1)
                            diagonal = state[:, d, :, :, :].rearrange("p k e f -> p k (e f)")[:, :, 0:(EXPERTS - 1) * 33 + 1:33]
                            nc.gpsimd.tensor_copy(past[:, d, q, :, :, bass.ds(at, 1)].rearrange("p k e a -> p k (e a)"),
                                                  diagonal).then_inc(sems["kept"][d], 1)
                    for d in range(2):
                        at = big * (2 * SUPER) + q * SUPER
                        t0 = at if d == 0 else at * (-1) + (steps - SUPER)
                        pool.wait_ge(sems["kept"][d], at + (SUPER + 1))
                        for k in range(KT):
                            nc.gpsimd.dma_start(hist[:, d, k, :, bass.ds(t0, SUPER)].rearrange("e p t -> p e t"),
                                                past[:, d, q, k, :, :]).then_inc(past_out[q], 16)

                rounds = steps // (2 * SUPER)
                chunk(0, 0, True)
                chunk(0, 1, True)
                with pool.Fori(1, rounds) as big:
                    chunk(big, 0, False)
                    chunk(big, 1, False)
                for q in range(2):
                    pool.wait_ge(past_out[q], rounds * 64)


def expert_back(c, a, e, hist, router):
    nc = c.nc
    with ExitStack() as mem:
        past = c.sb(mem, "b_past", [P, 2, KT, T])
        hid, gate, other = (c.sb(mem, n, [P, KT, T]) for n in ("b_hid", "b_gate", "b_other"))
        w1, w2 = c.sb(mem, "b_w1", [P, 2 * KT, W]), c.sb(mem, "b_w2", [P, KT, W])
        b1, b2 = c.sb(mem, "b_b1", [P, KT]), c.sb(mem, "b_b2", [P, KT])
        wd, rows = c.sb(mem, "b_wd", [P, KT, D]), c.sb(mem, "b_rows", [P, 3, D])

        def layer(src, w, kt, out, func, b, loads):
            dense_features(c, lambda k, n: src(k)[:, n * BLK:(n + 1) * BLK], lambda k, m: w[:, k, m * P:(m + 1) * P], kt, KT,
                           lambda m, n: out[:, m, n * BLK:(n + 1) * BLK], func, bias=lambda m: b[:, m:m + 1], loads=loads)

        first = [(past[:, d, k, :], hist[e, d, k, :, :]) for d in range(2) for k in range(KT)]
        for kind, func, out in (("sig", ACT.Sigmoid, gate), ("tan", ACT.Tanh, other)):
            layer(lambda k: past[:, k // KT, k % KT, :], w1, 2 * KT, hid, ACT.Relu, b1,
                  first + [(w1[:, :, :], a[kind + "_w1"][e]), (b1[:, :], a[kind + "_b1"][e]),
                           (w2[:, :, :], a[kind + "_w2"][e]), (b2[:, :], a[kind + "_b2"][e])])
            layer(lambda k: hid[:, k, :], w2, KT, out, func, b2, [])
            first = []
        with nc.Block() as block:
            @block.vector
            def _(dve):
                nc.vector.tensor_tensor(gate[:, :, :], gate[:, :, :], other[:, :, :], ALU.mult)
        layer(lambda k: gate[:, k, :], w2, KT, hid, ACT.Relu, b1,
              [(w2[:, :, :], a["dec_w1"][e]), (b1[:, :], a["dec_b1"][e]), (wd[:, :, :], a["dec_w2"][e])]
              + [(rows[:, j, :], wide(a[n][e])) for j, n in enumerate(("dec_b2", "dec_g", "dec_beta"))])
        y = other[:, 0, :].rearrange("p (i d) -> p i d", d=D)
        dense_tokens(c, lambda k, i: hid[:, k, i * P:(i + 1) * P], lambda k, n: wd[:, k, :], KT, [D],
                     lambda i, n: y[:, i, :], plus=lambda i, n: rows[:, 0, :])
        normalize(c, y, y, TILES, D, gamma=rows[:, 1, :], beta=rows[:, 2, :])
        with nc.Block() as block:
            @block.vector
            def _(dve):
                step = Chain(dve, c.stepped)
                step(nc.vector.tensor_tensor(y, y, router[:, :, bass.ds(e, 1)].to_broadcast([P, TILES, D]), ALU.mult))
                step(nc.vector.tensor_tensor(c.x[:, :, :], c.x[:, :, :], y, ALU.add))
        c.clear()


def layer1_experts(c, a, zx, hist):
    nc = c.nc
    with ExitStack() as mem:
        router = c.sb(mem, "e_router", [P, TILES, EXPERTS])
        with ExitStack() as m1:
            xT = c.sb(m1, "e_xT", [P, T])
            rw, rb = c.sb(m1, "e_router_w", [P, EXPERTS]), c.sb(m1, "e_router_b", [P, EXPERTS])
            total = c.sb(m1, "e_total", [P, TILES])
            with ExitStack() as m2:
                xn = c.sb(m2, "e_xn", [P, TILES, D])
                normalize(c, c.x[:, :, :], xn[:, :, :], TILES, D)
                transpose_tiles(c, [([xn[:, 4 * b + q, :] for q in range(4)], xT[:, b * BLK:(b + 1) * BLK]) for b in range(BLKS)])
            dense_tokens(c, lambda k, i: xT[:, i * P:(i + 1) * P], lambda k, n: rw[:, :], 1, [EXPERTS],
                         lambda i, n: router[:, i, :], plus=lambda i, n: rb[:, :],
                         loads=[(rw[:, :], a["router_w"]), (rb[:, :], wide(a["router_b"]))])
            with nc.Block() as block:
                def each(ap):
                    return ap.unsqueeze(2).to_broadcast([P, TILES, EXPERTS])

                @block.vector
                def _(dve):
                    step = Chain(dve, c.stepped)
                    step(nc.vector.tensor_reduce(total[:, :], router[:, :, :], AX, ALU.max))
                    step(nc.vector.tensor_tensor(router[:, :, :], router[:, :, :], each(total[:, :]), ALU.subtract))
                    dve.wait_ge(c.activated, 1)
                    step(nc.vector.tensor_reduce(total[:, :], router[:, :, :], AX, ALU.add))
                    step(nc.vector.reciprocal(total[:, :], total[:, :]))
                    step(nc.vector.tensor_tensor(router[:, :, :], router[:, :, :], each(total[:, :]), ALU.mult))

                @block.scalar
                def _(act):
                    act.wait_ge(c.stepped, 2)
                    nc.scalar.activation(router[:, :, :], router[:, :, :], ACT.Exp).then_inc(c.activated, 1)
            c.clear()
            with nc.Fori(0, EXPERTS) as e:
                expert_front(c, a, e, xT, zx)
        lstms(c, a, zx, hist)
        with nc.Fori(0, EXPERTS) as e:
            expert_back(c, a, e, hist, router)


def program(nc, a):
    with ExitStack() as ctx:
        c = Core(nc, ctx)
        zx = [nc.dram_tensor(f"projections_{d}", (T, 4, EXPERTS, W), F32).ap() for d in range(2)]
        hist = nc.dram_tensor("hidden_states", (EXPERTS, 2, KT, P, T), F32).ap()
        constants(c)
        gather(c, a["ids"], a["L0_tok_w"])
        layer0_attention(c, a["L0_attn_w_qkv"], a["L0_attn_w_proj"])
        moe(c, *(a["L0_ffn_" + n] for n in ("gate_w", "w1", "w3", "w2", "sw1", "sw3", "sw2")))
        layer1_attention(c, a)
        layer1_experts(c, {n[len("L1_ffn_"):]: v for n, v in a.items() if n.startswith("L1_ffn_")}, zx, hist)
        with nc.Block() as block:
            @block.sync
            def _(sp):
                sp.dma_start(a["out"].rearrange("a (i p) d -> p (a i) d", p=P), c.x[:, :, :]).then_inc(c.stored, 16)
                sp.wait_ge(c.stored, 16)


def lay_out(inputs):
    o = {}
    v = {n: np.asarray(x) for n, x in inputs.items()}
    o["ids"] = v["x"].reshape(TILES, P).T
    o["L0_tok_w"] = v["L0_tok_w"]
    o["L0_attn_w_qkv"] = v["L0_attn_w_qkv"].reshape(D, HEADS, 3, HD).transpose(0, 2, 1, 3).reshape(D, 3 * D)
    o["L0_attn_w_proj"] = v["L0_attn_w_proj"]
    o["L0_ffn_gate_w"] = v["L0_ffn_gate_w"].T
    for n in ("w1", "w3", "w2", "sw1", "sw3", "sw2"):
        o["L0_ffn_" + n] = v["L0_ffn_" + n]
    l = "L1_attn_"
    o[l + "conv_w"] = v[l + "conv_w"].transpose(1, 2, 0)
    o[l + "conv_b"] = v[l + "conv_b"].reshape(P, 1)
    o[l + "in_proj_w"] = v[l + "in_proj_w"].T
    o[l + "qk_b"] = v[l + "in_proj_b"][:2 * D].reshape(2, P).T
    o[l + "v_b"] = v[l + "in_proj_b"][2 * D:]
    o[l + "out_proj_w"] = v[l + "out_proj_w"].T
    o[l + "w1"] = v[l + "w1"].T
    o[l + "b1"] = v[l + "b1"].reshape(2, P).T
    o[l + "w2"] = v[l + "w2"].T.reshape(2, P, D).transpose(1, 0, 2)
    for n in ("out_proj_b", "b2", "ln1_g", "ln1_b", "ln2_g", "ln2_b"):
        o[l + n] = v[l + n]
    l = "L1_ffn_"
    for n in ("router_w", "router_b", "enc_w1", "enc_b2", "enc_g", "enc_beta", "attn_in_b", "dec_b2", "dec_g", "dec_beta"):
        o[l + n] = v[l + n]
    for n in ("enc_w2", "attn_in_w", "sig_w1", "sig_w2", "tan_w1", "tan_w2", "dec_w1", "dec_w2"):
        w = v[l + n]
        o[l + n] = w.reshape(EXPERTS, -1, P, w.shape[2]).transpose(0, 2, 1, 3)
    for n in ("enc_b1", "attn_out_b", "sig_b1", "sig_b2", "tan_b1", "tan_b2", "dec_b1"):
        o[l + n] = v[l + n].reshape(EXPERTS, KT, P).transpose(0, 2, 1)
    o[l + "attn_out_w"] = v[l + "attn_out_w"].reshape(EXPERTS, GROUPS, GH, HD, W)
    order = [0, 1, 3, 2]
    for way in "fb":
        for kind in ("wi_", "wh_"):
            w = v[l + "lstm_" + kind + way].reshape(EXPERTS, KT, P, 4, 4, UNITS)[:, :, :, order]
            o[l + "lstm_" + kind + way] = w.transpose(0, 2, 1, 4, 3, 5).reshape(EXPERTS, P, KT, GATES)
        b = v[l + "lstm_b_" + way].reshape(EXPERTS, 4, 4, UNITS)[:, order]
        o[l + "lstm_b_" + way] = b.transpose(0, 2, 1, 3).reshape(EXPERTS, GATES)
    return {n: np.ascontiguousarray(x) for n, x in o.items()}


def kernel(**inputs):
    import concourse.bacc as bacc
    from concourse.bass_utils import run_bass_kernel_spmd

    nc = bacc.Bacc("TRN2", target_bir_lowering=False, num_devices=1)
    arrays = {f"in_{n}": x for n, x in lay_out(inputs).items()}
    aps = {n[len("in_"):]: nc.dram_tensor(n, x.shape, mybir.dt.from_np(x.dtype), kind="ExternalInput").ap()
           for n, x in arrays.items()}
    aps["out"] = nc.dram_tensor("out_hidden", (1, T, D), F32, kind="ExternalOutput").ap()
    program(nc, aps)
    result = run_bass_kernel_spmd(nc, [arrays], core_ids=[0])
    return result.results[0]["out_hidden"]
```

```python
import numpy as np
from contextlib import ExitStack

import concourse.bass as bass
from concourse import mybir
from concourse.alu_op_type import AluOpType as ALU

F32 = mybir.dt.float32
BF16 = mybir.dt.bfloat16
F16 = mybir.dt.float16
I32 = mybir.dt.int32
ACT = mybir.ActivationFunctionType
AX = mybir.AxisListType.X

P = 128
T = 2048
D = 128
TILES = T // P
BLK = 512
BLKS = T // BLK
EPS = 1e-5
NEG = -1e30
HEADS = 8
HD = D // HEADS


class Core:

    def __init__(self, nc, ctx):
        self.nc = nc
        self.loaded = nc.alloc_semaphore("loaded")
        self.loaded_odd = nc.alloc_semaphore("loaded_odd")
        self.stored = nc.alloc_semaphore("stored")
        self.multiplied = nc.alloc_semaphore("multiplied")
        self.evacuated = nc.alloc_semaphore("evacuated")
        self.activated = nc.alloc_semaphore("activated")
        self.stepped = nc.alloc_semaphore("stepped")
        self.vectored = nc.alloc_semaphore("vectored")
        self.transposed = nc.alloc_semaphore("transposed")
        self.copied = nc.alloc_semaphore("copied")
        self.scored = nc.alloc_semaphore("scored")
        self.reduced = nc.alloc_semaphore("reduced")
        self.turned = nc.alloc_semaphore("turned")
        self.pooled = nc.alloc_semaphore("pooled")
        self.gathered = nc.alloc_semaphore("gathered")
        self.first, self.last = self.loaded.num, self.pooled.num
        self.count = 0
        self.psum = ctx.enter_context(nc.psum_tensor("banks", [P, 8, BLK], F32))
        self.ident = ctx.enter_context(nc.sbuf_tensor("ident", [P, P], F32))
        self.identb = ctx.enter_context(nc.sbuf_tensor("identb", [P, P], BF16))
        self.headmask = ctx.enter_context(nc.sbuf_tensor("headmask", [P, HEADS], F32))
        self.x = ctx.enter_context(nc.sbuf_tensor("x_resid", [P, TILES, D], F32))

    def sb(self, mem, name, shape, dtype=F32):
        self.count += 1
        return mem.enter_context(self.nc.sbuf_tensor(f"{name}_{self.count}", shape, dtype))

    def clear(self):
        with self.nc.Block() as block:
            @block.vector
            def _(dve):
                dve.sem_clear(range(self.first, self.last + 1))


class Chain:

    def __init__(self, eng, sem):
        self.eng, self.sem, self.n = eng, sem, 0

    def __call__(self, ins):
        self.n += 1
        ins.then_inc(self.sem, 1)
        self.eng.wait_ge(self.sem, self.n)


def constants(c):
    nc = c.nc
    with nc.Block() as block:
        @block.gpsimd
        def _(pool):
            step = Chain(pool, c.pooled)
            step(nc.gpsimd.memset(c.ident[:, :], 0.0))
            step(nc.gpsimd.affine_select(out=c.ident[:, :], in_=c.ident[:, :], compare_op=ALU.not_equal,
                                         fill=1.0, base=0, pattern=[[-1, P]], channel_multiplier=1))
            step(nc.gpsimd.memset(c.identb[:, :], 0.0))
            step(nc.gpsimd.affine_select(out=c.identb[:, :], in_=c.identb[:, :], compare_op=ALU.not_equal,
                                         fill=1.0, base=0, pattern=[[-1, P]], channel_multiplier=1))
            step(nc.gpsimd.memset(c.headmask[:, :], 1.0))
            step(nc.gpsimd.affine_select(out=c.headmask[:, :], in_=c.headmask[:, :], compare_op=ALU.is_ge,
                                         fill=0.0, base=0, pattern=[[-HD, HEADS]], channel_multiplier=1))
            step(nc.gpsimd.affine_select(out=c.headmask[:, :], in_=c.headmask[:, :], compare_op=ALU.is_ge,
                                         fill=0.0, base=HD - 1, pattern=[[HD, HEADS]], channel_multiplier=-1))
    c.clear()


def gather(c, ids, table):
    nc = c.nc
    with nc.sbuf_tensor("token_ids", [P, TILES], I32) as idx, nc.Block() as block:
        @block.gpsimd
        def _(pool):
            nc.gpsimd.dma_start(idx[:, :], ids).then_inc(c.gathered, 16)
            pool.wait_ge(c.gathered, 16)
            for i in range(TILES):
                nc.gpsimd.indirect_dma_start(
                    out=c.x[:, i, :], out_offset=None, in_=table,
                    in_offset=bass.IndirectOffsetOnAxis(ap=idx[:, i:i + 1], axis=0),
                ).then_inc(c.gathered, 16)
            pool.wait_ge(c.gathered, 16 * (TILES + 1))


def normalize(c, src, dst, n, width, gamma=None, beta=None, loads=(), plus=None, residual=None):
    nc = c.nc
    with ExitStack() as mem:
        sq = c.sb(mem, "ln_squares", [P, n, width])
        mean = c.sb(mem, "ln_mean", [P, n])
        var = c.sb(mem, "ln_var", [P, n])
        std = c.sb(mem, "ln_std", [P, n])
        block = mem.enter_context(nc.Block())

        def wide(ap):
            return ap.unsqueeze(2).to_broadcast([P, n, width])

        def row(ap):
            return ap.unsqueeze(1).to_broadcast([P, n, width])

        @block.sync
        def _(sp):
            for to, frm in loads:
                sp.dma_start(to, frm).then_inc(c.loaded, 16)
            if loads:
                sp.wait_ge(c.loaded, 16 * len(loads))

        @block.vector
        def _(dve):
            step = Chain(dve, c.stepped)
            inp = src
            if plus is not None:
                step(nc.vector.tensor_tensor(dst, src, plus, ALU.add))
                inp = dst
            step(nc.vector.tensor_reduce(mean[:, :], inp, AX, ALU.add))
            step(nc.vector.tensor_scalar(mean[:, :], mean[:, :], 1.0 / width, None, ALU.mult))
            step(nc.vector.tensor_tensor(dst, inp, wide(mean[:, :]), ALU.subtract))
            step(nc.vector.tensor_tensor(sq[:, :, :], dst, dst, ALU.mult))
            step(nc.vector.tensor_reduce(var[:, :], sq[:, :, :], AX, ALU.add))
            nc.vector.tensor_scalar(var[:, :], var[:, :], 1.0 / width, EPS, ALU.mult, ALU.add).then_inc(c.vectored, 1)
            dve.wait_ge(c.activated, 1)
            step(nc.vector.reciprocal(std[:, :], std[:, :]))
            step(nc.vector.tensor_tensor(dst, dst, wide(std[:, :]), ALU.mult))
            if gamma is not None:
                step(nc.vector.tensor_tensor(dst, dst, row(gamma), ALU.mult))
                step(nc.vector.tensor_tensor(dst, dst, row(beta), ALU.add))
            if residual is not None:
                step(nc.vector.tensor_tensor(residual, residual, dst, ALU.add))

        @block.scalar
        def _(act):
            act.wait_ge(c.vectored, 1)
            nc.scalar.activation(std[:, :], var[:, :], ACT.Sqrt).then_inc(c.activated, 1)
    c.clear()


def transpose_tiles(c, tiles):
    nc = c.nc
    with nc.Block() as block:
        @block.tensor
        def _(pe):
            for j, (sources, _) in enumerate(tiles):
                if j >= 8:
                    pe.wait_ge(c.evacuated, j - 7)
                for q, source in enumerate(sources):
                    last = nc.tensor.transpose(c.psum[:, j % 8, q * P:(q + 1) * P], source, c.ident[:, :])
                last.then_inc(c.transposed, 1)

        @block.scalar
        def _(act):
            for j, (sources, target) in enumerate(tiles):
                act.wait_ge(c.transposed, j + 1)
                nc.scalar.activation(target, c.psum[:, j % 8, :len(sources) * P], ACT.Copy).then_inc(c.evacuated, 1)
    c.clear()


def dense_features(c, xT, w, kt, mt, out, func, bias=None, loads=(), m_size=P, scale=1.0):
    nc = c.nc
    jobs = [(m, b) for m in range(mt) for b in range(BLKS)]
    with nc.Block() as block:
        @block.sync
        def _(sp):
            for to, frm in loads:
                sp.dma_start(to, frm).then_inc(c.loaded, 16)

        @block.tensor
        def _(pe):
            if loads:
                pe.wait_ge(c.loaded, 16 * len(loads))
            for j, (m, b) in enumerate(jobs):
                if j >= 8:
                    pe.wait_ge(c.evacuated, j - 7)
                for k in range(kt):
                    last = nc.tensor.matmul(c.psum[0:m_size, j % 8, :], w(k, m), xT(k, b),
                                            start=(k == 0), stop=(k == kt - 1))
                last.then_inc(c.multiplied, 1)

        @block.scalar
        def _(act):
            if loads:
                act.wait_ge(c.loaded, 16 * len(loads))
            for j, (m, b) in enumerate(jobs):
                act.wait_ge(c.multiplied, j + 1)
                if bias is None:
                    ins = nc.scalar.activation(out(m, b), c.psum[0:m_size, j % 8, :], func, scale=scale)
                else:
                    ins = nc.scalar.activation(out(m, b), c.psum[0:m_size, j % 8, :], func, bias=bias(m), scale=scale)
                ins.then_inc(c.evacuated, 1)
    c.clear()


def dense_tokens(c, xT, w, kt, cols, out, plus=None, loads=(), scale=None):
    nc = c.nc
    jobs = [(i, n) for i in range(TILES) for n in range(len(cols))]
    with nc.Block() as block:
        @block.sync
        def _(sp):
            for to, frm in loads:
                sp.dma_start(to, frm).then_inc(c.loaded, 16)

        @block.tensor
        def _(pe):
            if loads:
                pe.wait_ge(c.loaded, 16 * len(loads))
            for j, (i, n) in enumerate(jobs):
                if j >= 8:
                    pe.wait_ge(c.evacuated, j - 7)
                for k in range(kt):
                    last = nc.tensor.matmul(c.psum[:, j % 8, 0:cols[n]], xT(k, i), w(k, n),
                                            start=(k == 0), stop=(k == kt - 1))
                last.then_inc(c.multiplied, 1)

        @block.vector
        def _(dve):
            if loads:
                dve.wait_ge(c.loaded, 16 * len(loads))
            for j, (i, n) in enumerate(jobs):
                dve.wait_ge(c.multiplied, j + 1)
                ps = c.psum[:, j % 8, 0:cols[n]]
                if plus is None:
                    ins = nc.vector.tensor_copy(out(i, n), ps)
                else:
                    ins = nc.vector.tensor_tensor(out(i, n), ps, plus(i, n), ALU.add)
                ins.then_inc(c.evacuated, 1)
    c.clear()


def windowed_attention(c, qT, kTm, v, oT, w, scale):
    nc = c.nc
    span = 2 * w + 1
    hb = 8 if span * P <= BLK else 4
    per = 8 // hb
    with ExitStack() as mem:
        mask = c.sb(mem, "band_mask", [P, span * P])
        s = c.sb(mem, "scores", [P, hb, span * P])
        pT = c.sb(mem, "probs_T", [P, hb * span, P])
        qt = c.sb(mem, "q_tile", [P, P])
        mx = c.sb(mem, "row_max", [P, HEADS])
        total = c.sb(mem, "row_sum", [P, HEADS])
        o = c.sb(mem, "o_tile", [P, D])

        with nc.Block() as block:
            @block.gpsimd
            def _(pool):
                step = Chain(pool, c.pooled)
                step(nc.gpsimd.memset(mask[:, :], 0.0))
                step(nc.gpsimd.affine_select(out=mask[:, :], in_=mask[:, :], compare_op=ALU.is_ge, fill=NEG,
                                             base=0, pattern=[[1, span * P]], channel_multiplier=-1))
                step(nc.gpsimd.affine_select(out=mask[:, :], in_=mask[:, :], compare_op=ALU.is_ge, fill=NEG,
                                             base=2 * w * P, pattern=[[-1, span * P]], channel_multiplier=1))
        c.clear()

        def tile(i, lo, n, skip):
            cols = n * P
            banks = c.psum[:, :, :].rearrange("p (h two) f -> p h (two f)", two=per)
            flat = c.psum[:, :, :].rearrange("p b f -> p (b f)")
            for h0 in range(0, HEADS, hb):
                heads = range(h0, h0 + hb)
                with nc.Block() as block:
                    @block.tensor
                    def _(pe):
                        pe.wait_ge(c.stepped, 1)
                        for h in heads:
                            for at in range(0, cols, BLK):
                                size = min(BLK, cols - at)
                                last = nc.tensor.matmul(banks[:, h - h0, at:at + size], qt[:, :],
                                                        kTm[:, h, bass.ds(lo * P + at, size)], start=True, stop=True)
                        last.then_inc(c.multiplied, 1)
                        pe.wait_ge(c.activated, hb)
                        for j in range(hb * n):
                            h, kt = divmod(j, n)
                            last = nc.tensor.transpose(flat[:, j * P:(j + 1) * P], s[:, h, kt * P:(kt + 1) * P],
                                                       c.ident[:, :])
                        last.then_inc(c.transposed, 1)
                        pe.wait_ge(c.copied, 1)
                        for h in heads:
                            for kt in range(n):
                                last = nc.tensor.matmul(c.psum[:, 7, h * HD:(h + 1) * HD], pT[:, (h - h0) * n + kt, :],
                                                        v[:, bass.ds(lo + kt, 1), h * HD:(h + 1) * HD],
                                                        start=(kt == 0), stop=(kt == n - 1))
                        last.then_inc(c.multiplied, 1)
                        if h0 + hb == HEADS:
                            pe.wait_ge(c.vectored, 2)
                            nc.tensor.transpose(c.psum[:, 6, 0:P], o[:, :], c.ident[:, :]).then_inc(c.transposed, 1)

                    @block.vector
                    def _(dve):
                        step = Chain(dve, c.stepped)
                        step(nc.vector.tensor_copy(qt[:, :], qT[:, bass.ds(i * P, P)]))
                        dve.wait_ge(c.multiplied, 1)
                        step(nc.vector.tensor_tensor(
                            s[:, :, 0:cols], banks[:, 0:hb, 0:cols],
                            mask[:, skip:skip + cols].unsqueeze(1).to_broadcast([P, hb, cols]), ALU.add))
                        step(nc.vector.tensor_reduce(mx[:, 0:hb], s[:, :, 0:cols], AX, ALU.max))
                        nc.vector.tensor_scalar(mx[:, 0:hb], mx[:, 0:hb], -scale, None, ALU.mult).then_inc(c.vectored, 1)
                        dve.wait_ge(c.activated, hb)
                        step(nc.vector.reciprocal(total[:, 0:hb], total[:, 0:hb]))
                        dve.wait_ge(c.multiplied, 2)
                        nc.vector.tensor_tensor(
                            o[:, h0 * HD:(h0 + hb) * HD].rearrange("p (h d) -> p h d", d=HD),
                            c.psum[:, 7, h0 * HD:(h0 + hb) * HD].rearrange("p (h d) -> p h d", d=HD),
                            total[:, 0:hb].unsqueeze(2).to_broadcast([P, hb, HD]), ALU.mult).then_inc(c.vectored, 1)

                    @block.scalar
                    def _(act):
                        act.wait_ge(c.vectored, 1)
                        for j in range(hb):
                            nc.scalar.activation(s[:, j, 0:cols], s[:, j, 0:cols], ACT.Exp, bias=mx[:, j:j + 1],
                                                 scale=scale, accum_out=total[:, j:j + 1]).then_inc(c.activated, 1)
                        act.wait_ge(c.transposed, 1)
                        nc.scalar.activation(pT[:, 0:hb * n, :].rearrange("p a b -> p (a b)"), flat[:, 0:hb * n * P],
                                             ACT.Copy).then_inc(c.copied, 1)
                        if h0 + hb == HEADS:
                            act.wait_ge(c.transposed, 2)
                            nc.scalar.activation(oT[:, bass.ds(i * P, P)], c.psum[:, 6, 0:P], ACT.Copy).then_inc(c.copied, 1)
                c.clear()

        for i in range(w):
            tile(i, 0, i + w + 1, (w - i) * P)
        with nc.Fori(w, TILES - w) as i:
            tile(i, i - w, span, 0)
        for i in range(TILES - w, TILES):
            tile(i, i - w, TILES - i + w, 0)


def layer0_attention(c, w_qkv, w_proj):
    nc = c.nc
    with ExitStack() as mem:
        def sb(name, shape):
            return c.sb(mem, name, shape)
        xn = sb("a0_xn", [P, TILES, D])
        xT = sb("a0_xT", [P, T])
        wq = sb("a0_wqkv", [P, 3 * D])
        wp = sb("a0_wproj", [P, D])
        qT, kT, kTm = sb("a0_qT", [P, T]), sb("a0_kT", [P, T]), sb("a0_kTm", [P, HEADS, T])
        v = sb("a0_v", [P, TILES, D])
        normalize(c, c.x[:, :, :], xn[:, :, :], TILES, D)
        transpose_tiles(c, [([xn[:, 4 * b + q, :] for q in range(4)], xT[:, b * BLK:(b + 1) * BLK]) for b in range(BLKS)])
        dense_features(c, lambda k, b: xT[:, b * BLK:(b + 1) * BLK], lambda k, m: wq[:, m * D:(m + 1) * D], 1, 2,
                       lambda m, b: (qT, kT)[m][:, b * BLK:(b + 1) * BLK], ACT.Copy,
                       loads=[(wq[:, :], w_qkv), (wp[:, :], w_proj)])
        dense_tokens(c, lambda k, i: xT[:, i * P:(i + 1) * P], lambda k, n: wq[:, 2 * D:3 * D], 1, [D],
                     lambda i, n: v[:, i, :])
        mask_keys(c, kT, kTm)
        oT = kT
        windowed_attention(c, qT, kTm, v, oT, 1, float(D) ** -0.5)
        dense_tokens(c, lambda k, i: oT[:, i * P:(i + 1) * P], lambda k, n: wp[:, :], 1, [D],
                     lambda i, n: c.x[:, i, :], plus=lambda i, n: c.x[:, i, :])


def mask_keys(c, kT, kTm):
    nc = c.nc
    with nc.Block() as block:
        @block.vector
        def _(dve):
            for h in range(HEADS):
                nc.vector.tensor_scalar(kTm[:, h, :], kT[:, :], c.headmask[:, h:h + 1], None, ALU.mult)
    c.clear()


EXPERTS0, TOPK, SHARED = 64, 8, 352
SHARED_PARTS = [(0, 128), (128, 128), (256, 96)]


def moe(c, gate_wT, w1, w3, w2, sw1, sw3, sw2):
    nc = c.nc
    with ExitStack() as mem:
        def sb(name, shape):
            return c.sb(mem, name, shape)
        xn = sb("m_xn", [P, TILES, D])
        xT = sb("m_xT", [P, T])
        gw = sb("m_gate_w", [P, EXPERTS0])
        logits = sb("m_logits", [P, TILES, EXPERTS0])
        rest = sb("m_rest", [P, TILES, EXPERTS0])
        best = sb("m_best", [P, TILES, TOPK])
        gate = sb("m_gate", [P, TILES, EXPERTS0])
        total = sb("m_total", [P, TILES])
        s1, s3 = sb("m_sw1", [P, SHARED]), sb("m_sw3", [P, SHARED])
        s2 = sb("m_sw2", [P, 3, D])
        normalize(c, c.x[:, :, :], xn[:, :, :], TILES, D)
        transpose_tiles(c, [([xn[:, 4 * b + q, :] for q in range(4)], xT[:, b * BLK:(b + 1) * BLK]) for b in range(BLKS)])
        dense_tokens(c, lambda k, i: xT[:, i * P:(i + 1) * P], lambda k, n: gw[:, :], 1, [EXPERTS0],
                     lambda i, n: logits[:, i, :],
                     loads=[(gw[:, :], gate_wT), (s1[:, :], sw1), (s3[:, :], sw3)]
                     + [(s2[0:n, j, :], sw2[a:a + n, :]) for j, (a, n) in enumerate(SHARED_PARTS)])
        with nc.Block() as block:
            @block.vector
            def _(dve):
                step = Chain(dve, c.stepped)
                for i in range(TILES):
                    nc.vector.max(best[:, i, :], logits[:, i, :]).then_inc(c.vectored, 1)
                for i in range(TILES):
                    dve.wait_ge(c.vectored, i + 1)
                    last = nc.vector.match_replace(rest[:, i, :], best[:, i, :], logits[:, i, :], -3e38)
                step(last)
                step(nc.vector.tensor_tensor(gate[:, :, :], logits[:, :, :],
                                             best[:, :, 0:1].to_broadcast([P, TILES, EXPERTS0]), ALU.subtract))
                step(nc.vector.tensor_tensor(rest[:, :, :], rest[:, :, :], logits[:, :, :], ALU.not_equal))
                dve.wait_ge(c.activated, 1)
                step(nc.vector.tensor_tensor(gate[:, :, :], gate[:, :, :], rest[:, :, :], ALU.mult))
                step(nc.vector.tensor_reduce(total[:, :], gate[:, :, :], AX, ALU.add))
                step(nc.vector.reciprocal(total[:, :], total[:, :]))
                step(nc.vector.tensor_tensor(gate[:, :, :], gate[:, :, :],
                                             total[:, :].unsqueeze(2).to_broadcast([P, TILES, EXPERTS0]), ALU.mult))

            @block.scalar
            def _(act):
                act.wait_ge(c.stepped, 2)
                nc.scalar.activation(gate[:, :, :], gate[:, :, :], ACT.Exp).then_inc(c.activated, 1)
        c.clear()
        shared_expert(c, xT, s1, s3, s2)
        routed_experts(c, xT, gate, w1, w3, w2)


def shared_expert(c, xT, s1, s3, s2):
    nc = c.nc
    parts = len(SHARED_PARTS)
    with ExitStack() as mem:
        hid = c.sb(mem, "m_shared_hidden", [P, parts, T])
        sig = c.sb(mem, "m_sig", [P, 2, BLK])
        jobs = [(m, b) for m in range(parts) for b in range(BLKS)]
        with nc.Block() as block:
            @block.tensor
            def _(pe):
                for j, (m, b) in enumerate(jobs):
                    a, n = SHARED_PARTS[m]
                    if j >= 4:
                        pe.wait_ge(c.evacuated, j - 3)
                    nc.tensor.matmul(c.psum[0:n, 2 * (j % 4), :], s1[:, a:a + n], xT[:, b * BLK:(b + 1) * BLK],
                                     start=True, stop=True)
                    nc.tensor.matmul(c.psum[0:n, 2 * (j % 4) + 1, :], s3[:, a:a + n], xT[:, b * BLK:(b + 1) * BLK],
                                     start=True, stop=True).then_inc(c.multiplied, 1)

            @block.scalar
            def _(act):
                for j, (m, b) in enumerate(jobs):
                    n = SHARED_PARTS[m][1]
                    act.wait_ge(c.multiplied, j + 1)
                    if j >= 2:
                        act.wait_ge(c.evacuated, j - 1)
                    nc.scalar.activation(sig[0:n, j % 2, :], c.psum[0:n, 2 * (j % 4), :], ACT.Sigmoid).then_inc(c.activated, 1)

            @block.vector
            def _(dve):
                step = Chain(dve, c.stepped)
                for j, (m, b) in enumerate(jobs):
                    n = SHARED_PARTS[m][1]
                    h = hid[0:n, m, b * BLK:(b + 1) * BLK]
                    dve.wait_ge(c.activated, j + 1)
                    step(nc.vector.tensor_tensor(h, sig[0:n, j % 2, :], c.psum[0:n, 2 * (j % 4), :], ALU.mult))
                    nc.vector.tensor_tensor(h, h, c.psum[0:n, 2 * (j % 4) + 1, :], ALU.mult).then_inc(c.evacuated, 1)
        c.clear()
        dense_tokens(c, lambda k, i: hid[0:SHARED_PARTS[k][1], k, i * P:(i + 1) * P],
                     lambda k, n: s2[0:SHARED_PARTS[k][1], k, :], parts, [D],
                     lambda i, n: c.x[:, i, :], plus=lambda i, n: c.x[:, i, :])


def routed_experts(c, xT, gate, w1, w3, w2):
    nc = c.nc
    PAIRS = EXPERTS0 // 2
    LAST = (PAIRS - 1) * 8
    with ExitStack() as mem:
        wt = c.sb(mem, "m_weights", [P, 2, 3, D])
        sig = c.sb(mem, "m_sigmoid", [P, 2, BLK])
        hid = c.sb(mem, "m_hidden", [P, 2, BLK])
        hidden, output, added = c.vectored, c.transposed, c.evacuated
        weights = (c.loaded, c.loaded_odd)
        with nc.Block() as block:
            @block.vector
            def _(dve):
                dve.sem_inc(hidden, 2)
                dve.sem_inc(output, 6)
                dve.sem_inc(added, 4)

        with nc.Block() as block:
            @block.sync
            def _(sp):
                with sp.Fori(0, PAIRS) as pair:
                    for par in range(2):
                        sp.wait_ge(output, pair * 8 + (4 * par + 2))
                        for j, w in enumerate((w1, w3, w2)):
                            sp.dma_start(wt[:, par, j, :], w[bass.ds(pair * 2 + par, 1), :, :].rearrange("a p n -> p (a n)")
                                         ).then_inc(weights[par], 16)

            @block.tensor
            def _(pe):
                def up(n0, pos):
                    b, par, q = pos % 4, pos // 4 % 2, pos % 2
                    if b == 0:
                        pe.wait_ge(weights[par], (n0 + pos - 4 * par) * 6 + 48)
                    pe.wait_ge(hidden, n0 + pos + 1)
                    nc.tensor.matmul(c.psum[:, 2 * q, :], wt[:, par, 0, :], xT[:, b * BLK:(b + 1) * BLK],
                                     start=True, stop=True)
                    nc.tensor.matmul(c.psum[:, 2 * q + 1, :], wt[:, par, 1, :], xT[:, b * BLK:(b + 1) * BLK],
                                     start=True, stop=True).then_inc(c.multiplied, 1)

                def down(n0, pos):
                    par, q = pos // 4 % 2, pos % 2
                    pe.wait_ge(hidden, n0 + pos + 3)
                    pe.wait_ge(added, n0 + pos + 3)
                    for t in range(4):
                        last = nc.tensor.matmul(c.psum[:, 4 + q, t * D:(t + 1) * D], hid[:, q, t * P:(t + 1) * P],
                                                wt[:, par, 2, :], start=True, stop=True)
                    last.then_inc(output, 1)

                up(0, 0)
                with pe.Fori(0, PAIRS - 1) as pair:
                    for pos in range(8):
                        up(pair * 8, pos + 1)
                        down(pair * 8, pos)
                for pos in range(8):
                    if pos < 7:
                        up(LAST, pos + 1)
                    down(LAST, pos)

            @block.scalar
            def _(act):
                with act.Fori(0, PAIRS) as pair:
                    for pos in range(8):
                        act.wait_ge(c.multiplied, pair * 8 + (pos + 1))
                        act.wait_ge(hidden, pair * 8 + (pos + 1))
                        nc.scalar.activation(sig[:, pos % 2, :], c.psum[:, 2 * (pos % 2), :], ACT.Sigmoid).then_inc(c.activated, 1)

            @block.vector
            def _(dve):
                def make_hidden(n0, pos):
                    q = pos % 2
                    dve.wait_ge(c.activated, n0 + pos + 1)
                    nc.vector.tensor_tensor(sig[:, q, :], sig[:, q, :], c.psum[:, 2 * q, :], ALU.mult).then_inc(c.stepped, 1)
                    dve.wait_ge(c.stepped, n0 + pos + 1)
                    dve.wait_ge(output, n0 + pos + 5)
                    nc.vector.tensor_tensor(hid[:, q, :], sig[:, q, :], c.psum[:, 2 * q + 1, :], ALU.mult).then_inc(hidden, 1)

                def add(n0, pos, e):
                    b, q = pos % 4, pos % 2
                    dve.wait_ge(output, n0 + pos + 7)
                    dve.wait_ge(added, n0 + pos + 1)
                    for t in range(4):
                        i = 4 * b + t
                        last = nc.vector.scalar_tensor_tensor(
                            out=c.x[:, i, :], in0=c.psum[:, 4 + q, t * D:(t + 1) * D], scalar=gate[:, i, bass.ds(e, 1)],
                            in1=c.x[:, i, :], op0=ALU.mult, op1=ALU.add)
                    last.then_inc(added, 1)

                make_hidden(0, 0)
                with dve.Fori(0, PAIRS - 1) as pair:
                    for pos in range(8):
                        make_hidden(pair * 8, pos + 1)
                        add(pair * 8, pos, pair * 2 + pos // 4)
                for pos in range(8):
                    if pos < 7:
                        make_hidden(LAST, pos + 1)
                    add(LAST, pos, EXPERTS0 - 2 + pos // 4)
        c.clear()


def layer1_attention(c, a):
    nc = c.nc
    with ExitStack() as mem:
        def sb(name, shape):
            return c.sb(mem, name, shape)
        xn = sb("a1_xn", [P, TILES, D])
        xT = sb("a1_xT", [P, T + 2])
        conv, conv_b = sb("a1_conv", [P, 3, D]), sb("a1_conv_b", [P, 1])
        win, qk_b = sb("a1_in_proj", [P, 3 * D]), sb("a1_qk_b", [P, 2])
        v_b, out_b, b2 = sb("a1_v_b", [P, D]), sb("a1_out_b", [P, D]), sb("a1_b2", [P, D])
        ln = sb("a1_ln", [P, 4, D])
        wo, w1, b1, w2 = sb("a1_wo", [P, D]), sb("a1_w1", [P, 2 * D]), sb("a1_b1", [P, 2]), sb("a1_w2", [P, 2, D])
        v = sb("a1_v", [P, TILES, D])
        h = sb("a1_h", [P, TILES, D])

        def cols(b, tap=1):
            return xT[:, b * BLK + tap:(b + 1) * BLK + tap]

        def wide(row):
            return row.partition_broadcast(P)

        loads = [(conv[:, :, :], a["L1_attn_conv_w"]), (conv_b[:, :], a["L1_attn_conv_b"]),
                 (win[:, :], a["L1_attn_in_proj_w"]), (qk_b[:, :], a["L1_attn_qk_b"]),
                 (v_b[:, :], wide(a["L1_attn_v_b"])), (out_b[:, :], wide(a["L1_attn_out_proj_b"])),
                 (b2[:, :], wide(a["L1_attn_b2"])), (wo[:, :], a["L1_attn_out_proj_w"]),
                 (w1[:, :], a["L1_attn_w1"]), (b1[:, :], a["L1_attn_b1"]), (w2[:, :, :], a["L1_attn_w2"])]
        loads += [(ln[:, j, :], wide(a["L1_attn_" + n])) for j, n in enumerate(("ln1_g", "ln1_b", "ln2_g", "ln2_b"))]
        normalize(c, c.x[:, :, :], xn[:, :, :], TILES, D, loads=loads)
        with nc.Block() as block:
            @block.vector
            def _(dve):
                nc.vector.memset(xT[:, 0:1], 0.0)
                nc.vector.memset(xT[:, T + 1:T + 2], 0.0)
        transpose_tiles(c, [([xn[:, 4 * b + q, :] for q in range(4)], cols(b)) for b in range(BLKS)])
        with ExitStack() as inner:
            vinT = c.sb(inner, "a1_vinT", [P, T])
            qT = c.sb(inner, "a1_qT", [P, T])
            kT = c.sb(inner, "a1_kT", [P, T])
            kTm = c.sb(inner, "a1_kTm", [P, HEADS, T])
            dense_features(c, lambda k, b: cols(b, k), lambda k, m: conv[:, k, :], 3, 1,
                           lambda m, b: vinT[:, b * BLK:(b + 1) * BLK], ACT.Identity, bias=lambda m: conv_b[:, 0:1])
            dense_features(c, lambda k, b: cols(b), lambda k, m: win[:, m * D:(m + 1) * D], 1, 2,
                           lambda m, b: (qT, kT)[m][:, b * BLK:(b + 1) * BLK], ACT.Identity,
                           bias=lambda m: qk_b[:, m:m + 1])
            dense_tokens(c, lambda k, i: vinT[:, i * P:(i + 1) * P], lambda k, n: win[:, 2 * D:3 * D], 1, [D],
                         lambda i, n: v[:, i, :], plus=lambda i, n: v_b[:, :])
            mask_keys(c, kT, kTm)
            oT = kT
            windowed_attention(c, qT, kTm, v, oT, 2, float(HD) ** -0.5)
            dense_tokens(c, lambda k, i: oT[:, i * P:(i + 1) * P], lambda k, n: wo[:, :], 1, [D],
                         lambda i, n: h[:, i, :], plus=lambda i, n: xn[:, i, :])
        with nc.Block() as block:
            @block.vector
            def _(dve):
                nc.vector.tensor_tensor(h[:, :, :], h[:, :, :], out_b[:, :].unsqueeze(1).to_broadcast([P, TILES, D]), ALU.add)
        normalize(c, h[:, :, :], xn[:, :, :], TILES, D, gamma=ln[:, 0, :], beta=ln[:, 1, :])
        transpose_tiles(c, [([xn[:, 4 * b + q, :] for q in range(4)], cols(b)) for b in range(BLKS)])
        with ExitStack() as inner:
            hid = c.sb(inner, "a1_hidden", [P, 2, T])
            dense_features(c, lambda k, b: cols(b), lambda k, m: w1[:, m * D:(m + 1) * D], 1, 2,
                           lambda m, b: hid[:, m, b * BLK:(b + 1) * BLK], ACT.Relu, bias=lambda m: b1[:, m:m + 1])
            dense_tokens(c, lambda k, i: hid[:, k, i * P:(i + 1) * P], lambda k, n: w2[:, k, :], 2, [D],
                         lambda i, n: h[:, i, :], plus=lambda i, n: b2[:, :])
        normalize(c, h[:, :, :], h[:, :, :], TILES, D, gamma=ln[:, 2, :], beta=ln[:, 3, :], plus=xn[:, :, :],
                  residual=c.x[:, :, :])


EXPERTS = 4
W = 256
KT = W // P
GROUPS = 4
GH = 4
PARTS = 6
STACK = PARTS * HD
GATES = 4 * W
MT = GATES // P
UNITS = KT * EXPERTS
FULL = 2.0 ** 14
CH = 64
SUPER = 64


def wide(row):
    return row.partition_broadcast(P)


def expert_front(c, a, e, xT, zx):
    nc = c.nc
    with ExitStack() as mem:
        oT = c.sb(mem, "f_oT", [P, GROUPS, T])
        with ExitStack() as m1:
            qkv = c.sb(m1, "f_qkv", [P, TILES, 3 * W])
            with ExitStack() as m2:
                w1, b1 = c.sb(m2, "f_w1", [P, W]), c.sb(m2, "f_b1", [P, KT])
                w2, rows = c.sb(m2, "f_w2", [P, KT, W]), c.sb(m2, "f_rows", [P, 3, W])
                hid, h = c.sb(m2, "f_hid", [P, KT, T]), c.sb(m2, "f_h", [P, TILES, W])
                loads = [(w1[:, :], a["enc_w1"][e]), (b1[:, :], a["enc_b1"][e]), (w2[:, :, :], a["enc_w2"][e])]
                loads += [(rows[:, j, :], wide(a[n][e])) for j, n in enumerate(("enc_b2", "enc_g", "enc_beta"))]
                dense_features(c, lambda k, b: xT[:, b * BLK:(b + 1) * BLK], lambda k, m: w1[:, m * P:(m + 1) * P], 1, KT,
                               lambda m, b: hid[:, m, b * BLK:(b + 1) * BLK], ACT.Relu, bias=lambda m: b1[:, m:m + 1],
                               loads=loads)
                dense_tokens(c, lambda k, i: hid[:, k, i * P:(i + 1) * P], lambda k, n: w2[:, k, :], KT, [W],
                             lambda i, n: h[:, i, :], plus=lambda i, n: rows[:, 0, :])
                normalize(c, h[:, :, :], h[:, :, :], TILES, W, gamma=rows[:, 1, :], beta=rows[:, 2, :])
                transpose_tiles(c, [([h[:, 4 * b + q, k * P:(k + 1) * P] for q in range(4)], hid[:, k, b * BLK:(b + 1) * BLK])
                                    for k in range(KT) for b in range(BLKS)])
                with ExitStack() as m3:
                    win, bin_ = c.sb(m3, "f_in_w", [P, KT, 3 * W]), c.sb(m3, "f_in_b", [P, 3 * W])
                    at = [(0, BLK), (BLK, 3 * W)]
                    dense_tokens(c, lambda k, i: hid[:, k, i * P:(i + 1) * P], lambda k, n: win[:, k, at[n][0]:at[n][1]],
                                 KT, [y - x for x, y in at], lambda i, n: qkv[:, i, at[n][0]:at[n][1]],
                                 plus=lambda i, n: bin_[:, at[n][0]:at[n][1]],
                                 loads=[(win[:, :, :], a["attn_in_w"][e]), (bin_[:, :], wide(a["attn_in_b"][e]))])
            full_attention(c, qkv, oT)
            divide_by_sums(c, oT)
        hT = c.sb(mem, "f_hT", [P, KT, T])
        wo, bo = c.sb(mem, "f_wo", [P, GROUPS, W]), c.sb(mem, "f_bo", [P, KT])
        with nc.Block() as block:
            @block.vector
            def _(dve):
                nc.vector.memset(wo[:, :, :], 0.0)
        loads = [(wo[32 * h:32 * h + HD, :, :], a["attn_out_w"][e][:, h, :, :].rearrange("g d n -> d g n")) for h in range(GH)]
        dense_features(c, lambda k, b: oT[:, k, b * BLK:(b + 1) * BLK], lambda k, m: wo[:, k, m * P:(m + 1) * P], GROUPS, KT,
                       lambda m, b: hT[:, m, b * BLK:(b + 1) * BLK], ACT.Identity, bias=lambda m: bo[:, m:m + 1],
                       loads=loads + [(bo[:, :], a["attn_out_b"][e])])
        for d, way in enumerate("fb"):
            input_projection(c, hT, a["lstm_wi_" + way][e], a["lstm_b_" + way][e], zx[d], e)


def input_projection(c, hT, wi_dram, b_dram, zx, e):
    nc = c.nc
    jobs = [(m, b) for m in range(MT) for b in range(BLKS)]
    with ExitStack() as mem:
        wi, bias = c.sb(mem, "p_wi", [P, KT, GATES]), c.sb(mem, "p_b", [P, MT])
        stage = c.sb(mem, "p_stage", [P, 2, BLKS, BLK])
        with nc.Block() as block:
            @block.sync
            def _(sp):
                sp.dma_start(wi[:, :, :], wi_dram).then_inc(c.loaded, 16)
                sp.dma_start(bias[:, :], b_dram).then_inc(c.loaded, 16)
                for m in range(MT):
                    sp.wait_ge(c.evacuated, BLKS * (m + 1))
                    sp.dma_start(zx[:, m, bass.ds(e, 1), :].rearrange("p a t -> p (a t)"),
                                 stage[:, m % 2, :, :].rearrange("p b t -> p (b t)")).then_inc(c.stored, 16)
                    sp.wait_ge(c.stored, 16 * (m + 1))
                    sp.sem_inc(c.pooled, 1)

            @block.tensor
            def _(pe):
                pe.wait_ge(c.loaded, 32)
                for j, (m, b) in enumerate(jobs):
                    if j >= 8:
                        pe.wait_ge(c.evacuated, j - 7)
                    for k in range(KT):
                        last = nc.tensor.matmul(c.psum[:, j % 8, :], wi[:, k, m * P:(m + 1) * P],
                                                hT[:, k, b * BLK:(b + 1) * BLK], start=(k == 0), stop=(k == KT - 1))
                    last.then_inc(c.multiplied, 1)

            @block.scalar
            def _(act):
                act.wait_ge(c.loaded, 32)
                for j, (m, b) in enumerate(jobs):
                    act.wait_ge(c.multiplied, j + 1)
                    if b == 0 and m >= 2:
                        act.wait_ge(c.pooled, m - 1)
                    nc.scalar.activation(stage[:, m % 2, b, :], c.psum[:, j % 8, :], ACT.Identity,
                                         bias=bias[:, m:m + 1]).then_inc(c.evacuated, 1)
        c.clear()


def full_attention(c, qkv, oT):
    nc = c.nc
    with ExitStack() as mem:
        qs, ks = c.sb(mem, "g_qs", [P, GH, T], BF16), c.sb(mem, "g_ks", [P, GH, T], BF16)
        v4 = c.sb(mem, "g_v4", [P, TILES, GH, 32])
        with nc.Block() as block:
            @block.gpsimd
            def _(pool):
                step = Chain(pool, c.pooled)
                step(nc.gpsimd.memset(v4[:, :, :, HD:32], 0.0))
                step(nc.gpsimd.memset(v4[:, :, :, HD:HD + 1], 1.0))

            @block.vector
            def _(dve):
                nc.vector.memset(ks[STACK:STACK + 3, :, :], 1.0)
        c.clear()
        with nc.Fori(0, GROUPS) as g:
            split_heads(c, qkv, qs, ks, v4, g)
            first_maxima(c, qs, ks)
            with nc.Fori(0, BLKS - 1) as b:
                attend(c, qs, ks, v4, oT, g, b)
            attend(c, qs, ks, v4, oT, g, BLKS - 1, last_block=True)


def divide_by_sums(c, oT):
    nc = c.nc
    CUT = GROUPS * T // 32
    with ExitStack() as mem:
        sel = c.sb(mem, "d_sel", [P, GH, 32])
        sums = c.sb(mem, "d_sums", [P, CUT])
        rows = [oT[32 * h + HD:32 * h + HD + 1, :, :].rearrange("p g t -> p (g t)").rearrange("p (q n) -> p q n", n=CUT)
                for h in range(GH)]
        jobs = [(g, b) for g in range(GROUPS) for b in range(BLKS)]
        with nc.Block() as block:
            @block.gpsimd
            def _(pool):
                step = Chain(pool, c.pooled)
                step(nc.gpsimd.memset(sel[:, :, :], 0.0))
                step(nc.gpsimd.affine_select(out=sel[:, :, :], in_=sel[:, :, :], compare_op=ALU.not_equal, fill=1.0,
                                             base=-HD, pattern=[[-32, GH], [0, 32]], channel_multiplier=1))

            @block.sync
            def _(sp):
                for h in range(GH):
                    sp.dma_start(sums[32 * h:32 * h + 32, :], rows[h]).then_inc(c.loaded, 16)
                sp.wait_ge(c.vectored, 1)
                for h in range(GH):
                    sp.dma_start(rows[h], sums[32 * h:32 * h + 32, :]).then_inc(c.stored, 16)

            @block.tensor
            def _(pe):
                pe.wait_ge(c.pooled, 2)
                pe.wait_ge(c.stored, 16 * GH)
                for j, (g, b) in enumerate(jobs):
                    if j >= 8:
                        pe.wait_ge(c.evacuated, j - 7)
                    nc.tensor.matmul(c.psum[:, j % 8, :], sel[:, :, :].rearrange("p h m -> p (h m)"),
                                     oT[:, g, b * BLK:(b + 1) * BLK], start=True, stop=True).then_inc(c.multiplied, 1)

            @block.vector
            def _(dve):
                dve.wait_ge(c.loaded, 16 * GH)
                nc.vector.reciprocal(sums[:, :], sums[:, :]).then_inc(c.vectored, 1)
                for j, (g, b) in enumerate(jobs):
                    dve.wait_ge(c.multiplied, j + 1)
                    at = oT[:, g, b * BLK:(b + 1) * BLK]
                    nc.vector.tensor_tensor(at, at, c.psum[:, j % 8, :], ALU.mult).then_inc(c.evacuated, 1)
        c.clear()


def banks_bf16(c):
    return c.psum[:, :, :].rearrange("p b f -> p (b f)").bitcast(BF16).rearrange("p (b f) -> p b f", b=8)


def split_heads(c, qkv, qs, ks, v4, g):
    nc = c.nc
    with ExitStack() as mem:
        stacks = [c.sb(mem, "h_q", [P, TILES, GH, STACK], BF16), c.sb(mem, "h_k", [P, TILES, GH, STACK], BF16)]
        rest = [c.sb(mem, "h_qrest", [P, TILES, GH * HD]), c.sb(mem, "h_krest", [P, TILES, GH * HD])]
        places = [((0, 3, 5), (1, 4), (2,)), ((0, 1, 2), (3, 4), (5,))]

        def heads(ap):
            return ap.rearrange("p i (h d) -> p i h d", d=HD)

        def part(s, n):
            return stacks[s][:, :, :, n * HD:(n + 1) * HD]

        bf = banks_bf16(c)
        jobs = [(h, half, s) for h in range(GH) for half in range(2) for s in range(2)]
        with nc.Block() as block:
            @block.gpsimd
            def _(pool):
                for level in range(2):
                    for s in range(2):
                        pool.wait_ge(c.activated, 2 * level + s + 1)
                        for n in places[s][level][1:]:
                            nc.gpsimd.tensor_copy(part(s, n), part(s, places[s][level][0])).then_inc(c.pooled, 1)
                nc.gpsimd.tensor_copy(v4[:, :, :, 0:HD], heads(qkv[:, :, bass.ds(g * (GH * HD) + 2 * W, GH * HD)]))

            @block.scalar
            def _(act):
                for level in range(3):
                    for s in range(2):
                        if level:
                            act.wait_ge(c.vectored, 2 * (level - 1) + s + 1)
                        src = qkv[:, :, bass.ds(g * (GH * HD) + s * W, GH * HD)] if level == 0 else rest[s][:, :, :]
                        nc.scalar.activation(part(s, places[s][level][0]), heads(src), ACT.Copy).then_inc(c.activated, 1)
                for j, (h, half, s) in enumerate(jobs):
                    if s == 0:
                        continue
                    act.wait_ge(c.transposed, j + 1)
                    nc.scalar.activation(ks[0:STACK, h, half * 1024:(half + 1) * 1024], bf[0:STACK, j % 8, :],
                                         ACT.Copy).then_inc(c.copied, 1)

            @block.vector
            def _(dve):
                for level in range(2):
                    for s in range(2):
                        dve.wait_ge(c.activated, 2 * level + s + 1)
                        src = heads(qkv[:, :, bass.ds(g * (GH * HD) + s * W, GH * HD)]) if level == 0 else heads(rest[s][:, :, :])
                        if level:
                            dve.wait_ge(c.vectored, s + 1)
                        nc.vector.tensor_tensor(heads(rest[s][:, :, :]), src, part(s, places[s][level][0]),
                                                ALU.subtract).then_inc(c.vectored, 1)
                for j, (h, half, s) in enumerate(jobs):
                    if s == 1:
                        continue
                    dve.wait_ge(c.transposed, j + 1)
                    nc.vector.tensor_copy(qs[0:STACK, h, half * 1024:(half + 1) * 1024], bf[0:STACK, j % 8, :]).then_inc(c.evacuated, 1)

            @block.tensor
            def _(pe):
                pe.wait_ge(c.activated, 6)
                pe.wait_ge(c.pooled, 6)
                for j, (h, half, s) in enumerate(jobs):
                    if j >= 8:
                        pe.wait_ge(c.copied if s else c.evacuated, (j - 8) // 2 + 1)
                    for q in range(8):
                        last = nc.tensor.transpose(bf[0:STACK, j % 8, q * P:(q + 1) * P], stacks[s][:, half * 8 + q, h, :],
                                                   c.identb[:, :])
                    last.then_inc(c.transposed, 1)
        c.clear()


MAX_JOBS = GH * 4 * BLKS
MAX_BANK = 5
MAX_RING = 3
MAX_LEAD = 3
TURN_BANK = 6


class Maxima:

    def __init__(self, c, mem, qs, ks, b):
        self.c, self.qs, self.ks, self.b = c, qs, ks, b
        self.best = c.sb(mem, "r_best", [P, MAX_JOBS])
        self.neg = c.sb(mem, "r_neg", [P, GH * 4])
        self.parts = c.sb(mem, "r_parts", [P, GH * 4, 4], BF16)

    def multiply(self, pe, m):
        c = self.c
        h, i, kb = m // 16, m // 4 % 4, m % 4
        if m >= MAX_RING:
            pe.wait_ge(c.reduced, m - MAX_RING + 1)
        c.nc.tensor.matmul(c.psum[:, MAX_BANK + m % MAX_RING, :], self.qs[0:STACK, h, bass.ds(self.b * BLK + i * P, P)],
                           self.ks[0:STACK, h, kb * BLK:(kb + 1) * BLK], start=True, stop=True).then_inc(c.scored, 1)

    def reduce(self, dve, m):
        c = self.c
        dve.wait_ge(c.scored, m + 1)
        c.nc.vector.tensor_reduce(self.best[:, m:m + 1], c.psum[:, MAX_BANK + m % MAX_RING, :], AX, ALU.max).then_inc(c.reduced, 1)

    def multiply_row(self, pe, r):
        c = self.c
        if r >= 2:
            pe.wait_ge(c.reduced, r - 1)
        for kb in range(BLKS):
            last = c.nc.tensor.matmul(c.psum[:, 4 * (r % 2) + kb, :], self.qs[0:STACK, r // 4, bass.ds(self.b * BLK + r % 4 * P, P)],
                                      self.ks[0:STACK, r // 4, kb * BLK:(kb + 1) * BLK], start=True, stop=True)
        last.then_inc(c.scored, 1)

    def reduce_row(self, dve, r):
        c = self.c
        dve.wait_ge(c.scored, r + 1)
        c.nc.vector.tensor_reduce(self.best[:, r:r + 1], c.psum[:, 4 * (r % 2):4 * (r % 2) + 4, :].rearrange("p b f -> p (b f)"),
                                  AX, ALU.max).then_inc(c.reduced, 1)

    def split(self, dve, jobs=MAX_JOBS):
        c, nc = self.c, self.c.nc
        dve.wait_ge(c.reduced, jobs)
        step = Chain(dve, c.stepped)
        if jobs == MAX_JOBS:
            step(nc.vector.tensor_reduce(self.neg[:, :], self.best[:, :].rearrange("p (m k) -> p m k", k=BLKS), AX, ALU.max,
                                         negate=True))
        else:
            step(nc.vector.tensor_scalar(self.neg[:, :], self.best[:, 0:jobs], -1.0, None, ALU.mult))
        for n in range(3):
            step(nc.vector.tensor_copy(self.parts[:, :, n], self.neg[:, :]))
            if n < 2:
                step(nc.vector.tensor_tensor(self.neg[:, :], self.neg[:, :], self.parts[:, :, n], ALU.subtract))

    SPLIT_STEPS = 6

    def turn(self, pe):
        c = self.c
        bf = banks_bf16(c)
        pe.wait_ge(c.stepped, self.SPLIT_STEPS)
        for m in range(GH * 4):
            last = c.nc.tensor.transpose(bf[STACK:STACK + 3, TURN_BANK + m // 8, m % 8 * P:(m % 8 + 1) * P],
                                         self.parts[:, m, 0:3], c.identb[:, :])
        last.then_inc(c.turned, 1)

    def place(self, act):
        c = self.c
        bf = banks_bf16(c)
        act.wait_ge(c.turned, 1)
        for two in range(2):
            c.nc.scalar.activation(self.qs[STACK:STACK + 3, 2 * two:2 * two + 2, bass.ds(self.b * BLK, BLK)],
                                   bf[STACK:STACK + 3, TURN_BANK + two, :].rearrange("p (h f) -> p h f", f=BLK), ACT.Copy)


def first_maxima(c, qs, ks):
    with ExitStack() as mem:
        maxima = Maxima(c, mem, qs, ks, 0)
        with c.nc.Block() as block:
            @block.tensor
            def _(pe):
                for r in range(GH * 4):
                    maxima.multiply_row(pe, r)
                maxima.turn(pe)

            @block.vector
            def _(dve):
                for r in range(GH * 4):
                    maxima.reduce_row(dve, r)
                maxima.split(dve, GH * 4)

            @block.scalar
            def _(act):
                maxima.place(act)
        c.clear()


def attend(c, qs, ks, v4, oT, g, b, last_block=False):
    nc = c.nc
    jobs, rows = 2 * TILES, STACK + 3
    due = [min(MAX_JOBS, MAX_JOBS * n // (jobs - MAX_LEAD)) for n in range(jobs + 1)]
    with ExitStack() as mem:
        probs = c.sb(mem, "t_probs", [P, 3, 2 * BLK])
        maxima = None if last_block else Maxima(c, mem, qs, ks, b + 1)
        ring = 3 if last_block else 2
        out = 2 * ring
        with nc.Block() as block:
            @block.tensor
            def _(pe):
                def scores(n):
                    for two in range(2):
                        h = 2 * (n % 2) + two
                        last = nc.tensor.matmul(c.psum[:, 2 * (n % ring) + two, :], ks[0:rows, h, n // 2 * P:(n // 2 + 1) * P],
                                                qs[0:rows, h, bass.ds(b * BLK, BLK)], start=True, stop=True)
                    last.then_inc(c.multiplied, 1)

                for n in range(ring):
                    scores(n)
                for n in range(jobs):
                    pe.wait_ge(c.activated, n + 1)
                    if n + ring < jobs:
                        scores(n + ring)
                    if maxima:
                        for m in range(due[n], due[n + 1]):
                            maxima.multiply(pe, m)
                        if n == jobs - 1:
                            maxima.turn(pe)
                    for two in range(2):
                        h = 2 * (n % 2) + two
                        last = nc.tensor.matmul(c.psum[32 * h:32 * h + 32, out, :], v4[:, n // 2, h, :],
                                                probs[:, n % 3, two * BLK:(two + 1) * BLK],
                                                start=(n < 2), stop=(n >= jobs - 2))
                    last.then_inc(c.copied, 1)

            @block.scalar
            def _(act):
                for n in range(jobs):
                    act.wait_ge(c.multiplied, n + 1)
                    if n >= 3:
                        act.wait_ge(c.copied, n - 2)
                    pair = c.psum[:, 2 * (n % ring):2 * (n % ring) + 2, :].rearrange("p a f -> p (a f)")
                    nc.scalar.activation(probs[:, n % 3, :], pair, ACT.Exp, scale=float(HD) ** -0.5).then_inc(c.activated, 1)
                if maxima:
                    maxima.place(act)

            @block.vector
            def _(dve):
                if maxima:
                    for m in range(MAX_JOBS):
                        maxima.reduce(dve, m)
                    maxima.split(dve)
                dve.wait_ge(c.copied, jobs)
                nc.vector.tensor_copy(oT[:, bass.ds(g, 1), bass.ds(b * BLK, BLK)].rearrange("p a f -> p (a f)"),
                                      c.psum[:, out, :])
        c.clear()


def split_weights(c, a, wh, descale):
    nc = c.nc
    with ExitStack() as mem:
        raw = c.sb(mem, "w_raw", [P, 2, EXPERTS, KT, GATES])
        most = c.sb(mem, "w_most", [P, 2])
        size = c.sb(mem, "w_size", [P, 2])
        scale = c.sb(mem, "w_scale", [P, 2])
        with nc.Block() as block:
            @block.sync
            def _(sp):
                for d, sem in ((0, c.loaded), (1, c.loaded_odd)):
                    for e in range(EXPERTS):
                        sp.dma_start(raw[:, d, e, :, :], a["lstm_wh_" + "fb"[d]][e]).then_inc(sem, 16)

            @block.vector
            def _(dve):
                step = Chain(dve, c.stepped)
                for d, sem in ((0, c.loaded), (1, c.loaded_odd)):
                    w = raw[:, d, :, :, :].rearrange("p e k n -> p (e k n)")
                    hi, lo = (wh[:, part, d, :, :, :].rearrange("p e k n -> p (e k n)") for part in range(2))
                    dve.wait_ge(sem, 16 * EXPERTS)
                    step(nc.vector.tensor_reduce(most[:, d:d + 1], w, AX, ALU.max, apply_absolute_value=True))
                    nc.vector.tensor_scalar(most[:, d:d + 1], most[:, d:d + 1], 1e-30, None, ALU.max).then_inc(c.vectored, 1)
                    dve.wait_ge(c.pooled, d + 1)
                    s = size[:, d:d + 1]
                    step(nc.vector.tensor_scalar(s.bitcast(I32), s.bitcast(I32), 0x7F800000, None, ALU.bitwise_and))
                    step(nc.vector.reciprocal(scale[:, d:d + 1], s))
                    step(nc.vector.tensor_scalar(scale[:, d:d + 1], scale[:, d:d + 1], FULL, None, ALU.mult))
                    step(nc.vector.tensor_scalar(hi, w, scale[:, d:d + 1], None, ALU.mult))
                    step(nc.vector.scalar_tensor_tensor(out=lo, in0=w, scalar=scale[:, d:d + 1], in1=hi,
                                                        op0=ALU.mult, op1=ALU.subtract))
                    step(nc.vector.tensor_scalar(descale[:, d:d + 1], s, FULL ** -2, None, ALU.mult))

            @block.gpsimd
            def _(pool):
                for d in range(2):
                    pool.wait_ge(c.vectored, d + 1)
                    nc.gpsimd.partition_all_reduce(size[:, d:d + 1], most[:, d:d + 1], P,
                                                   bass.bass_isa.ReduceOp.max).then_inc(c.pooled, 1)
        c.clear()


def lstms(c, a, zx, hist):
    nc = c.nc
    steps = T
    with ExitStack() as mem:
        wh = c.sb(mem, "l_wh", [P, 2, 2, EXPERTS, KT, GATES], F16)
        descale = c.sb(mem, "l_descale", [P, 2])
        split_weights(c, a, wh, descale)
        state = c.sb(mem, "l_state", [P, 2, UNITS, 2], F16)
        xin = c.sb(mem, "l_xin", [P, 2, 2, MT * EXPERTS, CH])
        both = c.sb(mem, "l_both", [P, 2, MT * EXPERTS])
        z = c.sb(mem, "l_z", [P, 2, MT * EXPERTS])
        gates = c.sb(mem, "l_gates", [P, 2, MT * EXPERTS])
        cell = c.sb(mem, "l_cell", [P, 2, UNITS])
        kept = c.sb(mem, "l_kept", [P, 2, UNITS])
        fresh = c.sb(mem, "l_fresh", [P, 2, UNITS])
        opened = c.sb(mem, "l_opened", [P, 2, UNITS])
        squashed = c.sb(mem, "l_squashed", [P, 2, UNITS])
        h = c.sb(mem, "l_h", [P, 2, UNITS])
        past = c.sb(mem, "l_past", [P, 2, 2, UNITS, SUPER])
        sems = {}
        for what in ("summed", "z_made", "gated", "cell_made", "squashed", "state_made", "kept"):
            sems[what] = [nc.alloc_semaphore(f"{what}_{d}") for d in range(2)]
        dve_step = [nc.alloc_semaphore(f"products_{d}") for d in range(2)]
        xin_in = [[nc.alloc_semaphore(f"xin_{d}_{q}") for q in range(2)] for d in range(2)]
        past_out = [nc.alloc_semaphore(f"past_{q}") for q in range(2)]
        chunks = nc.alloc_semaphore("chunks_begun")

        with nc.Block() as block:
            @block.vector
            def _(dve):
                nc.vector.memset(state[:, :, :, :], 0.0)
                nc.vector.memset(cell[:, :, :], 0.0)
                nc.vector.memset(h[:, :, :], 0.0)
                for d in range(2):
                    dve.sem_inc(sems["summed"][d], 2 * CH)
                    dve.sem_inc(sems["kept"][d], 1)
                    dve.sem_inc(sems["state_made"][d], 1)

        with nc.Block() as block:
            @block.sync
            def _(sp):
                with sp.Fori(0, steps // (2 * CH)) as pair:
                    for q in range(2):
                        for d in range(2):
                            at = pair * (2 * CH) + q * CH
                            sp.wait_ge(sems["summed"][d], at + CH)
                            sp.sem_inc(chunks, 1)
                            first = at if d == 0 else at * (-1) + (steps - CH)
                            sp.dma_start(xin[:, d, q, :, :],
                                         zx[d][:, :, :, bass.ds(first, CH)].rearrange("p m e t -> p (m e) t")
                                         ).then_inc(xin_in[d][q], 16)

            @block.tensor
            def _(pe):
                with pe.Fori(0, steps) as s:
                    for d in range(2):
                        pe.wait_ge(sems["state_made"][d], s + 1)
                        for e in range(EXPERTS):
                            for m in range(MT):
                                at = (m * EXPERTS + e) * 2
                                for k, part in ((0, 0), (0, 1), (1, 0), (1, 1)):
                                    last = nc.tensor.matmul(c.psum[:, d, at:at + 2], wh[:, part, d, e, k, m * P:(m + 1) * P],
                                                            state[:, d, k * EXPERTS + e, :],
                                                            start=((k, part) == (0, 0)), stop=((k, part) == (1, 1)))
                        last.then_inc(sems["z_made"][d], 1)

            @block.scalar
            def _(act):
                nc.scalar.activation(squashed[:, :, :], h[:, :, :], ACT.Sigmoid)
                with act.Fori(0, steps) as s:
                    for d in range(2):
                        act.wait_ge(sems["summed"][d], s + (2 * CH + 1))
                        nc.scalar.activation(gates[:, d, 0:3 * UNITS], z[:, d, 0:3 * UNITS], ACT.Sigmoid).then_inc(sems["gated"][d], 1)
                        nc.scalar.activation(gates[:, d, 3 * UNITS:], z[:, d, 3 * UNITS:], ACT.Tanh).then_inc(sems["gated"][d], 1)
                        act.wait_ge(sems["cell_made"][d], s + 1)
                        nc.scalar.activation(squashed[:, d, :], cell[:, d, :], ACT.Tanh).then_inc(sems["squashed"][d], 1)

            @block.vector
            def _(dve):
                def gate(d, n):
                    return gates[:, d, n * UNITS:(n + 1) * UNITS]

                OWN = 5
                with dve.Fori(0, steps // (2 * CH)) as pair:
                    for q in range(2):
                        for d in range(2):
                            dve.wait_ge(xin_in[d][q], pair * 16 + 16)
                        dve.sem_inc(chunks, 1)
                        with dve.Fori(0, CH) as r:
                            s = pair * (2 * CH) + (r + q * CH)
                            for d in range(2):
                                at = r if d == 0 else r * (-1) + (CH - 1)
                                parts = c.psum[:, d, 0:MT * EXPERTS * 2].rearrange("p (n f) -> p n f", f=2)
                                dve.wait_ge(sems["z_made"][d], s + 1)
                                nc.vector.tensor_reduce(both[:, d, :], parts, AX, ALU.add).then_inc(dve_step[d], 1)
                                dve.wait_ge(dve_step[d], s * OWN + 1)
                                nc.vector.scalar_tensor_tensor(out=z[:, d, :], in0=both[:, d, :], scalar=descale[:, d:d + 1],
                                                               in1=xin[:, d, q, :, bass.ds(at, 1)].rearrange("p n a -> p (n a)"),
                                                               op0=ALU.mult, op1=ALU.add).then_inc(sems["summed"][d], 1)
                                dve.wait_ge(sems["gated"][d], s * 2 + 1)
                                nc.vector.tensor_tensor(kept[:, d, :], gate(d, 1), cell[:, d, :], ALU.mult).then_inc(dve_step[d], 1)
                                dve.wait_ge(sems["gated"][d], s * 2 + 2)
                                nc.vector.tensor_tensor(fresh[:, d, :], gate(d, 0), gate(d, 3), ALU.mult).then_inc(dve_step[d], 1)
                                dve.wait_ge(dve_step[d], s * OWN + 3)
                                nc.vector.tensor_tensor(cell[:, d, :], kept[:, d, :], fresh[:, d, :], ALU.add).then_inc(sems["cell_made"][d], 1)
                                nc.vector.tensor_scalar(opened[:, d, :], gate(d, 2), FULL, None, ALU.mult).then_inc(dve_step[d], 1)
                                dve.wait_ge(dve_step[d], s * OWN + 4)
                                dve.wait_ge(sems["squashed"][d], s + 1)
                                nc.vector.tensor_tensor(state[:, d, :, 0], opened[:, d, :], squashed[:, d, :], ALU.mult)
                                dve.wait_ge(sems["kept"][d], s + 1)
                                nc.vector.tensor_tensor(h[:, d, :], opened[:, d, :], squashed[:, d, :], ALU.mult).then_inc(dve_step[d], 1)
                                dve.wait_ge(dve_step[d], s * OWN + 5)
                                nc.vector.tensor_tensor(state[:, d, :, 1], h[:, d, :], state[:, d, :, 0],
                                                        ALU.subtract).then_inc(sems["state_made"][d], 1)

            @block.gpsimd
            def _(pool):
                def chunk(big, q, first):
                    if not first:
                        pool.wait_ge(past_out[q], big * 64)
                        pool.sem_inc(chunks, 1)
                    with pool.Fori(0, SUPER) as r:
                        s = big * (2 * SUPER) + (r + q * SUPER)
                        for d in range(2):
                            at = r if d == 0 else r * (-1) + (SUPER - 1)
                            pool.wait_ge(sems["state_made"][d], s + 2)
                            nc.gpsimd.tensor_copy(past[:, d, q, :, bass.ds(at, 1)].rearrange("p n a -> p (n a)"),
                                                  h[:, d, :]).then_inc(sems["kept"][d], 1)
                    for d in range(2):
                        at = big * (2 * SUPER) + q * SUPER
                        t0 = at if d == 0 else at * (-1) + (steps - SUPER)
                        pool.wait_ge(sems["kept"][d], at + (SUPER + 1))
                        for k in range(KT):
                            nc.gpsimd.dma_start(hist[:, d, k, :, bass.ds(t0, SUPER)].rearrange("e p t -> p e t"),
                                                past[:, d, q, k * EXPERTS:(k + 1) * EXPERTS, :]).then_inc(past_out[q], 16)

                rounds = steps // (2 * SUPER)
                chunk(0, 0, True)
                chunk(0, 1, True)
                with pool.Fori(1, rounds) as big:
                    chunk(big, 0, False)
                    chunk(big, 1, False)
                for q in range(2):
                    pool.wait_ge(past_out[q], rounds * 64)


def expert_back(c, a, e, hist, router):
    nc = c.nc
    with ExitStack() as mem:
        past = c.sb(mem, "b_past", [P, 2, KT, T])
        hid, gate, other = (c.sb(mem, n, [P, KT, T]) for n in ("b_hid", "b_gate", "b_other"))
        w1, w2 = c.sb(mem, "b_w1", [P, 2 * KT, W]), c.sb(mem, "b_w2", [P, KT, W])
        b1, b2 = c.sb(mem, "b_b1", [P, KT]), c.sb(mem, "b_b2", [P, KT])
        wd, rows = c.sb(mem, "b_wd", [P, KT, D]), c.sb(mem, "b_rows", [P, 3, D])

        def layer(src, w, kt, out, func, b, loads, scale=1.0):
            dense_features(c, lambda k, n: src(k)[:, n * BLK:(n + 1) * BLK], lambda k, m: w[:, k, m * P:(m + 1) * P], kt, KT,
                           lambda m, n: out[:, m, n * BLK:(n + 1) * BLK], func, bias=lambda m: b[:, m:m + 1], loads=loads,
                           scale=scale)

        first = [(past[:, d, k, :], hist[e, d, k, :, :]) for d in range(2) for k in range(KT)]
        for kind, func, out in (("sig", ACT.Sigmoid, gate), ("tan", ACT.Tanh, other)):
            layer(lambda k: past[:, k // KT, k % KT, :], w1, 2 * KT, hid, ACT.Relu, b1,
                  first + [(w1[:, :, :], a[kind + "_w1"][e]), (b1[:, :], a[kind + "_b1"][e]),
                           (w2[:, :, :], a[kind + "_w2"][e]), (b2[:, :], a[kind + "_b2"][e])],
                  scale=1 / FULL)
            layer(lambda k: hid[:, k, :], w2, KT, out, func, b2, [])
            first = []
        with nc.Block() as block:
            @block.vector
            def _(dve):
                nc.vector.tensor_tensor(gate[:, :, :], gate[:, :, :], other[:, :, :], ALU.mult)
        layer(lambda k: gate[:, k, :], w2, KT, hid, ACT.Relu, b1,
              [(w2[:, :, :], a["dec_w1"][e]), (b1[:, :], a["dec_b1"][e]), (wd[:, :, :], a["dec_w2"][e])]
              + [(rows[:, j, :], wide(a[n][e])) for j, n in enumerate(("dec_b2", "dec_g", "dec_beta"))])
        y = other[:, 0, :].rearrange("p (i d) -> p i d", d=D)
        dense_tokens(c, lambda k, i: hid[:, k, i * P:(i + 1) * P], lambda k, n: wd[:, k, :], KT, [D],
                     lambda i, n: y[:, i, :], plus=lambda i, n: rows[:, 0, :])
        normalize(c, y, y, TILES, D, gamma=rows[:, 1, :], beta=rows[:, 2, :])
        with nc.Block() as block:
            @block.vector
            def _(dve):
                step = Chain(dve, c.stepped)
                step(nc.vector.tensor_tensor(y, y, router[:, :, bass.ds(e, 1)].to_broadcast([P, TILES, D]), ALU.mult))
                step(nc.vector.tensor_tensor(c.x[:, :, :], c.x[:, :, :], y, ALU.add))
        c.clear()


def layer1_experts(c, a, zx, hist):
    nc = c.nc
    with ExitStack() as mem:
        router = c.sb(mem, "e_router", [P, TILES, EXPERTS])
        with ExitStack() as m1:
            xT = c.sb(m1, "e_xT", [P, T])
            rw, rb = c.sb(m1, "e_router_w", [P, EXPERTS]), c.sb(m1, "e_router_b", [P, EXPERTS])
            total = c.sb(m1, "e_total", [P, TILES])
            with ExitStack() as m2:
                xn = c.sb(m2, "e_xn", [P, TILES, D])
                normalize(c, c.x[:, :, :], xn[:, :, :], TILES, D)
                transpose_tiles(c, [([xn[:, 4 * b + q, :] for q in range(4)], xT[:, b * BLK:(b + 1) * BLK]) for b in range(BLKS)])
            dense_tokens(c, lambda k, i: xT[:, i * P:(i + 1) * P], lambda k, n: rw[:, :], 1, [EXPERTS],
                         lambda i, n: router[:, i, :], plus=lambda i, n: rb[:, :],
                         loads=[(rw[:, :], a["router_w"]), (rb[:, :], wide(a["router_b"]))])
            with nc.Block() as block:
                def each(ap):
                    return ap.unsqueeze(2).to_broadcast([P, TILES, EXPERTS])

                @block.vector
                def _(dve):
                    step = Chain(dve, c.stepped)
                    step(nc.vector.tensor_reduce(total[:, :], router[:, :, :], AX, ALU.max))
                    step(nc.vector.tensor_tensor(router[:, :, :], router[:, :, :], each(total[:, :]), ALU.subtract))
                    dve.wait_ge(c.activated, 1)
                    step(nc.vector.tensor_reduce(total[:, :], router[:, :, :], AX, ALU.add))
                    step(nc.vector.reciprocal(total[:, :], total[:, :]))
                    step(nc.vector.tensor_tensor(router[:, :, :], router[:, :, :], each(total[:, :]), ALU.mult))

                @block.scalar
                def _(act):
                    act.wait_ge(c.stepped, 2)
                    nc.scalar.activation(router[:, :, :], router[:, :, :], ACT.Exp).then_inc(c.activated, 1)
            c.clear()
            with nc.Fori(0, EXPERTS) as e:
                expert_front(c, a, e, xT, zx)
        lstms(c, a, zx, hist)
        with nc.Fori(0, EXPERTS) as e:
            expert_back(c, a, e, hist, router)


def program(nc, a):
    with ExitStack() as ctx:
        c = Core(nc, ctx)
        zx = [nc.dram_tensor(f"projections_{d}", (P, MT, EXPERTS, T), F32).ap() for d in range(2)]
        hist = nc.dram_tensor("hidden_states", (EXPERTS, 2, KT, P, T), F32).ap()
        constants(c)
        gather(c, a["ids"], a["L0_tok_w"])
        layer0_attention(c, a["L0_attn_w_qkv"], a["L0_attn_w_proj"])
        moe(c, *(a["L0_ffn_" + n] for n in ("gate_w", "w1", "w3", "w2", "sw1", "sw3", "sw2")))
        layer1_attention(c, a)
        layer1_experts(c, {n[len("L1_ffn_"):]: v for n, v in a.items() if n.startswith("L1_ffn_")}, zx, hist)
        with nc.Block() as block:
            @block.sync
            def _(sp):
                sp.dma_start(a["out"].rearrange("a (i p) d -> p (a i) d", p=P), c.x[:, :, :]).then_inc(c.stored, 16)
                sp.wait_ge(c.stored, 16)


def lay_out(inputs):
    o = {}
    v = {n: np.asarray(x) for n, x in inputs.items()}
    o["ids"] = v["x"].reshape(TILES, P).T
    o["L0_tok_w"] = v["L0_tok_w"]
    o["L0_attn_w_qkv"] = v["L0_attn_w_qkv"].reshape(D, HEADS, 3, HD).transpose(0, 2, 1, 3).reshape(D, 3 * D)
    o["L0_attn_w_proj"] = v["L0_attn_w_proj"]
    o["L0_ffn_gate_w"] = v["L0_ffn_gate_w"].T
    for n in ("w1", "w3", "w2", "sw1", "sw3", "sw2"):
        o["L0_ffn_" + n] = v["L0_ffn_" + n]
    l = "L1_attn_"
    o[l + "conv_w"] = v[l + "conv_w"].transpose(1, 2, 0)
    o[l + "conv_b"] = v[l + "conv_b"].reshape(P, 1)
    o[l + "in_proj_w"] = v[l + "in_proj_w"].T
    o[l + "qk_b"] = v[l + "in_proj_b"][:2 * D].reshape(2, P).T
    o[l + "v_b"] = v[l + "in_proj_b"][2 * D:]
    o[l + "out_proj_w"] = v[l + "out_proj_w"].T
    o[l + "w1"] = v[l + "w1"].T
    o[l + "b1"] = v[l + "b1"].reshape(2, P).T
    o[l + "w2"] = v[l + "w2"].T.reshape(2, P, D).transpose(1, 0, 2)
    for n in ("out_proj_b", "b2", "ln1_g", "ln1_b", "ln2_g", "ln2_b"):
        o[l + n] = v[l + n]
    l = "L1_ffn_"
    for n in ("router_w", "router_b", "enc_w1", "enc_b2", "enc_g", "enc_beta", "attn_in_b", "dec_b2", "dec_g", "dec_beta"):
        o[l + n] = v[l + n]
    for n in ("enc_w2", "attn_in_w", "sig_w1", "sig_w2", "tan_w1", "tan_w2", "dec_w1", "dec_w2"):
        w = v[l + n]
        o[l + n] = w.reshape(EXPERTS, -1, P, w.shape[2]).transpose(0, 2, 1, 3)
    for n in ("enc_b1", "attn_out_b", "sig_b1", "sig_b2", "tan_b1", "tan_b2", "dec_b1"):
        o[l + n] = v[l + n].reshape(EXPERTS, KT, P).transpose(0, 2, 1)
    o[l + "attn_out_w"] = v[l + "attn_out_w"].reshape(EXPERTS, GROUPS, GH, HD, W)
    order = [0, 1, 3, 2]
    for way in "fb":
        for kind in ("wi_", "wh_"):
            w = v[l + "lstm_" + kind + way].reshape(EXPERTS, KT, P, 4, W)[:, :, :, order]
            o[l + "lstm_" + kind + way] = w.transpose(0, 2, 1, 3, 4).reshape(EXPERTS, P, KT, GATES)
        b = v[l + "lstm_b_" + way].reshape(EXPERTS, 4, W)[:, order]
        o[l + "lstm_b_" + way] = b.reshape(EXPERTS, MT, P).transpose(0, 2, 1)
    return {n: np.ascontiguousarray(x) for n, x in o.items()}


def kernel(**inputs):
    import concourse.bacc as bacc
    from concourse.bass_utils import run_bass_kernel_spmd

    nc = bacc.Bacc("TRN2", target_bir_lowering=False, num_devices=1)
    arrays = {f"in_{n}": x for n, x in lay_out(inputs).items()}
    aps = {n[len("in_"):]: nc.dram_tensor(n, x.shape, mybir.dt.from_np(x.dtype), kind="ExternalInput").ap()
           for n, x in arrays.items()}
    aps["out"] = nc.dram_tensor("out_hidden", (1, T, D), F32, kind="ExternalOutput").ap()
    program(nc, aps)
    result = run_bass_kernel_spmd(nc, [arrays], core_ids=[0])
    return result.results[0]["out_hidden"]
```

```python
import numpy as np
from contextlib import ExitStack

import concourse.bass as bass
from concourse import mybir
from concourse.alu_op_type import AluOpType as ALU

F32 = mybir.dt.float32
BF16 = mybir.dt.bfloat16
F16 = mybir.dt.float16
I32 = mybir.dt.int32
ACT = mybir.ActivationFunctionType
AX = mybir.AxisListType.X

P = 128
T = 2048
D = 128
TILES = T // P
BLK = 512
BLKS = T // BLK
EPS = 1e-5
NEG = -1e30
HEADS = 8
HD = D // HEADS


class Core:

    def __init__(self, nc, ctx):
        self.nc = nc
        self.loaded = nc.alloc_semaphore("loaded")
        self.loaded_odd = nc.alloc_semaphore("loaded_odd")
        self.stored = nc.alloc_semaphore("stored")
        self.multiplied = nc.alloc_semaphore("multiplied")
        self.evacuated = nc.alloc_semaphore("evacuated")
        self.activated = nc.alloc_semaphore("activated")
        self.stepped = nc.alloc_semaphore("stepped")
        self.vectored = nc.alloc_semaphore("vectored")
        self.transposed = nc.alloc_semaphore("transposed")
        self.copied = nc.alloc_semaphore("copied")
        self.scored = nc.alloc_semaphore("scored")
        self.reduced = nc.alloc_semaphore("reduced")
        self.turned = nc.alloc_semaphore("turned")
        self.pooled = nc.alloc_semaphore("pooled")
        self.gathered = nc.alloc_semaphore("gathered")
        self.first, self.last = self.loaded.num, self.pooled.num
        self.count = 0
        self.psum = ctx.enter_context(nc.psum_tensor("banks", [P, 8, BLK], F32))
        self.ident = ctx.enter_context(nc.sbuf_tensor("ident", [P, P], F32))
        self.identb = ctx.enter_context(nc.sbuf_tensor("identb", [P, P], BF16))
        self.headmask = ctx.enter_context(nc.sbuf_tensor("headmask", [P, HEADS], F32))
        self.x = ctx.enter_context(nc.sbuf_tensor("x_resid", [P, TILES, D], F32))

    def sb(self, mem, name, shape, dtype=F32):
        self.count += 1
        return mem.enter_context(self.nc.sbuf_tensor(f"{name}_{self.count}", shape, dtype))

    def clear(self):
        with self.nc.Block() as block:
            @block.vector
            def _(dve):
                dve.sem_clear(range(self.first, self.last + 1))


class Chain:

    def __init__(self, eng, sem):
        self.eng, self.sem, self.n = eng, sem, 0

    def __call__(self, ins):
        self.n += 1
        ins.then_inc(self.sem, 1)
        self.eng.wait_ge(self.sem, self.n)


def constants(c):
    nc = c.nc
    with nc.Block() as block:
        @block.gpsimd
        def _(pool):
            step = Chain(pool, c.pooled)
            step(nc.gpsimd.memset(c.ident[:, :], 0.0))
            step(nc.gpsimd.affine_select(out=c.ident[:, :], in_=c.ident[:, :], compare_op=ALU.not_equal,
                                         fill=1.0, base=0, pattern=[[-1, P]], channel_multiplier=1))
            step(nc.gpsimd.memset(c.identb[:, :], 0.0))
            step(nc.gpsimd.affine_select(out=c.identb[:, :], in_=c.identb[:, :], compare_op=ALU.not_equal,
                                         fill=1.0, base=0, pattern=[[-1, P]], channel_multiplier=1))
            step(nc.gpsimd.memset(c.headmask[:, :], 1.0))
            step(nc.gpsimd.affine_select(out=c.headmask[:, :], in_=c.headmask[:, :], compare_op=ALU.is_ge,
                                         fill=0.0, base=0, pattern=[[-HD, HEADS]], channel_multiplier=1))
            step(nc.gpsimd.affine_select(out=c.headmask[:, :], in_=c.headmask[:, :], compare_op=ALU.is_ge,
                                         fill=0.0, base=HD - 1, pattern=[[HD, HEADS]], channel_multiplier=-1))
    c.clear()


def gather(c, ids, table):
    nc = c.nc
    with nc.sbuf_tensor("token_ids", [P, TILES], I32) as idx, nc.Block() as block:
        @block.gpsimd
        def _(pool):
            nc.gpsimd.dma_start(idx[:, :], ids).then_inc(c.gathered, 16)
            pool.wait_ge(c.gathered, 16)
            for i in range(TILES):
                nc.gpsimd.indirect_dma_start(
                    out=c.x[:, i, :], out_offset=None, in_=table,
                    in_offset=bass.IndirectOffsetOnAxis(ap=idx[:, i:i + 1], axis=0),
                ).then_inc(c.gathered, 16)
            pool.wait_ge(c.gathered, 16 * (TILES + 1))


def normalize(c, src, dst, n, width, gamma=None, beta=None, loads=(), plus=None, residual=None):
    nc = c.nc
    with ExitStack() as mem:
        sq = c.sb(mem, "ln_squares", [P, n, width])
        mean = c.sb(mem, "ln_mean", [P, n])
        var = c.sb(mem, "ln_var", [P, n])
        std = c.sb(mem, "ln_std", [P, n])
        block = mem.enter_context(nc.Block())

        def wide(ap):
            return ap.unsqueeze(2).to_broadcast([P, n, width])

        def row(ap):
            return ap.unsqueeze(1).to_broadcast([P, n, width])

        @block.sync
        def _(sp):
            for to, frm in loads:
                sp.dma_start(to, frm).then_inc(c.loaded, 16)
            if loads:
                sp.wait_ge(c.loaded, 16 * len(loads))

        @block.vector
        def _(dve):
            step = Chain(dve, c.stepped)
            inp = src
            if plus is not None:
                step(nc.vector.tensor_tensor(dst, src, plus, ALU.add))
                inp = dst
            step(nc.vector.tensor_reduce(mean[:, :], inp, AX, ALU.add))
            step(nc.vector.tensor_scalar(mean[:, :], mean[:, :], 1.0 / width, None, ALU.mult))
            step(nc.vector.tensor_tensor(dst, inp, wide(mean[:, :]), ALU.subtract))
            step(nc.vector.tensor_tensor(sq[:, :, :], dst, dst, ALU.mult))
            step(nc.vector.tensor_reduce(var[:, :], sq[:, :, :], AX, ALU.add))
            nc.vector.tensor_scalar(var[:, :], var[:, :], 1.0 / width, EPS, ALU.mult, ALU.add).then_inc(c.vectored, 1)
            dve.wait_ge(c.activated, 1)
            step(nc.vector.reciprocal(std[:, :], std[:, :]))
            step(nc.vector.tensor_tensor(dst, dst, wide(std[:, :]), ALU.mult))
            if gamma is not None:
                step(nc.vector.tensor_tensor(dst, dst, row(gamma), ALU.mult))
                step(nc.vector.tensor_tensor(dst, dst, row(beta), ALU.add))
            if residual is not None:
                step(nc.vector.tensor_tensor(residual, residual, dst, ALU.add))

        @block.scalar
        def _(act):
            act.wait_ge(c.vectored, 1)
            nc.scalar.activation(std[:, :], var[:, :], ACT.Sqrt).then_inc(c.activated, 1)
    c.clear()


def transpose_tiles(c, tiles):
    nc = c.nc
    with nc.Block() as block:
        @block.tensor
        def _(pe):
            for j, (sources, _) in enumerate(tiles):
                if j >= 8:
                    pe.wait_ge(c.evacuated, j - 7)
                for q, source in enumerate(sources):
                    last = nc.tensor.transpose(c.psum[:, j % 8, q * P:(q + 1) * P], source, c.ident[:, :])
                last.then_inc(c.transposed, 1)

        @block.scalar
        def _(act):
            for j, (sources, target) in enumerate(tiles):
                act.wait_ge(c.transposed, j + 1)
                nc.scalar.activation(target, c.psum[:, j % 8, :len(sources) * P], ACT.Copy).then_inc(c.evacuated, 1)
    c.clear()


def dense_features(c, xT, w, kt, mt, out, func, bias=None, loads=(), m_size=P, scale=1.0,
                   later=()):
    nc = c.nc
    jobs = [(m, b) for m in range(mt) for b in range(BLKS)]
    with nc.Block() as block:
        @block.sync
        def _(sp):
            for to, frm in loads:
                sp.dma_start(to, frm).then_inc(c.loaded, 16)
            for to, frm in later:
                sp.dma_start(to, frm).then_inc(c.loaded_odd, 16)
            if later:
                sp.wait_ge(c.loaded_odd, 16 * len(later))

        @block.tensor
        def _(pe):
            if loads:
                pe.wait_ge(c.loaded, 16 * len(loads))
            for j, (m, b) in enumerate(jobs):
                if j >= 8:
                    pe.wait_ge(c.evacuated, j - 7)
                for k in range(kt):
                    last = nc.tensor.matmul(c.psum[0:m_size, j % 8, :], w(k, m), xT(k, b),
                                            start=(k == 0), stop=(k == kt - 1))
                last.then_inc(c.multiplied, 1)

        @block.scalar
        def _(act):
            if loads:
                act.wait_ge(c.loaded, 16 * len(loads))
            for j, (m, b) in enumerate(jobs):
                act.wait_ge(c.multiplied, j + 1)
                if bias is None:
                    ins = nc.scalar.activation(out(m, b), c.psum[0:m_size, j % 8, :], func, scale=scale)
                else:
                    ins = nc.scalar.activation(out(m, b), c.psum[0:m_size, j % 8, :], func, bias=bias(m), scale=scale)
                ins.then_inc(c.evacuated, 1)
    c.clear()


def dense_tokens(c, xT, w, kt, cols, out, plus=None, loads=(), scale=None):
    nc = c.nc
    jobs = [(i, n) for i in range(TILES) for n in range(len(cols))]
    with nc.Block() as block:
        @block.sync
        def _(sp):
            for to, frm in loads:
                sp.dma_start(to, frm).then_inc(c.loaded, 16)

        @block.tensor
        def _(pe):
            if loads:
                pe.wait_ge(c.loaded, 16 * len(loads))
            for j, (i, n) in enumerate(jobs):
                if j >= 8:
                    pe.wait_ge(c.evacuated, j - 7)
                for k in range(kt):
                    last = nc.tensor.matmul(c.psum[:, j % 8, 0:cols[n]], xT(k, i), w(k, n),
                                            start=(k == 0), stop=(k == kt - 1))
                last.then_inc(c.multiplied, 1)

        @block.vector
        def _(dve):
            if loads:
                dve.wait_ge(c.loaded, 16 * len(loads))
            for j, (i, n) in enumerate(jobs):
                dve.wait_ge(c.multiplied, j + 1)
                ps = c.psum[:, j % 8, 0:cols[n]]
                if plus is None:
                    ins = nc.vector.tensor_copy(out(i, n), ps)
                else:
                    ins = nc.vector.tensor_tensor(out(i, n), ps, plus(i, n), ALU.add)
                ins.then_inc(c.evacuated, 1)
    c.clear()


def windowed_attention(c, qT, kTm, v, oT, w, scale):
    nc = c.nc
    span = 2 * w + 1
    hj = 2 if span * P <= BLK else 1
    per = 2 // hj
    inner = (TILES - 2 * w) // 2
    SLOTS = 3
    with ExitStack() as mem:
        mask = c.sb(mem, "band_mask", [P, span * P])
        s = c.sb(mem, "scores", [P, SLOTS, hj, span * P])
        pT = c.sb(mem, "probs_T", [P, 2, hj * span, P])
        qt = c.sb(mem, "q_tiles", [P, inner, P])
        mx = c.sb(mem, "row_max", [P, inner, HEADS])
        total = c.sb(mem, "row_sum", [P, inner, HEADS])
        o = c.sb(mem, "o_tiles", [P, inner, D])
        flat = c.psum[:, :, :].rearrange("p b f -> p (b f)")
        outs = flat[:, 2 * SLOTS * BLK:]

        with nc.Block() as block:
            @block.gpsimd
            def _(pool):
                step = Chain(pool, c.pooled)
                step(nc.gpsimd.memset(mask[:, :], 0.0))
                step(nc.gpsimd.affine_select(out=mask[:, :], in_=mask[:, :], compare_op=ALU.is_ge, fill=NEG,
                                             base=0, pattern=[[1, span * P]], channel_multiplier=-1))
                step(nc.gpsimd.affine_select(out=mask[:, :], in_=mask[:, :], compare_op=ALU.is_ge, fill=NEG,
                                             base=2 * w * P, pattern=[[-1, span * P]], channel_multiplier=1))
        c.clear()

        def run(first, tiles):
            count = len(tiles)
            jobs = [(t, h) for t in range(count) for h in range(0, HEADS, hj)]
            last_job = len(jobs) - 1

            def slot(j):
                at = 2 * (j % SLOTS) * BLK
                return flat[:, at:at + 2 * BLK]

            with nc.Block() as block:
                @block.tensor
                def _(pe):
                    def scores(j):
                        t, h0 = jobs[j]
                        lo, n, skip = tiles[t]
                        for x in range(hj):
                            for at in range(0, n * P, BLK):
                                size = min(BLK, n * P - at)
                                last = nc.tensor.matmul(slot(j)[:, x * per * BLK + at:x * per * BLK + at + size], qt[:, t, :],
                                                        kTm[:, h0 + x, bass.ds(lo * P + at, size)], start=True, stop=True)
                        last.then_inc(c.multiplied, 1)

                    def turn(j):
                        t, h0 = jobs[j]
                        n = tiles[t][1]
                        pe.wait_ge(c.activated, hj * (j + 1))
                        for y in range(hj * n):
                            x, kt = divmod(y, n)
                            last = nc.tensor.transpose(slot(j)[:, y * P:(y + 1) * P], s[:, j % SLOTS, x, kt * P:(kt + 1) * P],
                                                       c.ident[:, :])
                        last.then_inc(c.transposed, 1)

                    def outputs(j):
                        t, h0 = jobs[j]
                        lo, n, skip = tiles[t]
                        pe.wait_ge(c.copied, j + 1)
                        for x in range(hj):
                            at = t * D + (h0 + x) * HD
                            for kt in range(n):
                                last = nc.tensor.matmul(outs[:, at:at + HD], pT[:, j % 2, x * n + kt, :],
                                                        v[:, bass.ds(lo + kt, 1), (h0 + x) * HD:(h0 + x + 1) * HD],
                                                        start=(kt == 0), stop=(kt == n - 1))
                        return last

                    pe.wait_ge(c.stepped, 1)
                    scores(0)
                    scores(1)
                    for j in range(len(jobs)):
                        turn(j)
                        if j:
                            outputs(j - 1)
                        if j + 2 <= last_job:
                            scores(j + 2)
                    outputs(last_job).then_inc(c.scored, 1)
                    pe.wait_ge(c.reduced, 1)
                    for t in range(count):
                        last = nc.tensor.transpose(flat[:, t * P:(t + 1) * P], o[:, t, :], c.ident[:, :])
                    last.then_inc(c.turned, 1)

                @block.vector
                def _(dve):
                    step = Chain(dve, c.stepped)
                    step(nc.vector.tensor_copy(qt[:, 0:count, :].rearrange("p t q -> p (t q)"), qT[:, bass.ds(first * P, count * P)]))
                    for j, (t, h0) in enumerate(jobs):
                        lo, n, skip = tiles[t]
                        cols = n * P
                        here, most = s[:, j % SLOTS, :, 0:cols], mx[:, t, h0:h0 + hj]
                        dve.wait_ge(c.multiplied, j + 1)
                        step(nc.vector.tensor_tensor(
                            here, slot(j).rearrange("p (h f) -> p h f", h=hj)[:, :, 0:cols],
                            mask[:, skip:skip + cols].unsqueeze(1).to_broadcast([P, hj, cols]), ALU.add))
                        step(nc.vector.tensor_reduce(most, here, AX, ALU.max))
                        nc.vector.tensor_scalar(most, most, -scale, None, ALU.mult).then_inc(c.vectored, 1)
                    dve.wait_ge(c.activated, HEADS * count)
                    step(nc.vector.reciprocal(total[:, 0:count, :], total[:, 0:count, :]))
                    dve.wait_ge(c.scored, 1)
                    nc.vector.tensor_tensor(
                        o[:, 0:count, :].rearrange("p t (h d) -> p (t h) d", d=HD),
                        outs[:, 0:count * D].rearrange("p (a d) -> p a d", d=HD),
                        total[:, 0:count, :].rearrange("p t h -> p (t h)").unsqueeze(2).to_broadcast([P, count * HEADS, HD]),
                        ALU.mult).then_inc(c.reduced, 1)

                @block.scalar
                def _(act):
                    def copy(j):
                        act.wait_ge(c.transposed, j + 1)
                        width = hj * tiles[jobs[j][0]][1]
                        nc.scalar.activation(pT[:, j % 2, 0:width, :].rearrange("p a b -> p (a b)"), slot(j)[:, 0:width * P],
                                             ACT.Copy).then_inc(c.copied, 1)

                    for j, (t, h0) in enumerate(jobs):
                        cols = tiles[t][1] * P
                        act.wait_ge(c.vectored, j + 1)
                        for x in range(hj):
                            nc.scalar.activation(s[:, j % SLOTS, x, 0:cols], s[:, j % SLOTS, x, 0:cols], ACT.Exp,
                                                 bias=mx[:, t, h0 + x:h0 + x + 1], scale=scale,
                                                 accum_out=total[:, t, h0 + x:h0 + x + 1]).then_inc(c.activated, 1)
                        if j:
                            copy(j - 1)
                    copy(last_job)
                    act.wait_ge(c.turned, 1)
                    nc.scalar.activation(oT[:, bass.ds(first * P, count * P)], flat[:, 0:count * P], ACT.Copy)
            c.clear()

        run(0, [(0, i + w + 1, (w - i) * P) for i in range(w)])
        with nc.Fori(0, 2) as half:
            run(half * inner + w, [(half * inner + t, span, 0) for t in range(inner)])
        run(TILES - w, [(i - w, TILES - i + w, 0) for i in range(TILES - w, TILES)])


def layer0_attention(c, w_qkv, w_proj):
    nc = c.nc
    with ExitStack() as mem:
        def sb(name, shape):
            return c.sb(mem, name, shape)
        xn = sb("a0_xn", [P, TILES, D])
        xT = sb("a0_xT", [P, T])
        wq = sb("a0_wqkv", [P, 3 * D])
        wp = sb("a0_wproj", [P, D])
        qT, kT, kTm = sb("a0_qT", [P, T]), sb("a0_kT", [P, T]), sb("a0_kTm", [P, HEADS, T])
        v = sb("a0_v", [P, TILES, D])
        normalize(c, c.x[:, :, :], xn[:, :, :], TILES, D)
        transpose_tiles(c, [([xn[:, 4 * b + q, :] for q in range(4)], xT[:, b * BLK:(b + 1) * BLK]) for b in range(BLKS)])
        dense_features(c, lambda k, b: xT[:, b * BLK:(b + 1) * BLK], lambda k, m: wq[:, m * D:(m + 1) * D], 1, 2,
                       lambda m, b: (qT, kT)[m][:, b * BLK:(b + 1) * BLK], ACT.Copy,
                       loads=[(wq[:, :], w_qkv), (wp[:, :], w_proj)])
        dense_tokens(c, lambda k, i: xT[:, i * P:(i + 1) * P], lambda k, n: wq[:, 2 * D:3 * D], 1, [D],
                     lambda i, n: v[:, i, :])
        mask_keys(c, kT, kTm)
        oT = kT
        windowed_attention(c, qT, kTm, v, oT, 1, float(D) ** -0.5)
        dense_tokens(c, lambda k, i: oT[:, i * P:(i + 1) * P], lambda k, n: wp[:, :], 1, [D],
                     lambda i, n: c.x[:, i, :], plus=lambda i, n: c.x[:, i, :])


def mask_keys(c, kT, kTm):
    nc = c.nc
    with nc.Block() as block:
        @block.vector
        def _(dve):
            for h in range(HEADS):
                nc.vector.tensor_scalar(kTm[:, h, :], kT[:, :], c.headmask[:, h:h + 1], None, ALU.mult)
    c.clear()


EXPERTS0, TOPK, SHARED = 64, 8, 352
SHARED_PARTS = [(0, 128), (128, 128), (256, 96)]


def moe(c, gate_wT, w1, w3, w2, sw1, sw3, sw2):
    nc = c.nc
    with ExitStack() as mem:
        def sb(name, shape):
            return c.sb(mem, name, shape)
        xn = sb("m_xn", [P, TILES, D])
        xT = sb("m_xT", [P, T])
        gw = sb("m_gate_w", [P, EXPERTS0])
        logits = sb("m_logits", [P, TILES, EXPERTS0])
        rest = sb("m_rest", [P, TILES, EXPERTS0])
        best = sb("m_best", [P, TILES, TOPK])
        gate = sb("m_gate", [P, TILES, EXPERTS0])
        total = sb("m_total", [P, TILES])
        s1, s3 = sb("m_sw1", [P, SHARED]), sb("m_sw3", [P, SHARED])
        s2 = sb("m_sw2", [P, 3, D])
        normalize(c, c.x[:, :, :], xn[:, :, :], TILES, D)
        transpose_tiles(c, [([xn[:, 4 * b + q, :] for q in range(4)], xT[:, b * BLK:(b + 1) * BLK]) for b in range(BLKS)])
        dense_tokens(c, lambda k, i: xT[:, i * P:(i + 1) * P], lambda k, n: gw[:, :], 1, [EXPERTS0],
                     lambda i, n: logits[:, i, :],
                     loads=[(gw[:, :], gate_wT), (s1[:, :], sw1), (s3[:, :], sw3)]
                     + [(s2[0:n, j, :], sw2[a:a + n, :]) for j, (a, n) in enumerate(SHARED_PARTS)])
        with nc.Block() as block:
            @block.vector
            def _(dve):
                step = Chain(dve, c.stepped)
                for i in range(TILES):
                    nc.vector.max(best[:, i, :], logits[:, i, :]).then_inc(c.vectored, 1)
                for i in range(TILES):
                    dve.wait_ge(c.vectored, i + 1)
                    last = nc.vector.match_replace(rest[:, i, :], best[:, i, :], logits[:, i, :], -3e38)
                step(last)
                step(nc.vector.tensor_tensor(gate[:, :, :], logits[:, :, :],
                                             best[:, :, 0:1].to_broadcast([P, TILES, EXPERTS0]), ALU.subtract))
                step(nc.vector.tensor_tensor(rest[:, :, :], rest[:, :, :], logits[:, :, :], ALU.not_equal))
                dve.wait_ge(c.activated, 1)
                step(nc.vector.tensor_tensor(gate[:, :, :], gate[:, :, :], rest[:, :, :], ALU.mult))
                step(nc.vector.tensor_reduce(total[:, :], gate[:, :, :], AX, ALU.add))
                step(nc.vector.reciprocal(total[:, :], total[:, :]))
                step(nc.vector.tensor_tensor(gate[:, :, :], gate[:, :, :],
                                             total[:, :].unsqueeze(2).to_broadcast([P, TILES, EXPERTS0]), ALU.mult))

            @block.scalar
            def _(act):
                act.wait_ge(c.stepped, 2)
                nc.scalar.activation(gate[:, :, :], gate[:, :, :], ACT.Exp).then_inc(c.activated, 1)
        c.clear()
        shared_expert(c, xT, s1, s3, s2)
        routed_experts(c, xT, gate, w1, w3, w2)


def shared_expert(c, xT, s1, s3, s2):
    nc = c.nc
    parts = len(SHARED_PARTS)
    with ExitStack() as mem:
        hid = c.sb(mem, "m_shared_hidden", [P, parts, T])
        sig = c.sb(mem, "m_sig", [P, 2, BLK])
        jobs = [(m, b) for m in range(parts) for b in range(BLKS)]
        with nc.Block() as block:
            @block.tensor
            def _(pe):
                for j, (m, b) in enumerate(jobs):
                    a, n = SHARED_PARTS[m]
                    if j >= 4:
                        pe.wait_ge(c.evacuated, j - 3)
                    nc.tensor.matmul(c.psum[0:n, 2 * (j % 4), :], s1[:, a:a + n], xT[:, b * BLK:(b + 1) * BLK],
                                     start=True, stop=True)
                    nc.tensor.matmul(c.psum[0:n, 2 * (j % 4) + 1, :], s3[:, a:a + n], xT[:, b * BLK:(b + 1) * BLK],
                                     start=True, stop=True).then_inc(c.multiplied, 1)

            @block.scalar
            def _(act):
                for j, (m, b) in enumerate(jobs):
                    n = SHARED_PARTS[m][1]
                    act.wait_ge(c.multiplied, j + 1)
                    if j >= 2:
                        act.wait_ge(c.evacuated, j - 1)
                    nc.scalar.activation(sig[0:n, j % 2, :], c.psum[0:n, 2 * (j % 4), :], ACT.Sigmoid).then_inc(c.activated, 1)

            @block.vector
            def _(dve):
                step = Chain(dve, c.stepped)
                for j, (m, b) in enumerate(jobs):
                    n = SHARED_PARTS[m][1]
                    h = hid[0:n, m, b * BLK:(b + 1) * BLK]
                    dve.wait_ge(c.activated, j + 1)
                    step(nc.vector.tensor_tensor(h, sig[0:n, j % 2, :], c.psum[0:n, 2 * (j % 4), :], ALU.mult))
                    nc.vector.tensor_tensor(h, h, c.psum[0:n, 2 * (j % 4) + 1, :], ALU.mult).then_inc(c.evacuated, 1)
        c.clear()
        dense_tokens(c, lambda k, i: hid[0:SHARED_PARTS[k][1], k, i * P:(i + 1) * P],
                     lambda k, n: s2[0:SHARED_PARTS[k][1], k, :], parts, [D],
                     lambda i, n: c.x[:, i, :], plus=lambda i, n: c.x[:, i, :])


def routed_experts(c, xT, gate, w1, w3, w2):
    nc = c.nc
    PAIRS = EXPERTS0 // 2
    LAST = (PAIRS - 1) * 8
    with ExitStack() as mem:
        wt = c.sb(mem, "m_weights", [P, 2, 3, D])
        sig = c.sb(mem, "m_sigmoid", [P, 2, BLK])
        hid = c.sb(mem, "m_hidden", [P, 2, BLK])
        hidden, output, added = c.vectored, c.transposed, c.evacuated
        weights = (c.loaded, c.loaded_odd)
        with nc.Block() as block:
            @block.vector
            def _(dve):
                dve.sem_inc(hidden, 2)
                dve.sem_inc(output, 6)
                dve.sem_inc(added, 4)

        with nc.Block() as block:
            @block.sync
            def _(sp):
                with sp.Fori(0, PAIRS) as pair:
                    for par in range(2):
                        sp.wait_ge(output, pair * 8 + (4 * par + 2))
                        for j, w in enumerate((w1, w3, w2)):
                            sp.dma_start(wt[:, par, j, :], w[bass.ds(pair * 2 + par, 1), :, :].rearrange("a p n -> p (a n)")
                                         ).then_inc(weights[par], 16)

            @block.tensor
            def _(pe):
                def up(n0, pos):
                    b, par, q = pos % 4, pos // 4 % 2, pos % 2
                    if b == 0:
                        pe.wait_ge(weights[par], (n0 + pos - 4 * par) * 6 + 48)
                    pe.wait_ge(hidden, n0 + pos + 1)
                    nc.tensor.matmul(c.psum[:, 2 * q, :], wt[:, par, 0, :], xT[:, b * BLK:(b + 1) * BLK],
                                     start=True, stop=True)
                    nc.tensor.matmul(c.psum[:, 2 * q + 1, :], wt[:, par, 1, :], xT[:, b * BLK:(b + 1) * BLK],
                                     start=True, stop=True).then_inc(c.multiplied, 1)

                def down(n0, pos):
                    par, q = pos // 4 % 2, pos % 2
                    pe.wait_ge(hidden, n0 + pos + 3)
                    pe.wait_ge(added, n0 + pos + 3)
                    for t in range(4):
                        last = nc.tensor.matmul(c.psum[:, 4 + q, t * D:(t + 1) * D], hid[:, q, t * P:(t + 1) * P],
                                                wt[:, par, 2, :], start=True, stop=True)
                    last.then_inc(output, 1)

                up(0, 0)
                with pe.Fori(0, PAIRS - 1) as pair:
                    for pos in range(8):
                        up(pair * 8, pos + 1)
                        down(pair * 8, pos)
                for pos in range(8):
                    if pos < 7:
                        up(LAST, pos + 1)
                    down(LAST, pos)

            @block.scalar
            def _(act):
                with act.Fori(0, PAIRS) as pair:
                    for pos in range(8):
                        act.wait_ge(c.multiplied, pair * 8 + (pos + 1))
                        act.wait_ge(hidden, pair * 8 + (pos + 1))
                        nc.scalar.activation(sig[:, pos % 2, :], c.psum[:, 2 * (pos % 2), :], ACT.Sigmoid).then_inc(c.activated, 1)

            @block.vector
            def _(dve):
                def make_hidden(n0, pos):
                    q = pos % 2
                    dve.wait_ge(c.activated, n0 + pos + 1)
                    nc.vector.tensor_tensor(sig[:, q, :], sig[:, q, :], c.psum[:, 2 * q, :], ALU.mult).then_inc(c.stepped, 1)
                    dve.wait_ge(c.stepped, n0 + pos + 1)
                    dve.wait_ge(output, n0 + pos + 5)
                    nc.vector.tensor_tensor(hid[:, q, :], sig[:, q, :], c.psum[:, 2 * q + 1, :], ALU.mult).then_inc(hidden, 1)

                def add(n0, pos, e):
                    b, q = pos % 4, pos % 2
                    dve.wait_ge(output, n0 + pos + 7)
                    dve.wait_ge(added, n0 + pos + 1)
                    for t in range(4):
                        i = 4 * b + t
                        last = nc.vector.scalar_tensor_tensor(
                            out=c.x[:, i, :], in0=c.psum[:, 4 + q, t * D:(t + 1) * D], scalar=gate[:, i, bass.ds(e, 1)],
                            in1=c.x[:, i, :], op0=ALU.mult, op1=ALU.add)
                    last.then_inc(added, 1)

                make_hidden(0, 0)
                with dve.Fori(0, PAIRS - 1) as pair:
                    for pos in range(8):
                        make_hidden(pair * 8, pos + 1)
                        add(pair * 8, pos, pair * 2 + pos // 4)
                for pos in range(8):
                    if pos < 7:
                        make_hidden(LAST, pos + 1)
                    add(LAST, pos, EXPERTS0 - 2 + pos // 4)
        c.clear()


def layer1_attention(c, a):
    nc = c.nc
    with ExitStack() as mem:
        def sb(name, shape):
            return c.sb(mem, name, shape)
        xn = sb("a1_xn", [P, TILES, D])
        xT = sb("a1_xT", [P, T + 2])
        conv, conv_b = sb("a1_conv", [P, 3, D]), sb("a1_conv_b", [P, 1])
        win, qk_b = sb("a1_in_proj", [P, 3 * D]), sb("a1_qk_b", [P, 2])
        v_b, out_b, b2 = sb("a1_v_b", [P, D]), sb("a1_out_b", [P, D]), sb("a1_b2", [P, D])
        ln = sb("a1_ln", [P, 4, D])
        wo, w1, b1, w2 = sb("a1_wo", [P, D]), sb("a1_w1", [P, 2 * D]), sb("a1_b1", [P, 2]), sb("a1_w2", [P, 2, D])
        v = sb("a1_v", [P, TILES, D])
        h = sb("a1_h", [P, TILES, D])

        def cols(b, tap=1):
            return xT[:, b * BLK + tap:(b + 1) * BLK + tap]

        def wide(row):
            return row.partition_broadcast(P)

        loads = [(conv[:, :, :], a["L1_attn_conv_w"]), (conv_b[:, :], a["L1_attn_conv_b"]),
                 (win[:, :], a["L1_attn_in_proj_w"]), (qk_b[:, :], a["L1_attn_qk_b"]),
                 (v_b[:, :], wide(a["L1_attn_v_b"])), (out_b[:, :], wide(a["L1_attn_out_proj_b"])),
                 (b2[:, :], wide(a["L1_attn_b2"])), (wo[:, :], a["L1_attn_out_proj_w"]),
                 (w1[:, :], a["L1_attn_w1"]), (b1[:, :], a["L1_attn_b1"]), (w2[:, :, :], a["L1_attn_w2"])]
        loads += [(ln[:, j, :], wide(a["L1_attn_" + n])) for j, n in enumerate(("ln1_g", "ln1_b", "ln2_g", "ln2_b"))]
        normalize(c, c.x[:, :, :], xn[:, :, :], TILES, D, loads=loads)
        with nc.Block() as block:
            @block.vector
            def _(dve):
                nc.vector.memset(xT[:, 0:1], 0.0)
                nc.vector.memset(xT[:, T + 1:T + 2], 0.0)
        transpose_tiles(c, [([xn[:, 4 * b + q, :] for q in range(4)], cols(b)) for b in range(BLKS)])
        with ExitStack() as inner:
            vinT = c.sb(inner, "a1_vinT", [P, T])
            qT = c.sb(inner, "a1_qT", [P, T])
            kT = c.sb(inner, "a1_kT", [P, T])
            kTm = c.sb(inner, "a1_kTm", [P, HEADS, T])
            dense_features(c, lambda k, b: cols(b, k), lambda k, m: conv[:, k, :], 3, 1,
                           lambda m, b: vinT[:, b * BLK:(b + 1) * BLK], ACT.Identity, bias=lambda m: conv_b[:, 0:1])
            dense_features(c, lambda k, b: cols(b), lambda k, m: win[:, m * D:(m + 1) * D], 1, 2,
                           lambda m, b: (qT, kT)[m][:, b * BLK:(b + 1) * BLK], ACT.Identity,
                           bias=lambda m: qk_b[:, m:m + 1])
            dense_tokens(c, lambda k, i: vinT[:, i * P:(i + 1) * P], lambda k, n: win[:, 2 * D:3 * D], 1, [D],
                         lambda i, n: v[:, i, :], plus=lambda i, n: v_b[:, :])
            mask_keys(c, kT, kTm)
            oT = kT
            windowed_attention(c, qT, kTm, v, oT, 2, float(HD) ** -0.5)
            dense_tokens(c, lambda k, i: oT[:, i * P:(i + 1) * P], lambda k, n: wo[:, :], 1, [D],
                         lambda i, n: h[:, i, :], plus=lambda i, n: xn[:, i, :])
        with nc.Block() as block:
            @block.vector
            def _(dve):
                nc.vector.tensor_tensor(h[:, :, :], h[:, :, :], out_b[:, :].unsqueeze(1).to_broadcast([P, TILES, D]), ALU.add)
        normalize(c, h[:, :, :], xn[:, :, :], TILES, D, gamma=ln[:, 0, :], beta=ln[:, 1, :])
        transpose_tiles(c, [([xn[:, 4 * b + q, :] for q in range(4)], cols(b)) for b in range(BLKS)])
        with ExitStack() as inner:
            hid = c.sb(inner, "a1_hidden", [P, 2, T])
            dense_features(c, lambda k, b: cols(b), lambda k, m: w1[:, m * D:(m + 1) * D], 1, 2,
                           lambda m, b: hid[:, m, b * BLK:(b + 1) * BLK], ACT.Relu, bias=lambda m: b1[:, m:m + 1])
            dense_tokens(c, lambda k, i: hid[:, k, i * P:(i + 1) * P], lambda k, n: w2[:, k, :], 2, [D],
                         lambda i, n: h[:, i, :], plus=lambda i, n: b2[:, :])
        normalize(c, h[:, :, :], h[:, :, :], TILES, D, gamma=ln[:, 2, :], beta=ln[:, 3, :], plus=xn[:, :, :],
                  residual=c.x[:, :, :])


EXPERTS = 4
W = 256
KT = W // P
GROUPS = 4
GH = 4
PARTS = 6
STACK = PARTS * HD
GATES = 4 * W
MT = GATES // P
UNITS = KT * EXPERTS
FULL = 2.0 ** 14
CH = 64
SUPER = 64


def wide(row):
    return row.partition_broadcast(P)


def expert_front(c, a, e, xT, zx):
    nc = c.nc
    with ExitStack() as mem:
        oT = c.sb(mem, "f_oT", [P, GROUPS, T])
        with ExitStack() as m1:
            qkv = c.sb(m1, "f_qkv", [P, TILES, 3 * W])
            with ExitStack() as m2:
                w1, b1 = c.sb(m2, "f_w1", [P, W]), c.sb(m2, "f_b1", [P, KT])
                w2, rows = c.sb(m2, "f_w2", [P, KT, W]), c.sb(m2, "f_rows", [P, 3, W])
                hid, h = c.sb(m2, "f_hid", [P, KT, T]), c.sb(m2, "f_h", [P, TILES, W])
                win, bin_ = c.sb(m2, "f_in_w", [P, KT, 3 * W]), c.sb(m2, "f_in_b", [P, 3 * W])
                loads = [(w1[:, :], a["enc_w1"][e]), (b1[:, :], a["enc_b1"][e]), (w2[:, :, :], a["enc_w2"][e])]
                loads += [(rows[:, j, :], wide(a[n][e])) for j, n in enumerate(("enc_b2", "enc_g", "enc_beta"))]
                dense_features(c, lambda k, b: xT[:, b * BLK:(b + 1) * BLK], lambda k, m: w1[:, m * P:(m + 1) * P], 1, KT,
                               lambda m, b: hid[:, m, b * BLK:(b + 1) * BLK], ACT.Relu, bias=lambda m: b1[:, m:m + 1],
                               loads=loads)
                dense_tokens(c, lambda k, i: hid[:, k, i * P:(i + 1) * P], lambda k, n: w2[:, k, :], KT, [W],
                             lambda i, n: h[:, i, :], plus=lambda i, n: rows[:, 0, :])
                normalize(c, h[:, :, :], h[:, :, :], TILES, W, gamma=rows[:, 1, :], beta=rows[:, 2, :],
                          loads=[(win[:, :, :], a["attn_in_w"][e]), (bin_[:, :], wide(a["attn_in_b"][e]))])
                transpose_tiles(c, [([h[:, 4 * b + q, k * P:(k + 1) * P] for q in range(4)], hid[:, k, b * BLK:(b + 1) * BLK])
                                    for k in range(KT) for b in range(BLKS)])
                at = [(0, BLK), (BLK, 3 * W)]
                dense_tokens(c, lambda k, i: hid[:, k, i * P:(i + 1) * P], lambda k, n: win[:, k, at[n][0]:at[n][1]],
                             KT, [y - x for x, y in at], lambda i, n: qkv[:, i, at[n][0]:at[n][1]],
                             plus=lambda i, n: bin_[:, at[n][0]:at[n][1]])
            full_attention(c, qkv, oT)
        hT = c.sb(mem, "f_hT", [P, KT, T])
        wo, bo = c.sb(mem, "f_wo", [P, GROUPS, W]), c.sb(mem, "f_bo", [P, KT])
        wi, bi = c.sb(mem, "f_wi", [P, 2, KT, GATES]), c.sb(mem, "f_bi", [P, 2, MT])
        with nc.Block() as block:
            @block.vector
            def _(dve):
                nc.vector.memset(wo[:, :, :], 0.0)
        loads = [(wo[32 * h:32 * h + HD, :, :], a["attn_out_w"][e][:, h, :, :].rearrange("g d n -> d g n")) for h in range(GH)]
        divide_by_sums(c, oT, loads + [(bo[:, :], a["attn_out_b"][e])])
        dense_features(c, lambda k, b: oT[:, k, b * BLK:(b + 1) * BLK], lambda k, m: wo[:, k, m * P:(m + 1) * P], GROUPS, KT,
                       lambda m, b: hT[:, m, b * BLK:(b + 1) * BLK], ACT.Identity, bias=lambda m: bo[:, m:m + 1],
                       later=[(wi[:, d, :, :], a["lstm_wi_" + way][e]) for d, way in enumerate("fb")]
                       + [(bi[:, d, :], a["lstm_b_" + way][e]) for d, way in enumerate("fb")])
        input_projections(c, hT, wi, bi, zx, e)


def input_projections(c, hT, wi, bias, zx, e):
    nc = c.nc
    rounds = [(d, m) for d in range(2) for m in range(MT)]
    with ExitStack() as mem:
        stage = c.sb(mem, "p_stage", [P, 2, BLKS, BLK])
        with nc.Block() as block:
            @block.sync
            def _(sp):
                for r, (d, m) in enumerate(rounds):
                    sp.wait_ge(c.evacuated, BLKS * (r + 1))
                    sp.dma_start(zx[d][:, m, bass.ds(e, 1), :].rearrange("p a t -> p (a t)"),
                                 stage[:, r % 2, :, :].rearrange("p b t -> p (b t)")).then_inc(c.stored, 16)
                    sp.wait_ge(c.stored, 16 * (r + 1))
                    sp.sem_inc(c.pooled, 1)

            @block.tensor
            def _(pe):
                for j in range(BLKS * len(rounds)):
                    (d, m), b = rounds[j // BLKS], j % BLKS
                    if j >= 8:
                        pe.wait_ge(c.evacuated, j - 7)
                    for k in range(KT):
                        last = nc.tensor.matmul(c.psum[:, j % 8, :], wi[:, d, k, m * P:(m + 1) * P],
                                                hT[:, k, b * BLK:(b + 1) * BLK], start=(k == 0), stop=(k == KT - 1))
                    last.then_inc(c.multiplied, 1)

            @block.scalar
            def _(act):
                for j in range(BLKS * len(rounds)):
                    r, b = divmod(j, BLKS)
                    d, m = rounds[r]
                    act.wait_ge(c.multiplied, j + 1)
                    if b == 0 and r >= 2:
                        act.wait_ge(c.pooled, r - 1)
                    nc.scalar.activation(stage[:, r % 2, b, :], c.psum[:, j % 8, :], ACT.Identity,
                                         bias=bias[:, d, m:m + 1]).then_inc(c.evacuated, 1)
        c.clear()


def full_attention(c, qkv, oT):
    nc = c.nc
    with ExitStack() as mem:
        qs, ks = c.sb(mem, "g_qs", [P, 2, GH, T], BF16), c.sb(mem, "g_ks", [P, 2, GH, T], BF16)
        v4 = c.sb(mem, "g_v4", [P, 2, TILES, GH, 32])
        with nc.Block() as block:
            @block.gpsimd
            def _(pool):
                step = Chain(pool, c.pooled)
                step(nc.gpsimd.memset(v4[:, :, :, :, HD:32], 0.0))
                step(nc.gpsimd.memset(v4[:, :, :, :, HD:HD + 1], 1.0))
                nc.gpsimd.memset(ks[STACK:STACK + 3, 1, :, :], 1.0)

            @block.vector
            def _(dve):
                nc.vector.memset(ks[STACK:STACK + 3, 0, :, :], 1.0)
        c.clear()
        sets = [(qs[:, n, :, :], ks[:, n, :, :], v4[:, n, :, :, :]) for n in range(2)]
        split_heads(c, qkv, *sets[0], oT, 0)
        first_maxima(c, *sets[0][:2])
        for g in range(GROUPS):
            now, then = sets[g % 2], sets[(g + 1) % 2]
            with nc.Fori(0, BLKS - 1) as b:
                attend(c, *now, oT, g, b, (*now[:2], b + 1))
            if g + 1 < GROUPS:
                split_heads(c, qkv, *then, oT, g + 1)
                attend(c, *now, oT, g, BLKS - 1, (*then[:2], 0))
            else:
                attend(c, *now, oT, g, BLKS - 1, None)


def divide_by_sums(c, oT, loads):
    nc = c.nc
    CUT = GROUPS * T // 32
    with ExitStack() as mem:
        sel = c.sb(mem, "d_sel", [P, GH, 32])
        sums = c.sb(mem, "d_sums", [P, CUT])
        rows = [oT[32 * h + HD:32 * h + HD + 1, :, :].rearrange("p g t -> p (g t)").rearrange("p (q n) -> p q n", n=CUT)
                for h in range(GH)]
        jobs = [(g, b) for g in range(GROUPS) for b in range(BLKS)]
        with nc.Block() as block:
            @block.gpsimd
            def _(pool):
                step = Chain(pool, c.pooled)
                step(nc.gpsimd.memset(sel[:, :, :], 0.0))
                step(nc.gpsimd.affine_select(out=sel[:, :, :], in_=sel[:, :, :], compare_op=ALU.not_equal, fill=1.0,
                                             base=-HD, pattern=[[-32, GH], [0, 32]], channel_multiplier=1))

            @block.sync
            def _(sp):
                for h in range(GH):
                    sp.dma_start(sums[32 * h:32 * h + 32, :], rows[h]).then_inc(c.loaded, 16)
                for to, frm in loads:
                    sp.dma_start(to, frm).then_inc(c.loaded_odd, 16)
                sp.wait_ge(c.vectored, 1)
                for h in range(GH):
                    sp.dma_start(rows[h], sums[32 * h:32 * h + 32, :]).then_inc(c.stored, 16)
                sp.wait_ge(c.loaded_odd, 16 * len(loads))

            @block.tensor
            def _(pe):
                pe.wait_ge(c.pooled, 2)
                pe.wait_ge(c.stored, 16 * GH)
                for j, (g, b) in enumerate(jobs):
                    if j >= 8:
                        pe.wait_ge(c.evacuated, j - 7)
                    nc.tensor.matmul(c.psum[:, j % 8, :], sel[:, :, :].rearrange("p h m -> p (h m)"),
                                     oT[:, g, b * BLK:(b + 1) * BLK], start=True, stop=True).then_inc(c.multiplied, 1)

            @block.vector
            def _(dve):
                dve.wait_ge(c.loaded, 16 * GH)
                nc.vector.reciprocal(sums[:, :], sums[:, :]).then_inc(c.vectored, 1)
                for j, (g, b) in enumerate(jobs):
                    dve.wait_ge(c.multiplied, j + 1)
                    at = oT[:, g, b * BLK:(b + 1) * BLK]
                    nc.vector.tensor_tensor(at, at, c.psum[:, j % 8, :], ALU.mult).then_inc(c.evacuated, 1)
        c.clear()


def banks_bf16(c):
    return c.psum[:, :, :].rearrange("p b f -> p (b f)").bitcast(BF16).rearrange("p (b f) -> p b f", b=8)


def split_heads(c, qkv, qs, ks, v4, oT, g):
    nc = c.nc
    with ExitStack() as mem:
        stacks = [c.sb(mem, "h_q", [P, TILES, GH, STACK], BF16), c.sb(mem, "h_k", [P, TILES, GH, STACK], BF16)]
        size = T // 2
        rest = [oT[:, g, s * size:(s + 1) * size].rearrange("p (i n) -> p i n", n=GH * HD) for s in range(2)]
        places = [((0, 3, 5), (1, 4), (2,)), ((0, 1, 2), (3, 4), (5,))]

        def heads(ap):
            return ap.rearrange("p i (h d) -> p i h d", d=HD)

        def part(s, n):
            return stacks[s][:, :, :, n * HD:(n + 1) * HD]

        bf = banks_bf16(c)
        jobs = [(h, half, s) for h in range(GH) for half in range(2) for s in range(2)]
        with nc.Block() as block:
            @block.gpsimd
            def _(pool):
                nc.gpsimd.tensor_copy(v4[:, :, :, 0:HD], heads(qkv[:, :, bass.ds(g * (GH * HD) + 2 * W, GH * HD)]))

            @block.scalar
            def _(act):
                for level in range(3):
                    for s in range(2):
                        if level:
                            act.wait_ge(c.vectored, 2 * (level - 1) + s + 1)
                        src = qkv[:, :, bass.ds(g * (GH * HD) + s * W, GH * HD)] if level == 0 else rest[s][:, :, :]
                        nc.scalar.activation(part(s, places[s][level][0]), heads(src), ACT.Copy).then_inc(c.activated, 1)
                for j, (h, half, s) in enumerate(jobs):
                    if s == 0:
                        continue
                    act.wait_ge(c.transposed, j + 1)
                    nc.scalar.activation(ks[0:STACK, h, half * 1024:(half + 1) * 1024], bf[0:STACK, j % 8, :],
                                         ACT.Copy).then_inc(c.copied, 1)

            @block.vector
            def _(dve):
                for level in range(2):
                    for s in range(2):
                        dve.wait_ge(c.activated, 2 * level + s + 1)
                        src = heads(qkv[:, :, bass.ds(g * (GH * HD) + s * W, GH * HD)]) if level == 0 else heads(rest[s][:, :, :])
                        if level:
                            dve.wait_ge(c.vectored, s + 1)
                        nc.vector.tensor_tensor(heads(rest[s][:, :, :]), src, part(s, places[s][level][0]),
                                                ALU.subtract).then_inc(c.vectored, 1)
                    for s in range(2):
                        for n in places[s][level][1:]:
                            nc.vector.tensor_copy(part(s, n), part(s, places[s][level][0])).then_inc(c.stepped, 1)
                for j, (h, half, s) in enumerate(jobs):
                    if s == 1:
                        continue
                    dve.wait_ge(c.transposed, j + 1)
                    nc.vector.tensor_copy(qs[0:STACK, h, half * 1024:(half + 1) * 1024], bf[0:STACK, j % 8, :]).then_inc(c.evacuated, 1)

            @block.tensor
            def _(pe):
                pe.wait_ge(c.activated, 6)
                pe.wait_ge(c.stepped, 6)
                for j, (h, half, s) in enumerate(jobs):
                    if j >= 8:
                        pe.wait_ge(c.copied if s else c.evacuated, (j - 8) // 2 + 1)
                    for q in range(8):
                        last = nc.tensor.transpose(bf[0:STACK, j % 8, q * P:(q + 1) * P], stacks[s][:, half * 8 + q, h, :],
                                                   c.identb[:, :])
                    last.then_inc(c.transposed, 1)
        c.clear()


MAX_JOBS = GH * 4 * BLKS
MAX_BANK = 5
MAX_RING = 3
MAX_LEAD = 3
TURN_BANK = 6


class Maxima:

    def __init__(self, c, mem, qs, ks, b):
        self.c, self.qs, self.ks, self.b = c, qs, ks, b
        self.best = c.sb(mem, "r_best", [P, MAX_JOBS])
        self.neg = c.sb(mem, "r_neg", [P, GH * 4])
        self.parts = c.sb(mem, "r_parts", [P, GH * 4, 4], BF16)

    def multiply(self, pe, m):
        c = self.c
        h, i, kb = m // 16, m // 4 % 4, m % 4
        if m >= MAX_RING:
            pe.wait_ge(c.reduced, m - MAX_RING + 1)
        c.nc.tensor.matmul(c.psum[:, MAX_BANK + m % MAX_RING, :], self.qs[0:STACK, h, bass.ds(self.b * BLK + i * P, P)],
                           self.ks[0:STACK, h, kb * BLK:(kb + 1) * BLK], start=True, stop=True).then_inc(c.scored, 1)

    def reduce(self, dve, m):
        c = self.c
        dve.wait_ge(c.scored, m + 1)
        c.nc.vector.tensor_reduce(self.best[:, m:m + 1], c.psum[:, MAX_BANK + m % MAX_RING, :], AX, ALU.max).then_inc(c.reduced, 1)

    def multiply_row(self, pe, r):
        c = self.c
        if r >= 2:
            pe.wait_ge(c.reduced, r - 1)
        for kb in range(BLKS):
            last = c.nc.tensor.matmul(c.psum[:, 4 * (r % 2) + kb, :], self.qs[0:STACK, r // 4, bass.ds(self.b * BLK + r % 4 * P, P)],
                                      self.ks[0:STACK, r // 4, kb * BLK:(kb + 1) * BLK], start=True, stop=True)
        last.then_inc(c.scored, 1)

    def reduce_row(self, dve, r):
        c = self.c
        dve.wait_ge(c.scored, r + 1)
        c.nc.vector.tensor_reduce(self.best[:, r:r + 1], c.psum[:, 4 * (r % 2):4 * (r % 2) + 4, :].rearrange("p b f -> p (b f)"),
                                  AX, ALU.max).then_inc(c.reduced, 1)

    def split(self, dve, jobs=MAX_JOBS):
        c, nc = self.c, self.c.nc
        dve.wait_ge(c.reduced, jobs)
        step = Chain(dve, c.stepped)
        if jobs == MAX_JOBS:
            step(nc.vector.tensor_reduce(self.neg[:, :], self.best[:, :].rearrange("p (m k) -> p m k", k=BLKS), AX, ALU.max,
                                         negate=True))
        else:
            step(nc.vector.tensor_scalar(self.neg[:, :], self.best[:, 0:jobs], -1.0, None, ALU.mult))
        for n in range(3):
            step(nc.vector.tensor_copy(self.parts[:, :, n], self.neg[:, :]))
            if n < 2:
                step(nc.vector.tensor_tensor(self.neg[:, :], self.neg[:, :], self.parts[:, :, n], ALU.subtract))

    SPLIT_STEPS = 6

    def turn(self, pe):
        c = self.c
        bf = banks_bf16(c)
        pe.wait_ge(c.stepped, self.SPLIT_STEPS)
        for m in range(GH * 4):
            last = c.nc.tensor.transpose(bf[STACK:STACK + 3, TURN_BANK + m // 8, m % 8 * P:(m % 8 + 1) * P],
                                         self.parts[:, m, 0:3], c.identb[:, :])
        last.then_inc(c.turned, 1)

    def place(self, act):
        c = self.c
        bf = banks_bf16(c)
        act.wait_ge(c.turned, 1)
        for two in range(2):
            c.nc.scalar.activation(self.qs[STACK:STACK + 3, 2 * two:2 * two + 2, bass.ds(self.b * BLK, BLK)],
                                   bf[STACK:STACK + 3, TURN_BANK + two, :].rearrange("p (h f) -> p h f", f=BLK), ACT.Copy)


def first_maxima(c, qs, ks):
    with ExitStack() as mem:
        maxima = Maxima(c, mem, qs, ks, 0)
        with c.nc.Block() as block:
            @block.tensor
            def _(pe):
                for r in range(GH * 4):
                    maxima.multiply_row(pe, r)
                maxima.turn(pe)

            @block.vector
            def _(dve):
                for r in range(GH * 4):
                    maxima.reduce_row(dve, r)
                maxima.split(dve, GH * 4)

            @block.scalar
            def _(act):
                maxima.place(act)
        c.clear()


def attend(c, qs, ks, v4, oT, g, b, upcoming):
    nc = c.nc
    jobs, rows = 2 * TILES, STACK + 3
    due = [min(MAX_JOBS, MAX_JOBS * n // (jobs - MAX_LEAD)) for n in range(jobs + 1)]
    with ExitStack() as mem:
        probs = c.sb(mem, "t_probs", [P, 3, 2 * BLK])
        maxima = Maxima(c, mem, *upcoming) if upcoming else None
        ring = 2 if upcoming else 3
        out = 2 * ring
        with nc.Block() as block:
            @block.tensor
            def _(pe):
                def scores(n):
                    for two in range(2):
                        h = 2 * (n % 2) + two
                        last = nc.tensor.matmul(c.psum[:, 2 * (n % ring) + two, :], ks[0:rows, h, n // 2 * P:(n // 2 + 1) * P],
                                                qs[0:rows, h, bass.ds(b * BLK, BLK)], start=True, stop=True)
                    last.then_inc(c.multiplied, 1)

                for n in range(ring):
                    scores(n)
                for n in range(jobs):
                    pe.wait_ge(c.activated, n + 1)
                    if n + ring < jobs:
                        scores(n + ring)
                    if maxima and due[n] < due[n + 1]:
                        maxima.multiply(pe, due[n])
                    if maxima and n == jobs - 1:
                        maxima.turn(pe)
                    for two in range(2):
                        h = 2 * (n % 2) + two
                        last = nc.tensor.matmul(c.psum[32 * h:32 * h + 32, out, :], v4[:, n // 2, h, :],
                                                probs[:, n % 3, two * BLK:(two + 1) * BLK],
                                                start=(n < 2), stop=(n >= jobs - 2))
                    last.then_inc(c.copied, 1)
                    if maxima:
                        for m in range(due[n] + 1, due[n + 1]):
                            maxima.multiply(pe, m)

            @block.scalar
            def _(act):
                for n in range(jobs):
                    act.wait_ge(c.multiplied, n + 1)
                    if n >= 3:
                        act.wait_ge(c.copied, n - 2)
                    pair = c.psum[:, 2 * (n % ring):2 * (n % ring) + 2, :].rearrange("p a f -> p (a f)")
                    nc.scalar.activation(probs[:, n % 3, :], pair, ACT.Exp, scale=float(HD) ** -0.5).then_inc(c.activated, 1)
                if maxima:
                    maxima.place(act)

            @block.vector
            def _(dve):
                if maxima:
                    for m in range(MAX_JOBS):
                        maxima.reduce(dve, m)
                    maxima.split(dve)
                dve.wait_ge(c.copied, jobs)
                nc.vector.tensor_copy(oT[:, bass.ds(g, 1), bass.ds(b * BLK, BLK)].rearrange("p a f -> p (a f)"),
                                      c.psum[:, out, :])
        c.clear()


def split_weights(c, a, wh, descale):
    nc = c.nc
    with ExitStack() as mem:
        raw = c.sb(mem, "w_raw", [P, 2, EXPERTS, KT, GATES])
        most = c.sb(mem, "w_most", [P, 2])
        size = c.sb(mem, "w_size", [P, 2])
        scale = c.sb(mem, "w_scale", [P, 2])
        with nc.Block() as block:
            @block.sync
            def _(sp):
                for d, sem in ((0, c.loaded), (1, c.loaded_odd)):
                    for e in range(EXPERTS):
                        sp.dma_start(raw[:, d, e, :, :], a["lstm_wh_" + "fb"[d]][e]).then_inc(sem, 16)

            @block.vector
            def _(dve):
                step = Chain(dve, c.stepped)
                for d, sem in ((0, c.loaded), (1, c.loaded_odd)):
                    w = raw[:, d, :, :, :].rearrange("p e k n -> p (e k n)")
                    hi, lo = (wh[:, part, d, :, :, :].rearrange("p e k n -> p (e k n)") for part in range(2))
                    dve.wait_ge(sem, 16 * EXPERTS)
                    step(nc.vector.tensor_reduce(most[:, d:d + 1], w, AX, ALU.max, apply_absolute_value=True))
                    nc.vector.tensor_scalar(most[:, d:d + 1], most[:, d:d + 1], 1e-30, None, ALU.max).then_inc(c.vectored, 1)
                    dve.wait_ge(c.pooled, d + 1)
                    s = size[:, d:d + 1]
                    step(nc.vector.tensor_scalar(s.bitcast(I32), s.bitcast(I32), 0x7F800000, None, ALU.bitwise_and))
                    step(nc.vector.reciprocal(scale[:, d:d + 1], s))
                    step(nc.vector.tensor_scalar(scale[:, d:d + 1], scale[:, d:d + 1], FULL, None, ALU.mult))
                    step(nc.vector.tensor_scalar(hi, w, scale[:, d:d + 1], None, ALU.mult))
                    step(nc.vector.scalar_tensor_tensor(out=lo, in0=w, scalar=scale[:, d:d + 1], in1=hi,
                                                        op0=ALU.mult, op1=ALU.subtract))
                    step(nc.vector.tensor_scalar(descale[:, d:d + 1], s, FULL ** -2, None, ALU.mult))

            @block.gpsimd
            def _(pool):
                for d in range(2):
                    pool.wait_ge(c.vectored, d + 1)
                    nc.gpsimd.partition_all_reduce(size[:, d:d + 1], most[:, d:d + 1], P,
                                                   bass.bass_isa.ReduceOp.max).then_inc(c.pooled, 1)
        c.clear()


def lstms(c, a, zx, hist):
    nc = c.nc
    steps = T
    with ExitStack() as mem:
        wh = c.sb(mem, "l_wh", [P, 2, 2, EXPERTS, KT, GATES], F16)
        descale = c.sb(mem, "l_descale", [P, 2])
        split_weights(c, a, wh, descale)
        state = c.sb(mem, "l_state", [P, 2, UNITS, 2], F16)
        xin = c.sb(mem, "l_xin", [P, 2, 2, MT * EXPERTS, CH])
        both = c.sb(mem, "l_both", [P, 2, MT * EXPERTS])
        z = c.sb(mem, "l_z", [P, 2, MT * EXPERTS])
        gates = c.sb(mem, "l_gates", [P, 2, MT * EXPERTS])
        cell = c.sb(mem, "l_cell", [P, 2, UNITS])
        kept = c.sb(mem, "l_kept", [P, 2, UNITS])
        fresh = c.sb(mem, "l_fresh", [P, 2, UNITS])
        opened = c.sb(mem, "l_opened", [P, 2, UNITS])
        squashed = c.sb(mem, "l_squashed", [P, 2, UNITS])
        h = c.sb(mem, "l_h", [P, 2, UNITS])
        past = c.sb(mem, "l_past", [P, 2, 2, UNITS, SUPER])
        sems = {}
        for what in ("summed", "z_made", "gated", "cell_made", "squashed", "state_made", "kept"):
            sems[what] = [nc.alloc_semaphore(f"{what}_{d}") for d in range(2)]
        dve_step = [nc.alloc_semaphore(f"products_{d}") for d in range(2)]
        xin_in = [[nc.alloc_semaphore(f"xin_{d}_{q}") for q in range(2)] for d in range(2)]
        past_out = [nc.alloc_semaphore(f"past_{q}") for q in range(2)]
        chunks = nc.alloc_semaphore("chunks_begun")

        with nc.Block() as block:
            @block.vector
            def _(dve):
                nc.vector.memset(state[:, :, :, :], 0.0)
                nc.vector.memset(cell[:, :, :], 0.0)
                nc.vector.memset(h[:, :, :], 0.0)
                for d in range(2):
                    dve.sem_inc(sems["summed"][d], 2 * CH)
                    dve.sem_inc(sems["kept"][d], 1)
                    dve.sem_inc(sems["state_made"][d], 1)

        with nc.Block() as block:
            @block.sync
            def _(sp):
                with sp.Fori(0, steps // (2 * CH)) as pair:
                    for q in range(2):
                        for d in range(2):
                            at = pair * (2 * CH) + q * CH
                            sp.wait_ge(sems["summed"][d], at + CH)
                            sp.sem_inc(chunks, 1)
                            first = at if d == 0 else at * (-1) + (steps - CH)
                            sp.dma_start(xin[:, d, q, :, :],
                                         zx[d][:, :, :, bass.ds(first, CH)].rearrange("p m e t -> p (m e) t")
                                         ).then_inc(xin_in[d][q], 16)

            @block.tensor
            def _(pe):
                with pe.Fori(0, steps) as s:
                    for d in range(2):
                        pe.wait_ge(sems["state_made"][d], s + 1)
                        for e in range(EXPERTS):
                            for m in range(MT):
                                at = (m * EXPERTS + e) * 2
                                for k, part in ((0, 0), (0, 1), (1, 0), (1, 1)):
                                    last = nc.tensor.matmul(c.psum[:, d, at:at + 2], wh[:, part, d, e, k, m * P:(m + 1) * P],
                                                            state[:, d, k * EXPERTS + e, :],
                                                            start=((k, part) == (0, 0)), stop=((k, part) == (1, 1)))
                        last.then_inc(sems["z_made"][d], 1)

            @block.scalar
            def _(act):
                nc.scalar.activation(squashed[:, :, :], h[:, :, :], ACT.Sigmoid)
                with act.Fori(0, steps) as s:
                    for d in range(2):
                        act.wait_ge(sems["summed"][d], s + (2 * CH + 1))
                        nc.scalar.activation(gates[:, d, 0:3 * UNITS], z[:, d, 0:3 * UNITS], ACT.Sigmoid).then_inc(sems["gated"][d], 1)
                        nc.scalar.activation(gates[:, d, 3 * UNITS:], z[:, d, 3 * UNITS:], ACT.Tanh).then_inc(sems["gated"][d], 1)
                        act.wait_ge(sems["cell_made"][d], s + 1)
                        nc.scalar.activation(squashed[:, d, :], cell[:, d, :], ACT.Tanh).then_inc(sems["squashed"][d], 1)

            @block.vector
            def _(dve):
                def gate(d, n):
                    return gates[:, d, n * UNITS:(n + 1) * UNITS]

                OWN = 5
                with dve.Fori(0, steps // (2 * CH)) as pair:
                    for q in range(2):
                        for d in range(2):
                            dve.wait_ge(xin_in[d][q], pair * 16 + 16)
                        dve.sem_inc(chunks, 1)
                        with dve.Fori(0, CH) as r:
                            s = pair * (2 * CH) + (r + q * CH)
                            for d in range(2):
                                at = r if d == 0 else r * (-1) + (CH - 1)
                                parts = c.psum[:, d, 0:MT * EXPERTS * 2].rearrange("p (n f) -> p n f", f=2)
                                dve.wait_ge(sems["z_made"][d], s + 1)
                                nc.vector.tensor_reduce(both[:, d, :], parts, AX, ALU.add).then_inc(dve_step[d], 1)
                                dve.wait_ge(dve_step[d], s * OWN + 1)
                                nc.vector.scalar_tensor_tensor(out=z[:, d, :], in0=both[:, d, :], scalar=descale[:, d:d + 1],
                                                               in1=xin[:, d, q, :, bass.ds(at, 1)].rearrange("p n a -> p (n a)"),
                                                               op0=ALU.mult, op1=ALU.add).then_inc(sems["summed"][d], 1)
                                dve.wait_ge(sems["gated"][d], s * 2 + 1)
                                nc.vector.tensor_tensor(kept[:, d, :], gate(d, 1), cell[:, d, :], ALU.mult).then_inc(dve_step[d], 1)
                                dve.wait_ge(sems["gated"][d], s * 2 + 2)
                                nc.vector.tensor_tensor(fresh[:, d, :], gate(d, 0), gate(d, 3), ALU.mult).then_inc(dve_step[d], 1)
                                dve.wait_ge(dve_step[d], s * OWN + 3)
                                nc.vector.tensor_tensor(cell[:, d, :], kept[:, d, :], fresh[:, d, :], ALU.add).then_inc(sems["cell_made"][d], 1)
                                nc.vector.tensor_scalar(opened[:, d, :], gate(d, 2), FULL, None, ALU.mult).then_inc(dve_step[d], 1)
                                dve.wait_ge(dve_step[d], s * OWN + 4)
                                dve.wait_ge(sems["squashed"][d], s + 1)
                                nc.vector.tensor_tensor(state[:, d, :, 0], opened[:, d, :], squashed[:, d, :], ALU.mult)
                                dve.wait_ge(sems["kept"][d], s + 1)
                                nc.vector.tensor_tensor(h[:, d, :], opened[:, d, :], squashed[:, d, :], ALU.mult).then_inc(dve_step[d], 1)
                                dve.wait_ge(dve_step[d], s * OWN + 5)
                                nc.vector.tensor_tensor(state[:, d, :, 1], h[:, d, :], state[:, d, :, 0],
                                                        ALU.subtract).then_inc(sems["state_made"][d], 1)

            @block.gpsimd
            def _(pool):
                def chunk(big, q, first):
                    if not first:
                        pool.wait_ge(past_out[q], big * 64)
                        pool.sem_inc(chunks, 1)
                    with pool.Fori(0, SUPER) as r:
                        s = big * (2 * SUPER) + (r + q * SUPER)
                        for d in range(2):
                            at = r if d == 0 else r * (-1) + (SUPER - 1)
                            pool.wait_ge(sems["state_made"][d], s + 2)
                            nc.gpsimd.tensor_copy(past[:, d, q, :, bass.ds(at, 1)].rearrange("p n a -> p (n a)"),
                                                  h[:, d, :]).then_inc(sems["kept"][d], 1)
                    for d in range(2):
                        at = big * (2 * SUPER) + q * SUPER
                        t0 = at if d == 0 else at * (-1) + (steps - SUPER)
                        pool.wait_ge(sems["kept"][d], at + (SUPER + 1))
                        for k in range(KT):
                            nc.gpsimd.dma_start(hist[:, d, k, :, bass.ds(t0, SUPER)].rearrange("e p t -> p e t"),
                                                past[:, d, q, k * EXPERTS:(k + 1) * EXPERTS, :]).then_inc(past_out[q], 16)

                rounds = steps // (2 * SUPER)
                chunk(0, 0, True)
                chunk(0, 1, True)
                with pool.Fori(1, rounds) as big:
                    chunk(big, 0, False)
                    chunk(big, 1, False)
                for q in range(2):
                    pool.wait_ge(past_out[q], rounds * 64)


def expert_back(c, a, e, hist, router):
    nc = c.nc
    with ExitStack() as mem:
        past = c.sb(mem, "b_past", [P, 2, KT, T])
        hid, gate, other = (c.sb(mem, n, [P, KT, T]) for n in ("b_hid", "b_gate", "b_other"))
        w1, w2 = c.sb(mem, "b_w1", [P, 2 * KT, W]), c.sb(mem, "b_w2", [P, KT, W])
        b1, b2 = c.sb(mem, "b_b1", [P, KT]), c.sb(mem, "b_b2", [P, KT])
        wd, rows = c.sb(mem, "b_wd", [P, KT, D]), c.sb(mem, "b_rows", [P, 3, D])

        def layer(src, w, kt, out, func, b, loads, scale=1.0):
            dense_features(c, lambda k, n: src(k)[:, n * BLK:(n + 1) * BLK], lambda k, m: w[:, k, m * P:(m + 1) * P], kt, KT,
                           lambda m, n: out[:, m, n * BLK:(n + 1) * BLK], func, bias=lambda m: b[:, m:m + 1], loads=loads,
                           scale=scale)

        first = [(past[:, d, k, :], hist[e, d, k, :, :]) for d in range(2) for k in range(KT)]
        for kind, func, out in (("sig", ACT.Sigmoid, gate), ("tan", ACT.Tanh, other)):
            layer(lambda k: past[:, k // KT, k % KT, :], w1, 2 * KT, hid, ACT.Relu, b1,
                  first + [(w1[:, :, :], a[kind + "_w1"][e]), (b1[:, :], a[kind + "_b1"][e]),
                           (w2[:, :, :], a[kind + "_w2"][e]), (b2[:, :], a[kind + "_b2"][e])],
                  scale=1 / FULL)
            layer(lambda k: hid[:, k, :], w2, KT, out, func, b2, [])
            first = []
        with nc.Block() as block:
            @block.vector
            def _(dve):
                nc.vector.tensor_tensor(gate[:, :, :], gate[:, :, :], other[:, :, :], ALU.mult)
        layer(lambda k: gate[:, k, :], w2, KT, hid, ACT.Relu, b1,
              [(w2[:, :, :], a["dec_w1"][e]), (b1[:, :], a["dec_b1"][e]), (wd[:, :, :], a["dec_w2"][e])]
              + [(rows[:, j, :], wide(a[n][e])) for j, n in enumerate(("dec_b2", "dec_g", "dec_beta"))])
        y = other[:, 0, :].rearrange("p (i d) -> p i d", d=D)
        dense_tokens(c, lambda k, i: hid[:, k, i * P:(i + 1) * P], lambda k, n: wd[:, k, :], KT, [D],
                     lambda i, n: y[:, i, :], plus=lambda i, n: rows[:, 0, :])
        normalize(c, y, y, TILES, D, gamma=rows[:, 1, :], beta=rows[:, 2, :])
        with nc.Block() as block:
            @block.vector
            def _(dve):
                step = Chain(dve, c.stepped)
                step(nc.vector.tensor_tensor(y, y, router[:, :, bass.ds(e, 1)].to_broadcast([P, TILES, D]), ALU.mult))
                step(nc.vector.tensor_tensor(c.x[:, :, :], c.x[:, :, :], y, ALU.add))
        c.clear()


def layer1_experts(c, a, zx, hist):
    nc = c.nc
    with ExitStack() as mem:
        router = c.sb(mem, "e_router", [P, TILES, EXPERTS])
        with ExitStack() as m1:
            xT = c.sb(m1, "e_xT", [P, T])
            rw, rb = c.sb(m1, "e_router_w", [P, EXPERTS]), c.sb(m1, "e_router_b", [P, EXPERTS])
            total = c.sb(m1, "e_total", [P, TILES])
            with ExitStack() as m2:
                xn = c.sb(m2, "e_xn", [P, TILES, D])
                normalize(c, c.x[:, :, :], xn[:, :, :], TILES, D)
                transpose_tiles(c, [([xn[:, 4 * b + q, :] for q in range(4)], xT[:, b * BLK:(b + 1) * BLK]) for b in range(BLKS)])
            dense_tokens(c, lambda k, i: xT[:, i * P:(i + 1) * P], lambda k, n: rw[:, :], 1, [EXPERTS],
                         lambda i, n: router[:, i, :], plus=lambda i, n: rb[:, :],
                         loads=[(rw[:, :], a["router_w"]), (rb[:, :], wide(a["router_b"]))])
            with nc.Block() as block:
                def each(ap):
                    return ap.unsqueeze(2).to_broadcast([P, TILES, EXPERTS])

                @block.vector
                def _(dve):
                    step = Chain(dve, c.stepped)
                    step(nc.vector.tensor_reduce(total[:, :], router[:, :, :], AX, ALU.max))
                    step(nc.vector.tensor_tensor(router[:, :, :], router[:, :, :], each(total[:, :]), ALU.subtract))
                    dve.wait_ge(c.activated, 1)
                    step(nc.vector.tensor_reduce(total[:, :], router[:, :, :], AX, ALU.add))
                    step(nc.vector.reciprocal(total[:, :], total[:, :]))
                    step(nc.vector.tensor_tensor(router[:, :, :], router[:, :, :], each(total[:, :]), ALU.mult))

                @block.scalar
                def _(act):
                    act.wait_ge(c.stepped, 2)
                    nc.scalar.activation(router[:, :, :], router[:, :, :], ACT.Exp).then_inc(c.activated, 1)
            c.clear()
            with nc.Fori(0, EXPERTS) as e:
                expert_front(c, a, e, xT, zx)
        lstms(c, a, zx, hist)
        with nc.Fori(0, EXPERTS) as e:
            expert_back(c, a, e, hist, router)


def program(nc, a):
    with ExitStack() as ctx:
        c = Core(nc, ctx)
        zx = [nc.dram_tensor(f"projections_{d}", (P, MT, EXPERTS, T), F32).ap() for d in range(2)]
        hist = nc.dram_tensor("hidden_states", (EXPERTS, 2, KT, P, T), F32).ap()
        constants(c)
        gather(c, a["ids"], a["L0_tok_w"])
        layer0_attention(c, a["L0_attn_w_qkv"], a["L0_attn_w_proj"])
        moe(c, *(a["L0_ffn_" + n] for n in ("gate_w", "w1", "w3", "w2", "sw1", "sw3", "sw2")))
        layer1_attention(c, a)
        layer1_experts(c, {n[len("L1_ffn_"):]: v for n, v in a.items() if n.startswith("L1_ffn_")}, zx, hist)
        with nc.Block() as block:
            @block.sync
            def _(sp):
                sp.dma_start(a["out"].rearrange("a (i p) d -> p (a i) d", p=P), c.x[:, :, :]).then_inc(c.stored, 16)
                sp.wait_ge(c.stored, 16)


def lay_out(inputs):
    o = {}
    v = {n: np.asarray(x) for n, x in inputs.items()}
    o["ids"] = v["x"].reshape(TILES, P).T
    o["L0_tok_w"] = v["L0_tok_w"]
    o["L0_attn_w_qkv"] = v["L0_attn_w_qkv"].reshape(D, HEADS, 3, HD).transpose(0, 2, 1, 3).reshape(D, 3 * D)
    o["L0_attn_w_proj"] = v["L0_attn_w_proj"]
    o["L0_ffn_gate_w"] = v["L0_ffn_gate_w"].T
    for n in ("w1", "w3", "w2", "sw1", "sw3", "sw2"):
        o["L0_ffn_" + n] = v["L0_ffn_" + n]
    l = "L1_attn_"
    o[l + "conv_w"] = v[l + "conv_w"].transpose(1, 2, 0)
    o[l + "conv_b"] = v[l + "conv_b"].reshape(P, 1)
    o[l + "in_proj_w"] = v[l + "in_proj_w"].T
    o[l + "qk_b"] = v[l + "in_proj_b"][:2 * D].reshape(2, P).T
    o[l + "v_b"] = v[l + "in_proj_b"][2 * D:]
    o[l + "out_proj_w"] = v[l + "out_proj_w"].T
    o[l + "w1"] = v[l + "w1"].T
    o[l + "b1"] = v[l + "b1"].reshape(2, P).T
    o[l + "w2"] = v[l + "w2"].T.reshape(2, P, D).transpose(1, 0, 2)
    for n in ("out_proj_b", "b2", "ln1_g", "ln1_b", "ln2_g", "ln2_b"):
        o[l + n] = v[l + n]
    l = "L1_ffn_"
    for n in ("router_w", "router_b", "enc_w1", "enc_b2", "enc_g", "enc_beta", "attn_in_b", "dec_b2", "dec_g", "dec_beta"):
        o[l + n] = v[l + n]
    for n in ("enc_w2", "attn_in_w", "sig_w1", "sig_w2", "tan_w1", "tan_w2", "dec_w1", "dec_w2"):
        w = v[l + n]
        o[l + n] = w.reshape(EXPERTS, -1, P, w.shape[2]).transpose(0, 2, 1, 3)
    for n in ("enc_b1", "attn_out_b", "sig_b1", "sig_b2", "tan_b1", "tan_b2", "dec_b1"):
        o[l + n] = v[l + n].reshape(EXPERTS, KT, P).transpose(0, 2, 1)
    o[l + "attn_out_w"] = v[l + "attn_out_w"].reshape(EXPERTS, GROUPS, GH, HD, W)
    order = [0, 1, 3, 2]
    for way in "fb":
        for kind in ("wi_", "wh_"):
            w = v[l + "lstm_" + kind + way].reshape(EXPERTS, KT, P, 4, W)[:, :, :, order]
            o[l + "lstm_" + kind + way] = w.transpose(0, 2, 1, 3, 4).reshape(EXPERTS, P, KT, GATES)
        b = v[l + "lstm_b_" + way].reshape(EXPERTS, 4, W)[:, order]
        o[l + "lstm_b_" + way] = b.reshape(EXPERTS, MT, P).transpose(0, 2, 1)
    return {n: np.ascontiguousarray(x) for n, x in o.items()}


def kernel(**inputs):
    import concourse.bacc as bacc
    from concourse.bass_utils import run_bass_kernel_spmd

    nc = bacc.Bacc("TRN2", target_bir_lowering=False, num_devices=1)
    arrays = {f"in_{n}": x for n, x in lay_out(inputs).items()}
    aps = {n[len("in_"):]: nc.dram_tensor(n, x.shape, mybir.dt.from_np(x.dtype), kind="ExternalInput").ap()
           for n, x in arrays.items()}
    aps["out"] = nc.dram_tensor("out_hidden", (1, T, D), F32, kind="ExternalOutput").ap()
    program(nc, aps)
    result = run_bass_kernel_spmd(nc, [arrays], core_ids=[0])
    return result.results[0]["out_hidden"]
```
